# Optimizing a Trainium2 kernel written in Bass

```python
import numpy as np
import jax
import jax.numpy as jnp

def _softmax(x, axis=-1):
    return jax.nn.softmax(x, axis=axis)

def _gelu(x):
    return jax.nn.gelu(x, approximate=True)

def _silu(x):
    return jax.nn.silu(x)

def _sigmoid(x):
    return jax.nn.sigmoid(x)

def _layernorm(x, axis=-1, eps=1e-05):
    m = jnp.mean(x, axis=axis, keepdims=True)
    v = jnp.var(x, axis=axis, keepdims=True)
    return (x - m) / jnp.sqrt(v + eps)

def _scatter_add(tgt, idx, src, axis=0):
    return tgt.at[idx].add(src)

def _segment_sum(src, seg, n):
    return jax.ops.segment_sum(src, seg, n)
kernel_name = 'mk_xattn_ffn_d1_seqx_r4_61b588'

def setup_inputs(seed: int=0):
    np.random.seed(seed)
    _w = jnp.asarray

    def _rec_inputs():
        import jax
        import jax.numpy as jnp
        _rk = jax.random.key(seed)
        x = 0.0002279 + 0.9999 * jax.random.normal(jax.random.fold_in(_rk, 1), (4, 1024, 256), jnp.float32)
        _lenS = 1024 - jax.random.randint(jax.random.fold_in(_rk, 7), (4,), 0, max(1, 1024 // 4) + 1, jnp.int32)
        _lenS2 = 77 - jax.random.randint(jax.random.fold_in(_rk, 8), (4,), 0, max(1, 77 // 4) + 1, jnp.int32)
        _ctx_1024P = jax.random.normal(jax.random.fold_in(_rk, 11), (4, 16, 256), jnp.float32)
        _ctx_1024c = jax.random.dirichlet(jax.random.fold_in(_rk, 511), 0.3 * jnp.ones((16,), jnp.float32), (4, 77))
        _ctx_1024t = jnp.einsum('bsk,bkd->bsd', _ctx_1024c, _ctx_1024P)
        _ctx_1024t = _ctx_1024t * jax.lax.rsqrt(jnp.mean(jnp.square(_ctx_1024t)) + 1e-12) * 0.953939
        ctx_1024 = -0.000392918 + 0.999932 * (_ctx_1024t + 0.3 * jax.random.normal(jax.random.fold_in(_rk, 611), (4, 77, 256), jnp.float32))
        fside_Bx16_0 = 0.119436 + 0.907674 * jax.random.normal(jax.random.fold_in(_rk, 12), (4, 16), jnp.float32)
        return (x, ctx_1024, fside_Bx16_0)
    x, ctx_1024, fside_Bx16_0 = _rec_inputs()

    def _L0_xattn_setup():
        import jax, jax.numpy as jnp
        import numpy as np
        DIM = 256
        HEADS = 16
        DIM_HEAD = 64
        INNER = HEADS * DIM_HEAD
        EPS = 1e-05

        def layernorm(x, w, b):
            mu = jnp.mean(x, axis=-1, keepdims=True)
            var = jnp.mean(jnp.square(x - mu), axis=-1, keepdims=True)
            return (x - mu) * jax.lax.rsqrt(var + EPS) * w + b
        key = jax.random.key(seed)
        ks = jax.random.split(key, 9)
        b, n1, n2 = (4, 1024, 64)
        x = jax.random.normal(ks[0], (b, n1, DIM), dtype=jnp.float32)
        latents = jax.random.normal(ks[1], (b, n2, DIM), dtype=jnp.float32)
        shift = jax.random.normal(ks[2], (b, HEADS), dtype=jnp.float32)
        scale = jax.random.normal(ks[3], (b, HEADS), dtype=jnp.float32)
        s = 1.0 / np.sqrt(DIM)
        Wq = jax.random.normal(ks[4], (DIM, INNER), dtype=jnp.float32) * s
        Wkv = jax.random.normal(ks[5], (DIM, 2 * INNER), dtype=jnp.float32) * s
        Wout = jax.random.normal(ks[6], (INNER, DIM), dtype=jnp.float32) * (1.0 / np.sqrt(INNER))
        ln1_w = jnp.ones((DIM,), jnp.float32)
        ln1_b = jnp.zeros((DIM,), jnp.float32)
        ln2_w = jnp.ones((DIM,), jnp.float32)
        ln2_b = jnp.zeros((DIM,), jnp.float32)
        return {'x': x, 'latents': latents, 'shift': shift, 'scale': scale, 'ln1_w': ln1_w, 'ln1_b': ln1_b, 'ln2_w': ln2_w, 'ln2_b': ln2_b, 'Wq': Wq, 'Wkv': Wkv, 'Wout': Wout}
    _L0_xattn_all = _L0_xattn_setup()
    _L0_xattn_in = {k: v for k, v in _L0_xattn_all.items() if k in ('ln1_w', 'ln1_b', 'ln2_w', 'ln2_b', 'Wq', 'Wkv', 'Wout')}
    del _L0_xattn_all

    def _L0_ffn_setup():
        import jax, jax.numpy as jnp
        import numpy as np
        NUM_EXPERTS_TOTAL = 9
        TOP_K = 2
        key = jax.random.key(seed)
        k0, k1, k2, k3, k4 = jax.random.split(key, 5)
        B, S, H, I = (2, 512, 256, 704)
        E = NUM_EXPERTS_TOTAL
        x = jax.random.normal(k0, (B, S, H), dtype=jnp.float32)
        Wr = jax.random.normal(k1, (H, E), dtype=jnp.float32) * 0.02
        Wg = jax.random.normal(k2, (E, H, I), dtype=jnp.float32) * 0.02
        Wu = jax.random.normal(k3, (E, H, I), dtype=jnp.float32) * 0.02
        Wd = jax.random.normal(k4, (E, I, H), dtype=jnp.float32) * 0.02
        return {'x': x, 'Wr': Wr, 'Wg': Wg, 'Wu': Wu, 'Wd': Wd}
    _L0_ffn_all = _L0_ffn_setup()
    _L0_ffn_in = {k: v for k, v in _L0_ffn_all.items() if k in ('Wr', 'Wg', 'Wu', 'Wd')}
    del _L0_ffn_all
    return {'x': x, 'ctx_1024': ctx_1024, 'fside_Bx16_0': fside_Bx16_0, 'L0_xattn_ln1_w': _L0_xattn_in['ln1_w'], 'L0_xattn_ln1_b': _L0_xattn_in['ln1_b'], 'L0_xattn_ln2_w': _L0_xattn_in['ln2_w'], 'L0_xattn_ln2_b': _L0_xattn_in['ln2_b'], 'L0_xattn_Wq': _L0_xattn_in['Wq'], 'L0_xattn_Wkv': _L0_xattn_in['Wkv'], 'L0_xattn_Wout': _L0_xattn_in['Wout'], 'L0_ffn_Wr': _L0_ffn_in['Wr'], 'L0_ffn_Wg': _L0_ffn_in['Wg'], 'L0_ffn_Wu': _L0_ffn_in['Wu'], 'L0_ffn_Wd': _L0_ffn_in['Wd']}

def reference(x, ctx_1024, fside_Bx16_0, L0_xattn_ln1_w, L0_xattn_ln1_b, L0_xattn_ln2_w, L0_xattn_ln2_b, L0_xattn_Wq, L0_xattn_Wkv, L0_xattn_Wout, L0_ffn_Wr, L0_ffn_Wg, L0_ffn_Wu, L0_ffn_Wd):
    import jax
    import jax.numpy as jnp

    def _L0_xattn_ref(x, latents, shift, scale, ln1_w, ln1_b, ln2_w, ln2_b, Wq, Wkv, Wout):
        import jax, jax.numpy as jnp
        import numpy as np
        DIM = 256
        HEADS = 16
        DIM_HEAD = 64
        INNER = HEADS * DIM_HEAD
        EPS = 1e-05

        def layernorm(x, w, b):
            mu = jnp.mean(x, axis=-1, keepdims=True)
            var = jnp.mean(jnp.square(x - mu), axis=-1, keepdims=True)
            return (x - mu) * jax.lax.rsqrt(var + EPS) * w + b
        b = x.shape[0]
        xn = layernorm(x, ln1_w, ln1_b)
        ln = layernorm(latents, ln2_w, ln2_b)
        q = ln @ Wq
        kv = xn @ Wkv
        k, v = jnp.split(kv, 2, axis=-1)
        q = q.reshape(b, -1, HEADS, DIM_HEAD)
        k = k.reshape(b, -1, HEADS, DIM_HEAD)
        v = v.reshape(b, -1, HEADS, DIM_HEAD)
        q = q * (1.0 + scale[:, None, :, None]) + shift[:, None, :, None]
        attn_scale = DIM_HEAD ** (-0.5)
        qk = jnp.einsum('bihd,bjhd->bhij', q.astype(jnp.float32), k.astype(jnp.float32)) * attn_scale
        attn = jax.nn.softmax(qk, axis=-1).astype(v.dtype)
        out = jnp.einsum('bhij,bjhd->bihd', attn, v)
        out = out.reshape(b, -1, INNER)
        return out @ Wout

    def _L0_ffn_ref(x, Wr, Wg, Wu, Wd):
        import jax, jax.numpy as jnp
        import numpy as np
        NUM_EXPERTS_TOTAL = 9
        TOP_K = 2
        B, S, H = x.shape
        E = NUM_EXPERTS_TOTAL
        T = B * S
        logits = jnp.einsum('bsh,he->bse', x, Wr)
        probs = jax.nn.softmax(logits, axis=-1)
        topk_w, topk_idx = jax.lax.top_k(probs, TOP_K)
        topk_w = topk_w / jnp.sum(topk_w, axis=-1, keepdims=True)
        xf = x.reshape(T, H)
        wf = topk_w.reshape(T, TOP_K)
        idxf = topk_idx.reshape(T, TOP_K)
        cw = jnp.zeros((T, E), dtype=x.dtype).at[jnp.arange(T)[:, None], idxf].add(wf)
        gate = jax.nn.silu(jnp.einsum('th,ehi->tei', xf, Wg))
        hidden = gate * jnp.einsum('th,ehi->tei', xf, Wu)
        out = jnp.einsum('tei,eih,te->th', hidden, Wd, cw)
        return out.reshape(B, S, H)
    x = x + _L0_xattn_ref(ctx_1024, _layernorm(x, axis=-1), fside_Bx16_0, fside_Bx16_0, L0_xattn_ln1_w, L0_xattn_ln1_b, L0_xattn_ln2_w, L0_xattn_ln2_b, L0_xattn_Wq, L0_xattn_Wkv, L0_xattn_Wout)
    x = x + _L0_ffn_ref(_layernorm(x, axis=-1), L0_ffn_Wr, L0_ffn_Wg, L0_ffn_Wu, L0_ffn_Wd)
    return x

_drawn_inputs = setup_inputs


def setup_inputs(seed=0):
    import zlib

    import numpy as np

    out = dict(_drawn_inputs(seed))
    spreads = {'L0_xattn_ln1_w': (1.0, 0.2),
     'L0_xattn_ln1_b': (0.0, 0.1),
     'L0_xattn_ln2_w': (1.0, 0.2),
     'L0_xattn_ln2_b': (0.0, 0.282)}
    factors = {'L0_ffn_Wr': 3.867, 'L0_ffn_Wg': 3.44, 'L0_ffn_Wu': 3.399, 'L0_ffn_Wd': 3.408}
    for name, (base, spread) in spreads.items():
        noise = np.random.default_rng([zlib.crc32(name.encode()), seed]).standard_normal(out[name].shape)
        drawn = base * np.exp(spread * noise) if base else spread * noise
        out[name] = jnp.asarray(drawn.astype(out[name].dtype))
    for name, factor in factors.items():
        out[name] = (out[name] * factor).astype(out[name].dtype)
    return out
```

```python
from contextlib import ExitStack

import concourse.bass as bass
from concourse import mybir

F32 = mybir.dt.float32
I32 = mybir.dt.int32
U32 = mybir.dt.uint32
ALU = mybir.AluOpType
ACT = mybir.ActivationFunctionType
AX_X = mybir.AxisListType.X

P = 128
B, S, D = 4, 1024, 256
M, H, DH = 77, 16, 64
INNER = H * DH
E, FI = 9, 704
KT = D // P
T = B * S // P
TB = S // P
HK = H * M
KC = (HK + P - 1) // P
KLAST = HK - (KC - 1) * P
PAIRS = H // 2
EPS = 1e-5
QK_SCALE = float(DH) ** -0.5
HEADS_IN_BANK = 512 // M
SCORE_BANKS = [(h, min(h + HEADS_IN_BANK, H)) for h in range(0, H, HEADS_IN_BANK)]
KEY_GROUPS = [(h, h + 4) for h in range(0, H, 4)]
PT_GROUPS = [(c, min(c + 4, KC)) for c in range(0, KC, 4)]
NG = len(PT_GROUPS)

W = 512
WB = W // P
REGION = B * S + W
NT = (2 * B * S + E * (W - 1)) // W
MAX_TILES = B * S // W
SPARE = (NT - 2 * B * S // W) * W
ROWS = E * REGION + SPARE
FC = (FI + P - 1) // P
FLAST = FI - (FC - 1) * P
WCOLS = 2 * KT * FI + FC * D


def program(nc, x, ctx_rows, fside, ln1_w, ln1_b, ln2_w, ln2_b, wq, wkv, wout, wr, wg, wu, wd, out):
    valmat_dram = nc.dram_tensor("valmat_dram", (B, HK, D), F32).ap()
    expert_in = nc.dram_tensor("expert_in", (ROWS, D), F32).ap()
    expert_out = nc.dram_tensor("expert_out", (NT * W, D), F32).ap()

    with ExitStack() as ctx:
        def sem(name):
            return ctx.enter_context(nc.semaphore(name))

        def sb(name, shape, dt=F32, on=ctx):
            return on.enter_context(nc.sbuf_tensor(name, shape, dt))

        bank = [ctx.enter_context(nc.psum_tensor(f"bank{i}", [P, 512], F32)) for i in range(8)]

        xs = sb("xs", [P, T * D])
        ident = sb("ident", [P, P])
        before = sb("before", [P, P])
        ones = sb("ones", [P, P])
        zeros = sb("zeros", [P, WB * D])
        expert_ids = sb("expert_ids", [P, E])
        region_start = sb("region_start", [P, E])
        next_row = sb("next_row", [P, E])
        tile_ids = sb("tile_ids", [P, NT])
        minus_half = sb("minus_half", [P, T])
        wr_sb = sb("wr_sb", [P, KT, E])
        slots = sb("slots", [P, T * 2])
        slots_past = sb("slots_past", [P, T * 2])
        result_f = sb("result_f", [P, T * 2])
        result_row = sb("result_row", [P, T * 2], I32)
        lead = sb("lead", [P, E])
        logit_gap = sb("logit_gap", [P, T])
        gate1 = sb("gate1", [P, T])
        gate2 = sb("gate2", [P, T])
        gap_exp = sb("gap_exp", [P, T])
        gate_den = sb("gate_den", [P, T])
        tile_table = sb("tile_table", [P, 2, NT], I32)
        tail_row = sb("tail_row", [P, E], I32)
        count = sb("count", [P, E])
        tiles_of = sb("tiles_of", [P, E])
        tiles_upto = sb("tiles_upto", [P, E])
        jump = sb("jump", [P, E])
        past = sb("past", [P, NT, E])
        table_f = sb("table_f", [P, 2, NT])

        att = ExitStack()
        keymat_all = sb("keymat_all", [P, B * KT * HK], F32, att)
        zn = [sb(f"zn{i}", [P, D], F32, att) for i in range(2)]
        zn_t = [sb(f"zn_t{i}", [P, KT, P], F32, att) for i in range(2)]
        xn = [sb(f"xn{i}", [P, D], F32, att) for i in range(4)]
        xn_t = [sb(f"xn_t{i}", [P, KT, P], F32, att) for i in range(2)]
        top_slot = [sb(f"top_slot{i}", [P, 2], I32, att) for i in range(4)]
        x_stats = sb("x_stats", [P, T, 6], F32, att)
        x_mean = sb("x_mean", [P, T], F32, att)
        x_var = sb("x_var", [P, T], F32, att)
        x_odd = sb("x_odd", [P, T], F32, att)
        x_rstd = sb("x_rstd", [P, T], F32, att)
        x_var2 = sb("x_var2", [P, T], F32, att)
        y_stats = sb("y_stats", [P, 6], F32, att)
        y_mv = sb("y_mv", [P, 2], F32, att)
        y_rstd = sb("y_rstd", [P, 1], F32, att)
        row_max = sb("row_max", [P, H], F32, att)
        row_sum = sb("row_sum", [P, H], F32, att)
        row_inv = [sb(f"row_inv{i}", [P, H], F32, att) for i in range(2)]
        logits = sb("logits", [P, E], F32, att)
        top8 = sb("top8", [P, 8], F32, att)
        top8_id = sb("top8_id", [P, 8], U32, att)
        top_id = sb("top_id", [P, 2], F32, att)
        pick1 = sb("pick1", [P, E], F32, att)
        pick2 = sb("pick2", [P, E], F32, att)
        picks = sb("picks", [P, E], F32, att)
        place = sb("place", [P, E], F32, att)
        picked = sb("picked", [P, 2, E], F32, att)
        slot_f = sb("slot_f", [P, 2], F32, att)
        prep = ExitStack()
        wq_sb = sb("wq_sb", [P, KT, INNER], F32, prep)
        wkv_sb = sb("wkv_sb", [P, KT, 2 * INNER], F32, prep)
        wout_sb = sb("wout_sb", [P, PAIRS, D], F32, prep)
        wq_t = sb("wq_t", [P, PAIRS, D], F32, prep)
        q_lead = sb("q_lead", [P, PAIRS], F32, prep)
        wq_head = [sb(f"wq_head{i}", [P, PAIRS, D], F32, prep) for i in range(1)]
        kv_t = sb("kv_t", [P, 2 * PAIRS, B * M], F32, prep)
        c_sb = sb("c_sb", [M, B, D], F32, prep)
        c_stats = sb("c_stats", [M, B, 6], F32, prep)
        c_mv = sb("c_mv", [M, B, 2], F32, prep)
        c_rstd = sb("c_rstd", [M, B], F32, prep)
        c_t = sb("c_t", [P, KT, B * M], F32, prep)
        ln_cols = sb("ln_cols", [P, 4, KT], F32, prep)
        q_mix = sb("q_mix", [P, KT], F32, prep)
        side = sb("side", [P, B, PAIRS], F32, prep)
        side_scale = sb("side_scale", [P, B, PAIRS], F32, prep)
        side_shift = sb("side_shift", [P, B, PAIRS], F32, prep)
        valmat_st = [sb(f"valmat_st{i}", [M, 2, D], F32, prep) for i in range(4)]
        prep.close()
        keymat = sb("keymat", [P, KT, HK], F32, att)
        valmat_in = sb("valmat_in", [P, KC, D], F32, att)
        valmat = sb("valmat", [P, KC, D], F32, att)
        prob = [sb(f"prob{i}", [P, HK], F32, att) for i in range(2)]
        prob_t = [sb(f"prob_t{i}", [P, KC, P], F32, att) for i in range(2)]
        att.close()

        ffn = ExitStack()
        wgt = [sb(f"wgt{i}", [P, WCOLS], F32, ffn) for i in range(2)]
        tok = [sb(f"tok{i}", [P, WB, D], F32, ffn) for i in range(2)]
        tok_t = [sb(f"tok_t{i}", [P, KT, W], F32, ffn) for i in range(2)]
        gate_act = [sb(f"gate_act{i}", [P, W], F32, ffn) for i in range(2)]
        hid = [sb(f"hid{i}", [P, FC, W], F32, ffn) for i in range(2)]
        res = [sb(f"res{i}", [P, WB, D], F32, ffn) for i in range(2)]
        y1 = [sb(f"y1_{i}", [P, D], F32, ffn) for i in range(4)]
        y2 = [sb(f"y2_{i}", [P, D], F32, ffn) for i in range(4)]
        pick_row = [sb(f"pick_row{i}", [P, 2], I32, ffn) for i in range(4)]
        half = [sb(f"half{i}", [P, D], F32, ffn) for i in range(2)]
        fin = [sb(f"fin{i}", [P, D], F32, ffn) for i in range(4)]
        ffn.close()

        def wg_at(i):
            return wgt[i][:, 0:KT * FI].rearrange("p (k f) -> p k f", k=KT)

        def wu_at(i):
            return wgt[i][:, KT * FI:2 * KT * FI].rearrange("p (k f) -> p k f", k=KT)

        def wd_at(i):
            return wgt[i][:, 2 * KT * FI:].rearrange("p (c n) -> p c n", c=FC)

        x_loaded = sem("x_loaded")
        ctx_loaded = sem("ctx_loaded")
        weights_loaded = sem("weights_loaded")
        small_loaded = sem("small_loaded")
        consts_zero = sem("consts_zero")
        consts_made = sem("consts_made")
        ctx_stats = sem("ctx_stats")
        ctx_rstd = sem("ctx_rstd")
        ctx_normed = sem("ctx_normed")
        q_mixed = sem("q_mixed")
        wq_scaled = sem("wq_scaled")
        side_made = sem("side_made")
        x_stats_made = sem("x_stats_made")
        x_rstd_pow = sem("x_rstd_pow")
        x_var2_made = sem("x_var2_made")
        x_rstd_pow2 = sem("x_rstd_pow2")
        prep_made = sem("prep_made")
        prep_moved = sem("prep_moved")
        wq_head_made = sem("wq_head_made")
        key_products = sem("key_products")
        valmat_stored = [sem(f"valmat_stored{i}") for i in range(4)]
        valmat_loaded = sem("valmat_loaded")
        key_ready = sem("key_ready")
        val_ready = sem("val_ready")
        zn_ready = sem("zn_ready")
        turn_done = sem("turn_done")
        turn_moved = sem("turn_moved")
        scores_done = sem("scores_done")
        scores_moved = sem("scores_moved")
        exp_done = sem("exp_done")
        inv_done = sem("inv_done")
        prob_ready = sem("prob_ready")
        prob_turned = sem("prob_turned")
        prob_moved = sem("prob_moved")
        att_done = sem("att_done")
        att_added = sem("att_added")
        y_stats_made = sem("y_stats_made")
        y_rstd_made = sem("y_rstd_made")
        xn_ready = sem("xn_ready")
        logits_done = sem("logits_done")
        picks_ready = sem("picks_ready")
        ranks_done = sem("ranks_done")
        slot_ready = sem("slot_ready")
        scattered = [sem(f"scattered{i}") for i in range(4)]
        scatters_begun = sem("scatters_begun")
        gathers_begun = sem("gathers_begun")
        spare_zeroed = sem("spare_zeroed")
        table_ready = sem("table_ready")
        gap_done = sem("gap_done")
        tails_zeroed = sem("tails_zeroed")
        wgu_loaded = [sem(f"wgu_loaded{i}") for i in range(2)]
        wd_loaded = [sem(f"wd_loaded{i}") for i in range(2)]
        tok_loaded = [sem(f"tok_loaded{i}") for i in range(2)]
        tok_turned = sem("tok_turned")
        tok_moved = sem("tok_moved")
        gu_done = sem("gu_done")
        silu_done = sem("silu_done")
        hid_ready = sem("hid_ready")
        down_done = sem("down_done")
        res_ready = sem("res_ready")
        res_stored = [sem(f"res_stored{i}") for i in range(2)]
        rows_picked = sem("rows_picked")
        gathered = [sem(f"gathered{i}") for i in range(4)]
        fin_ready = sem("fin_ready")
        fin_stored = [sem(f"fin_stored{i}") for i in range(4)]

        PREP_LEAD = KT
        PREP_WQ = PREP_LEAD + 1
        PREP_KV = PREP_WQ + PAIRS
        PREP_B = PREP_KV + 2 * PAIRS
        PREP_KEYS = KT * len(KEY_GROUPS)
        PREP_ROW = PREP_KEYS + PAIRS

        def prep_bank(n):
            return bank[n % 4]

        def half_and_pair(h):
            return h // PAIRS * DH, h % PAIRS

        LOOP0, UNROLL = 6, 8

        def all_steps(eng, step):
            for s in range(LOOP0):
                step(s, s)
            with eng.Fori(0, T // UNROLL - 1) as i:
                for c in range(LOOP0, LOOP0 + UNROLL):
                    step(i * UNROLL + c, c)
            for s in range(T - UNROLL + LOOP0, T + 2):
                step(s, s)

        def batch_of(s, c):
            return s // TB if isinstance(s, int) else (s - c) // UNROLL + c // UNROLL

        def has(s, lag):
            return not isinstance(s, int) or 0 <= s - lag < T

        block = ctx.enter_context(nc.Block())

        @block.sync
        def _(sp):
            for i in range(2):
                sp.sem_inc(res_stored[i], 16)
            for i in range(4):
                sp.sem_inc(fin_stored[i], 16)
            sp.dma_start(c_sb[:], ctx_rows.rearrange("b k d -> k b d")).then_inc(ctx_loaded, 16)
            for i, v in enumerate((ln1_w, ln1_b, ln2_w, ln2_b)):
                sp.dma_start(ln_cols[:, i, :], v.rearrange("(k p) -> p k", p=P),
                             allow_slow_non_contiguous=True).then_inc(small_loaded, 16)
            by_half = fside.rearrange("b (c two) -> two b c", two=2)
            for i in range(2):
                sp.dma_start(side[i * DH:(i + 1) * DH], by_half[i].partition_broadcast(DH),
                             allow_slow_non_contiguous=True).then_inc(small_loaded, 16)
            sp.dma_start(wr_sb[:], wr.rearrange("(k p) e -> p k e", p=P)).then_inc(small_loaded, 16)
            sp.dma_start(wq_sb[:], wq.rearrange("(k p) n -> p k n", p=P)).then_inc(weights_loaded, 16)
            sp.dma_start(wkv_sb[:], wkv.rearrange("(k p) n -> p k n", p=P)).then_inc(weights_loaded, 16)
            sp.dma_start(wout_sb[:], wout.rearrange("(c p) n -> p c n", p=P)).then_inc(weights_loaded, 16)
            tokens = x.rearrange("b (t p) d -> p (b t) d", p=P)
            for b in range(B):
                sp.dma_start(xs[:, b * TB * D:(b + 1) * TB * D].rearrange("p (t d) -> p t d", d=D),
                             tokens[:, b * TB:(b + 1) * TB, :]).then_inc(x_loaded, 16)
            sp.wait_ge(consts_zero, 2)
            for i in range(SPARE // W):
                at = E * REGION + i * W
                sp.dma_start(expert_in[at:at + W, :].rearrange("(a p) d -> p a d", p=P),
                             zeros[:].rearrange("p (a d) -> p a d", d=D)).then_inc(spare_zeroed, 16)
            for b in range(B):
                for c in range(PAIRS):
                    n = b * PAIRS + c
                    sp.wait_ge(prep_moved, PREP_B + b * PREP_ROW + PREP_KEYS + c + 1)
                    sp.dma_start(valmat_dram[b, 2 * c * M:2 * (c + 1) * M, :].rearrange("(h k) n -> k h n", h=2),
                                 valmat_st[n % 4][:]).then_inc(valmat_stored[n % 4], 16)
            for i in range(4):
                sp.wait_ge(valmat_stored[i], 16 * (B * PAIRS // 4))
            for b in range(B):
                if b:
                    sp.wait_ge(val_ready, b)
                sp.dma_start(valmat_in[:, 0:KC - 1, :],
                             valmat_dram[b, 0:(KC - 1) * P, :].rearrange("(c p) n -> p c n", p=P)
                             ).then_inc(valmat_loaded, 16)
                sp.dma_start(valmat_in[0:KLAST, KC - 1, :], valmat_dram[b, (KC - 1) * P:, :]
                             ).then_inc(valmat_loaded, 16)
            sp.wait_ge(table_ready, 1)
            for e in range(E):
                row = sp.value_load(tail_row[0:1, e:e + 1], min_val=0, max_val=E * REGION - W)
                sp.dma_start(expert_in[bass.ds(row, W), :].rearrange("(a p) d -> p a d", p=P),
                             zeros[:].rearrange("p (a d) -> p a d", d=D)).then_inc(tails_zeroed, 16)
            for i in range(4):
                sp.wait_ge(scattered[i], 32 * (T // 4))
            sp.wait_ge(spare_zeroed, 16 * (SPARE // W))
            sp.wait_ge(tails_zeroed, 16 * E)

            def load_gate_up(j, i):
                e = sp.value_load(tile_table[0:1, 0, bass.ds(j, 1)], min_val=0, max_val=E - 1)
                row = sp.value_load(tile_table[0:1, 1, bass.ds(j, 1)], min_val=0, max_val=ROWS - W)
                sp.dma_start(tok[i][:], expert_in[bass.ds(row, W), :].rearrange("(a p) d -> p a d", p=P)
                             ).then_inc(tok_loaded[i], 16)
                for w, to in ((wg, wg_at(i)), (wu, wu_at(i))):
                    sp.dma_start(to, w[bass.ds(e, 1), :, :].rearrange("a (k p) f -> p (a k) f", p=P)
                                 ).then_inc(wgu_loaded[i], 16)
                return e

            def load_down(e, i):
                rows = wd[bass.ds(e, 1), :, :].rearrange("a f n -> (a f) n")
                sp.dma_start(wd_at(i)[:, 0:FC - 1, :],
                             rows[0:(FC - 1) * P, :].rearrange("(c p) n -> p c n", p=P)).then_inc(wd_loaded[i], 16)
                sp.dma_start(wd_at(i)[0:FLAST, FC - 1, :], rows[(FC - 1) * P:, :]).then_inc(wd_loaded[i], 16)

            def store(j, i):
                sp.dma_start(expert_out[bass.ds(j * W, W), :].rearrange("(a p) d -> p a d", p=P), res[i][:]
                             ).then_inc(res_stored[i], 16)

            load_down(load_gate_up(0, 0), 0)
            load_down(load_gate_up(1, 1), 1)

            def step(j, i):
                sp.wait_ge(gu_done, j * FC)
                e = load_gate_up(j + 1, i)
                sp.wait_ge(down_done, j * WB // 2)
                load_down(e, i)
                sp.wait_ge(res_ready, j * WB // 2)
                store(j - 1, i)

            for j in range(1, 3):
                step(j, (j + 1) % 2)
            with sp.Fori(0, (NT - 4) // 2) as it:
                for u in range(2):
                    step(it * 2 + (3 + u), u)
            for j in range(NT - 2, NT):
                sp.wait_ge(res_ready, (j + 1) * WB // 2)
                store(j, j % 2)
            for i in range(2):
                sp.wait_ge(res_stored[i], 16 * (NT // 2 + 1))
            result = out.rearrange("b (t p) d -> p (b t) d", p=P)
            with sp.Fori(0, T // 4) as it:
                for u in range(4):
                    sp.wait_ge(fin_ready, it * 4 + (u + 1))
                    sp.dma_start(result[:, bass.ds(it * 4 + u, 1), :].rearrange("p a d -> p (a d)"),
                                 fin[u][:]).then_inc(fin_stored[u], 16)
            for u in range(4):
                sp.wait_ge(fin_stored[u], 16 * (T // 4 + 1))

        @block.gpsimd
        def _(pool):
            nc.gpsimd.memset(zeros[:], 0.0).then_inc(consts_zero, 1)
            nc.gpsimd.memset(ident[:], 0.0).then_inc(consts_zero, 1)
            nc.gpsimd.memset(ones[:], 1.0).then_inc(consts_zero, 1)
            nc.gpsimd.memset(minus_half[:], -0.5).then_inc(consts_zero, 1)
            pool.wait_ge(consts_zero, 4)
            nc.gpsimd.affine_select(out=ident[:], in_=ident[:], compare_op=ALU.not_equal, fill=1.0, base=0,
                                    pattern=[[-1, P]], channel_multiplier=1).then_inc(consts_made, 1)
            nc.gpsimd.affine_select(out=before[:], in_=ones[:], compare_op=ALU.is_gt, fill=0.0, base=0,
                                    pattern=[[1, P]], channel_multiplier=-1).then_inc(consts_made, 1)
            for to, step, n in ((expert_ids, 1, E), (region_start, REGION, E), (next_row, REGION, E), (tile_ids, 1, NT)):
                nc.gpsimd.iota(to[:], pattern=[[step, n]], base=0, channel_multiplier=0,
                               allow_small_or_imprecise_dtypes=True).then_inc(consts_made, 1)
            pool.wait_ge(ctx_stats, 1)
            nc.gpsimd.tensor_tensor(c_rstd[:], c_rstd[:], minus_half[0:M, 0:B], ALU.pow).then_inc(ctx_rstd, 1)
            pool.wait_ge(x_stats_made, 1)
            nc.gpsimd.tensor_tensor(x_rstd[:], x_rstd[:], minus_half[:], ALU.pow).then_inc(x_rstd_pow, 1)
            pool.wait_ge(x_var2_made, 1)
            nc.gpsimd.tensor_tensor(x_var2[:], x_var2[:], minus_half[:], ALU.pow).then_inc(x_rstd_pow2, 1)

            def step(s, c):
                if has(s, 2):
                    pool.wait_ge(y_stats_made, s - 1)
                    nc.gpsimd.tensor_tensor(y_rstd[:], y_mv[:, 1:2], minus_half[:, 0:1], ALU.pow
                                            ).then_inc(y_rstd_made, 1)
                if has(s, 0):
                    pool.wait_ge(inv_done, s + 1)
                    p = prob[c % 2][:].rearrange("p (h k) -> p h k", h=H)
                    nc.gpsimd.tensor_tensor(p, p, row_inv[c % 2][:].unsqueeze(2).to_broadcast([P, H, M]), ALU.mult
                                            ).then_inc(prob_ready, 1)
                if has(s, 2):
                    i = (c - 2) % 4
                    pool.wait_ge(slot_ready, s - 1)
                    pool.sem_inc(scatters_begun, 1)
                    for k in range(2):
                        nc.gpsimd.indirect_dma_start(
                            expert_in, bass.IndirectOffsetOnAxis(ap=top_slot[i][:, k:k + 1], axis=0),
                            xn[i][:], None).then_inc(scattered[i], 16)

            all_steps(pool, step)

            for i in range(2):
                pool.wait_ge(res_stored[i], 16 * (NT // 2 + 1))
            with pool.Fori(0, T // 4) as it:
                for u in range(4):
                    pool.wait_ge(rows_picked, it * 4 + (u + 1))
                    pool.sem_inc(gathers_begun, 1)
                    for k, y in enumerate((y1, y2)):
                        nc.gpsimd.indirect_dma_start(
                            y[u][:], None, expert_out,
                            bass.IndirectOffsetOnAxis(ap=pick_row[u][:, k:k + 1], axis=0)).then_inc(gathered[u], 16)

        @block.scalar
        def _(act):
            def empty(n, to, src):
                act.wait_ge(prep_made, n + 1)
                nc.scalar.activation(to, src, ACT.Copy).then_inc(prep_moved, 1)

            act.wait_ge(small_loaded, 112)
            for k in range(KT):
                act.wait_ge(prep_made, k + 1)
                nc.scalar.activation(c_t[:, k, :], prep_bank(k)[:, 0:B * M], ACT.Identity,
                                     bias=ln_cols[:, 1, k:k + 1], scale=ln_cols[:, 0, k:k + 1]).then_inc(prep_moved, 1)
            empty(PREP_LEAD, q_lead[:], prep_bank(PREP_LEAD)[:, 0:PAIRS])
            act.wait_ge(prep_moved, PREP_WQ)
            for c in range(PAIRS):
                act.wait_ge(prep_made, PREP_WQ + c + 1)
                nc.scalar.activation(wq_t[:, c, :], prep_bank(PREP_WQ + c)[:, 0:D], ACT.Identity,
                                     bias=q_lead[:, c:c + 1]).then_inc(prep_moved, 1)
            for c in range(2 * PAIRS):
                empty(PREP_KV + c, kv_t[:, c, :], prep_bank(PREP_KV + c)[:, 0:B * M])
            for b in range(B):
                n = PREP_B + b * PREP_ROW
                for k in range(KT):
                    for h0, h1 in KEY_GROUPS:
                        at = (b * KT + k) * HK
                        empty(n, keymat_all[:, at + h0 * M:at + h1 * M], prep_bank(n)[:, 0:(h1 - h0) * M])
                        n += 1
                for c in range(PAIRS):
                    m = b * PAIRS + c
                    if m >= 4:
                        act.wait_ge(valmat_stored[m % 4], 16 * (m // 4))
                    empty(n, valmat_st[m % 4][:].rearrange("k h n -> k (h n)"), prep_bank(n)[0:M, 0:2 * D])
                    n += 1

            def key_swap(s, c):
                b = batch_of(s, c)
                if c:
                    act.wait_ge(scores_done, s)
                else:
                    act.wait_ge(prep_moved, PREP_B + B * PREP_ROW)
                nc.scalar.activation(keymat[:].rearrange("p k n -> p (k n)"),
                                     keymat_all[:, bass.ds(b * (KT * HK), KT * HK)], ACT.Copy).then_inc(key_ready, 1)

            def val_swap(s, c):
                b = batch_of(s - 1, c - 1)
                act.wait_ge(valmat_loaded, b * 32 + 32)
                if c > 1:
                    act.wait_ge(att_done, s - 1)
                nc.scalar.activation(valmat[:, 0:KC - 1, :], valmat_in[:, 0:KC - 1, :], ACT.Copy)
                nc.scalar.activation(valmat[0:KLAST, KC - 1, :], valmat_in[0:KLAST, KC - 1, :], ACT.Copy
                                     ).then_inc(val_ready, 1)

            def turn_move(s, c):
                act.wait_ge(turn_done, s + 2)
                both = has(s, -1) and has(s, 2)
                src = bank[5][:].rearrange("p (k n) -> p k n", n=P)
                if has(s, -1):
                    ins = nc.scalar.activation(zn_t[(c + 1) % 2][:], src[:, 0:KT, :], ACT.Copy)
                    if not both:
                        ins.then_inc(turn_moved, 1)
                if has(s, 2):
                    nc.scalar.activation(xn_t[c % 2][:], src[:, KT:2 * KT, :], ACT.Copy).then_inc(turn_moved, 1)
                elif not has(s, -1):
                    raise AssertionError

            def step(s, c):
                if has(s, 0) and c % UNROLL == 0:
                    key_swap(s, c)
                turn_move(s, c)
                if has(s, 1) and c % UNROLL == 1:
                    val_swap(s, c)
                if has(s, 1):
                    for g, (c0, c1) in enumerate(PT_GROUPS):
                        q = (s - 1) * NG + g
                        act.wait_ge(prob_turned, q + 1)
                        nc.scalar.activation(prob_t[(c - 1) % 2][:, c0:c1, :].rearrange("p c n -> p (c n)"),
                                             bank[3 + ((c - 1) * NG + g) % 2][:, 0:(c1 - c0) * P], ACT.Copy
                                             ).then_inc(prob_moved, 1)
                if has(s, 0):
                    act.wait_ge(scores_moved, s + 1)
                    nc.scalar.activation(prob[c % 2][:], prob[c % 2][:], ACT.Exp).then_inc(exp_done, 1)

            turn_move(-1, -1)
            all_steps(act, step)
            act.wait_ge(gap_done, 1)
            nc.scalar.activation(gap_exp[:], logit_gap[:], ACT.Exp).then_inc(gap_done, 1)

            def tok_move(j, i):
                for k in range(KT):
                    act.wait_ge(tok_turned, j * KT + (k + 1))
                    nc.scalar.activation(tok_t[i][:, k, :], bank[4 + k][:], ACT.Copy).then_inc(tok_moved, 1)

            def silu(j):
                for f in range(FC):
                    rows = P if f < FC - 1 else FLAST
                    act.wait_ge(gu_done, j * FC + (f + 1))
                    if not (isinstance(j, int) and j == 0 and f < 2):
                        act.wait_ge(hid_ready, j * FC + (f - 1))
                    nc.scalar.activation(gate_act[f % 2][0:rows, :], bank[f % 2][0:rows, :], ACT.Silu
                                         ).then_inc(silu_done, 1)

            def res_move(j, i):
                for a in range(WB // 2):
                    act.wait_ge(down_done, j * (WB // 2) + (a + 1))
                    if a == 0:
                        act.wait_ge(res_stored[i], ((j - i) // 2) * 16 + 16)
                    nc.scalar.activation(res[i][:, 2 * a:2 * a + 2, :].rearrange("p a n -> p (a n)"),
                                         bank[6 + a][:], ACT.Copy).then_inc(res_ready, 1)

            tok_move(0, 0)
            silu(0)
            tok_move(1, 1)

            def expert_step(j, i):
                silu(j)
                tok_move(j + 1, i)
                res_move(j - 1, i)

            for j in range(1, 3):
                expert_step(j, (j + 1) % 2)
            with act.Fori(0, (NT - 4) // 2) as it:
                for u in range(2):
                    expert_step(it * 2 + (3 + u), u)
            silu(NT - 1)
            res_move(NT - 2, 0)
            res_move(NT - 1, 1)

        @block.tensor
        def _(pe):
            def fill(n):
                if n >= 4:
                    pe.wait_ge(prep_moved, n - 3)
                return prep_bank(n)

            pe.wait_ge(consts_made, 2)
            pe.wait_ge(ctx_normed, 1)
            for k in range(KT):
                to = fill(k)
                for b in range(B):
                    mm = nc.tensor.transpose(to[:, b * M:(b + 1) * M], c_sb[:, b, k * P:(k + 1) * P], ident[0:M, 0:M])
                mm.then_inc(prep_made, 1)
            pe.wait_ge(q_mixed, 1)
            pe.wait_ge(weights_loaded, 48)
            to = fill(PREP_LEAD)
            for c in range(PAIRS):
                for k in range(KT):
                    mm = nc.tensor.matmul(to[:, c:c + 1], wq_sb[:, k, c * P:(c + 1) * P], q_mix[:, k:k + 1],
                                          start=k == 0, stop=k == KT - 1)
            mm.then_inc(wq_scaled, 1)
            mm = nc.tensor.matmul(to[:, PAIRS:PAIRS + 1], wq_sb[:, 0, 0:P], q_mix[:, 0:1], start=True, stop=True)
            mm.then_inc(prep_made, 1)
            pe.wait_ge(wq_scaled, 2)
            for c in range(PAIRS):
                to = fill(PREP_WQ + c)
                for k in range(KT):
                    mm = nc.tensor.transpose(to[:, k * P:(k + 1) * P], wq_sb[:, k, c * P:(c + 1) * P], ident[:])
                mm.then_inc(prep_made, 1)
            pe.wait_ge(prep_moved, KT)
            for c in range(2 * PAIRS):
                to = fill(PREP_KV + c)
                for k in range(KT):
                    mm = nc.tensor.matmul(to[:, 0:B * M], wkv_sb[:, k, c * P:(c + 1) * P], c_t[:, k, :],
                                          start=k == 0, stop=k == KT - 1)
                mm.then_inc(prep_made, 1)
            pe.wait_ge(prep_moved, PREP_KV + 2 * PAIRS)
            for b in range(B):
                n = PREP_B + b * PREP_ROW
                pe.wait_ge(wq_head_made, b + 1)
                for k in range(KT):
                    for h0, h1 in KEY_GROUPS:
                        to = fill(n)
                        for h in range(h0, h1):
                            r, c = half_and_pair(h)
                            mm = nc.tensor.matmul(to[:, (h - h0) * M:(h - h0 + 1) * M],
                                                  wq_head[0][r:r + DH, c, k * P:(k + 1) * P],
                                                  kv_t[r:r + DH, c, b * M:(b + 1) * M], start=True, stop=True)
                        mm.then_inc(prep_made, 1)
                        n += 1
                for h0 in range(0, H, 2):
                    to = fill(n)
                    for i in range(2):
                        r, c = half_and_pair(h0 + i)
                        mm = nc.tensor.matmul(to[0:M, i * D:(i + 1) * D],
                                              kv_t[r:r + DH, PAIRS + c, b * M:(b + 1) * M],
                                              wout_sb[r:r + DH, c, :], start=True, stop=True)
                    mm.then_inc(prep_made, 1)
                    n += 1
            pe.wait_ge(prep_moved, PREP_B + B * PREP_ROW)

            def turn(s, c):
                if c >= 0:
                    pe.wait_ge(turn_moved, s + 1)
                if has(s, -1):
                    pe.wait_ge(zn_ready, s + 2)
                    for k in range(KT):
                        mm = nc.tensor.transpose(bank[5][:, k * P:(k + 1) * P], zn[(c + 1) % 2][:, k * P:(k + 1) * P], ident[:])
                if has(s, 2):
                    pe.wait_ge(xn_ready, s - 1)
                    for k in range(KT):
                        mm = nc.tensor.transpose(bank[5][:, (KT + k) * P:(KT + k + 1) * P],
                                                 xn[(c - 2) % 4][:, k * P:(k + 1) * P], ident[:])
                mm.then_inc(turn_done, 1)

            def step(s, c):
                if has(s, 0):
                    pe.wait_ge(turn_moved, s + 1)
                    if c:
                        pe.wait_ge(scores_moved, s)
                    if c % UNROLL == 0:
                        pe.wait_ge(key_ready, batch_of(s, c) + 1)
                    for i, (h0, h1) in enumerate(SCORE_BANKS):
                        for k in range(KT):
                            mm = nc.tensor.matmul(bank[i][:, 0:(h1 - h0) * M], zn_t[c % 2][:, k, :],
                                                  keymat[:, k, h0 * M:h1 * M], start=k == 0, stop=k == KT - 1)
                    mm.then_inc(scores_done, 1)
                turn(s, c)
                if has(s, 1):
                    pe.wait_ge(prob_ready, s)
                    for g, (c0, c1) in enumerate(PT_GROUPS):
                        if c > 1 or g > 1:
                            pe.wait_ge(prob_moved, (s - 1) * NG + (g - 1))
                        for m in range(c0, c1):
                            n = P if m < KC - 1 else KLAST
                            mm = nc.tensor.transpose(bank[3 + ((c - 1) * NG + g) % 2][0:n, (m - c0) * P:(m - c0 + 1) * P],
                                                     prob[(c - 1) % 2][:, m * P:m * P + n], ident[:])
                        mm.then_inc(prob_turned, 1)
                if has(s, 2):
                    pe.wait_ge(turn_moved, s + 2)
                    if c > 2:
                        pe.wait_ge(slot_ready, s - 2)
                    for k in range(KT):
                        mm = nc.tensor.matmul(bank[7][:, 0:E], xn_t[c % 2][:, k, :], wr_sb[:, k, :],
                                              start=k == 0, stop=k == KT - 1)
                    mm.then_inc(logits_done, 1)
                if has(s, 1):
                    if c % UNROLL == 1:
                        pe.wait_ge(val_ready, batch_of(s - 1, c - 1) + 1)
                    if c > 1:
                        pe.wait_ge(att_added, s - 1)
                    for g, (c0, c1) in enumerate(PT_GROUPS):
                        pe.wait_ge(prob_moved, (s - 1) * NG + (g + 1))
                        for m in range(c0, c1):
                            n = P if m < KC - 1 else KLAST
                            mm = nc.tensor.matmul(bank[6][:, 0:D], prob_t[(c - 1) % 2][0:n, m, :], valmat[0:n, m, :],
                                                  start=m == 0, stop=m == KC - 1)
                    mm.then_inc(att_done, 1)
                if has(s, 2):
                    pe.wait_ge(picks_ready, s - 1)
                    nc.tensor.matmul(bank[7][:, 16:16 + E], before[:], picks[:], start=True, stop=True)
                    nc.tensor.matmul(bank[7][:, 32:32 + E], ones[:], picks[:], start=True, stop=True
                                     ).then_inc(ranks_done, 1)

            turn(-1, -1)
            all_steps(pe, step)

            def tok_turn(j, i):
                pe.wait_ge(tok_loaded[i], (j // 2 if isinstance(j, int) else (j - i) // 2) * 16 + 16)
                for k in range(KT):
                    if not (isinstance(j, int) and j == 0):
                        pe.wait_ge(tok_moved, (j - 1) * KT + (k + 1))
                    for a in range(WB):
                        mm = nc.tensor.transpose(bank[4 + k][:, a * P:(a + 1) * P], tok[i][:, a, k * P:(k + 1) * P], ident[:])
                    mm.then_inc(tok_turned, 1)

            def gate_up(j, i):
                pe.wait_ge(wgu_loaded[i], (j // 2 if isinstance(j, int) else (j - i) // 2) * 32 + 32)
                pe.wait_ge(tok_moved, j * KT + KT)
                for f in range(FC):
                    rows = P if f < FC - 1 else FLAST
                    if not (isinstance(j, int) and j == 0 and f < 2):
                        pe.wait_ge(hid_ready, j * FC + (f - 1))
                    for w, to in ((wg_at(i), bank[f % 2]), (wu_at(i), bank[2 + f % 2])):
                        for k in range(KT):
                            mm = nc.tensor.matmul(to[0:rows, :], w[:, k, f * P:f * P + rows], tok_t[i][:, k, :],
                                                  start=k == 0, stop=k == KT - 1)
                    mm.then_inc(gu_done, 1)

            def down(j, i):
                pe.wait_ge(wd_loaded[i], (j // 2 if isinstance(j, int) else (j - i) // 2) * 32 + 32)
                pe.wait_ge(hid_ready, j * FC + FC)
                for a in range(WB):
                    if a % 2 == 0 and not (isinstance(j, int) and j == 0):
                        pe.wait_ge(res_ready, (j - 1) * (WB // 2) + (a // 2 + 1))
                    for f in range(FC):
                        rows = P if f < FC - 1 else FLAST
                        mm = nc.tensor.matmul(bank[6 + a // 2][:, (a % 2) * D:(a % 2 + 1) * D],
                                              hid[i][0:rows, f, a * P:(a + 1) * P], wd_at(i)[0:rows, f, :],
                                              start=f == 0, stop=f == FC - 1)
                    if a % 2:
                        mm.then_inc(down_done, 1)

            tok_turn(0, 0)
            gate_up(0, 0)
            tok_turn(1, 1)

            def expert_step(j, i):
                gate_up(j, 1 - i)
                tok_turn(j + 1, i)
                down(j - 1, i)

            for j in range(1, 3):
                expert_step(j, (j + 1) % 2)
            with pe.Fori(0, (NT - 4) // 2) as it:
                for u in range(2):
                    expert_step(it * 2 + (3 + u), u)
            gate_up(NT - 1, 1)
            down(NT - 2, 0)
            down(NT - 1, 1)

        @block.vector
        def _(dve):
            def settle():
                dve.drain()

            dve.wait_ge(ctx_loaded, 16)
            for b in range(B):
                nc.vector.bn_stats(c_stats[:, b, :], c_sb[:, b, :])
            settle()
            for b in range(B):
                nc.vector.bn_aggr(c_mv[:, b, :], c_stats[:, b, :])
            settle()
            nc.vector.tensor_scalar(c_rstd[:], c_mv[:, :, 1], EPS, None, ALU.add).then_inc(ctx_stats, 1)
            dve.wait_ge(ctx_rstd, 1)
            for b in range(B):
                ins = nc.vector.tensor_scalar(c_sb[:, b, :], c_sb[:, b, :], c_mv[:, b, 0:1], c_rstd[:, b:b + 1],
                                              ALU.subtract, ALU.mult)
            ins.then_inc(ctx_normed, 1)
            dve.wait_ge(small_loaded, 112)
            nc.vector.tensor_tensor(q_mix[:], ln_cols[:, 3, :], ln_cols[:, 2, :], ALU.subtract)
            settle()
            nc.vector.tensor_scalar(q_mix[:], q_mix[:], 1.0 / D, None, ALU.mult).then_inc(q_mixed, 1)
            nc.vector.tensor_scalar(side_scale[:], side[:], 1.0, QK_SCALE, ALU.add, ALU.mult)
            nc.vector.tensor_scalar(side_shift[:], side[:], QK_SCALE / D, None, ALU.mult)
            dve.wait_ge(wq_scaled, 1)
            dve.wait_ge(prep_made, PREP_WQ)
            for k in range(KT):
                ins = nc.vector.tensor_scalar(wq_sb[:, k, :], wq_sb[:, k, :], ln_cols[:, 2, k:k + 1], None, ALU.mult)
            ins.then_inc(wq_scaled, 1)

            dve.wait_ge(x_loaded, 16 * B)
            with dve.Fori(0, T // 4) as it:
                for u in range(4):
                    t = it * 4 + u
                    nc.vector.bn_stats(x_stats[:, bass.ds(t, 1), :].rearrange("p a s -> p (a s)"), xs[:, bass.ds(t * D, D)])
            settle()
            nc.vector.tensor_tensor(x_mean[:], x_stats[:, :, 1], x_stats[:, :, 4], ALU.add)
            nc.vector.tensor_tensor(x_odd[:], x_stats[:, :, 4], x_stats[:, :, 1], ALU.subtract)
            nc.vector.tensor_tensor(x_var[:], x_stats[:, :, 2], x_stats[:, :, 5], ALU.add)
            settle()
            nc.vector.tensor_scalar(x_mean[:], x_mean[:], 0.5, None, ALU.mult)
            nc.vector.scalar_tensor_tensor(out=x_odd[:], in0=x_odd[:], scalar=0.25, in1=x_odd[:], op0=ALU.mult, op1=ALU.mult)
            settle()
            nc.vector.scalar_tensor_tensor(out=x_var[:], in0=x_var[:], scalar=1.0 / D, in1=x_odd[:], op0=ALU.mult, op1=ALU.add)
            settle()
            nc.vector.tensor_scalar(x_rstd[:], x_var[:], EPS, None, ALU.add).then_inc(x_stats_made, 1)
            dve.wait_ge(x_rstd_pow, 1)
            nc.vector.tensor_tensor(x_var2[:], x_var[:], x_rstd[:], ALU.mult)
            settle()
            nc.vector.tensor_tensor(x_var2[:], x_var2[:], x_rstd[:], ALU.mult)
            settle()
            nc.vector.tensor_scalar(x_var2[:], x_var2[:], EPS, None, ALU.add).then_inc(x_var2_made, 1)
            dve.wait_ge(x_rstd_pow2, 1)
            nc.vector.tensor_tensor(x_rstd[:], x_rstd[:], x_var2[:], ALU.mult)
            settle()

            dve.wait_ge(prep_moved, PREP_WQ + PAIRS)
            for b in range(B):
                if b:
                    dve.wait_ge(prep_made, PREP_B + (b - 1) * PREP_ROW + PREP_KEYS)
                for c in range(PAIRS):
                    ins = nc.vector.tensor_scalar(wq_head[0][:, c, :], wq_t[:, c, :], side_scale[:, b, c:c + 1],
                                                  side_shift[:, b, c:c + 1], ALU.mult, ALU.add)
                ins.then_inc(wq_head_made, 1)

            def normed_plus_one(t, i):
                mean, rstd = x_mean[:, bass.ds(t, 1)], x_rstd[:, bass.ds(t, 1)]
                nc.vector.tensor_scalar(zn[i][:], xs[:, bass.ds(t * D, D)], mean, rstd, ALU.subtract, ALU.mult)
                settle()
                nc.vector.tensor_scalar(zn[i][:], zn[i][:], 1.0, None, ALU.add).then_inc(zn_ready, 1)

            def add_attention(t):
                dve.wait_ge(att_done, t + 1)
                row = xs[:, bass.ds(t * D, D)]
                nc.vector.tensor_tensor(row, row, bank[6][:, 0:D], ALU.add).then_inc(att_added, 1)
                settle()
                nc.vector.bn_stats(y_stats[:], row)
                settle()
                nc.vector.bn_aggr(y_mv[:], y_stats[:])
                settle()
                nc.vector.tensor_scalar(y_mv[:, 1:2], y_mv[:, 1:2], EPS, None, ALU.add).then_inc(y_stats_made, 1)

            def normalise(t, c):
                dve.wait_ge(y_rstd_made, t + 1)
                if c >= 4:
                    dve.wait_ge(scattered[c % 4], ((t - c) // 4 + c // 4) * 32)
                nc.vector.tensor_scalar(xn[c % 4][:], xs[:, bass.ds(t * D, D)], y_mv[:, 0:1], y_rstd[:],
                                        ALU.subtract, ALU.mult).then_inc(xn_ready, 1)

            def softmax_in(t, c):
                dve.wait_ge(scores_done, t + 1)
                for i, (h0, h1) in enumerate(SCORE_BANKS):
                    nc.vector.tensor_reduce(row_max[:, h0:h1], bank[i][:, 0:(h1 - h0) * M].rearrange("p (h k) -> p h k", k=M),
                                            AX_X, ALU.max)
                settle()
                for i, (h0, h1) in enumerate(SCORE_BANKS):
                    ins = nc.vector.tensor_tensor(
                        prob[c % 2][:, h0 * M:h1 * M].rearrange("p (h k) -> p h k", k=M),
                        bank[i][:, 0:(h1 - h0) * M].rearrange("p (h k) -> p h k", k=M),
                        row_max[:, h0:h1].unsqueeze(2).to_broadcast([P, h1 - h0, M]), ALU.subtract)
                ins.then_inc(scores_moved, 1)

            def softmax_sum(t, c):
                dve.wait_ge(exp_done, t + 1)
                nc.vector.tensor_reduce(row_sum[:], prob[c % 2][:].rearrange("p (h k) -> p h k", k=M), AX_X, ALU.add)
                settle()
                nc.vector.reciprocal(row_inv[c % 2][:], row_sum[:]).then_inc(inv_done, 1)

            def route(t):
                dve.wait_ge(logits_done, t + 1)
                nc.vector.tensor_copy(logits[:], bank[7][:, 0:E])
                settle()
                nc.vector.max(top8[:], logits[:])
                settle()
                nc.vector.max_index(top8_id[:], top8[:], logits[:])
                nc.vector.tensor_tensor(logit_gap[:, bass.ds(t, 1)], top8[:, 1:2], top8[:, 0:1], ALU.subtract)
                settle()
                nc.vector.tensor_copy(top_id[:], top8_id[:, 0:2])
                settle()
                nc.vector.tensor_scalar(pick1[:], expert_ids[:], top_id[:, 0:1], None, ALU.is_equal)
                nc.vector.tensor_scalar(pick2[:], expert_ids[:], top_id[:, 1:2], None, ALU.is_equal)
                settle()
                nc.vector.tensor_tensor(picks[:], pick1[:], pick2[:], ALU.add).then_inc(picks_ready, 1)

            def allot(t, c):
                dve.wait_ge(ranks_done, t + 1)
                nc.vector.tensor_tensor(place[:], bank[7][:, 16:16 + E], next_row[:], ALU.add)
                settle()
                nc.vector.tensor_tensor(next_row[:], bank[7][:, 32:32 + E], next_row[:], ALU.add)
                nc.vector.tensor_tensor(picked[:, 0, :], pick1[:], place[:], ALU.mult)
                nc.vector.tensor_tensor(picked[:, 1, :], pick2[:], place[:], ALU.mult)
                settle()
                nc.vector.tensor_reduce(slot_f[:], picked[:], AX_X, ALU.add)
                settle()
                nc.vector.tensor_copy(slots[:, bass.ds(t * 2, 2)], slot_f[:])
                nc.vector.tensor_copy(top_slot[c % 4][:], slot_f[:]).then_inc(slot_ready, 1)

            def step(s, c):
                if has(s, 2):
                    add_attention(s - 2)
                if has(s, -1):
                    normed_plus_one(s + 1, (c + 1) % 2)
                if has(s, 2):
                    normalise(s - 2, c - 2)
                if has(s, 0):
                    softmax_in(s, c)
                if has(s, 2):
                    route(s - 2)
                if has(s, 0):
                    softmax_sum(s, c)
                if has(s, 2):
                    allot(s - 2, c - 2)

            dve.wait_ge(consts_made, 6)
            normed_plus_one(0, 0)
            all_steps(dve, step)
            settle()

            nc.vector.tensor_tensor(count[:], next_row[:], region_start[:], ALU.subtract)
            nc.vector.tensor_copy(tail_row[:], next_row[:])
            settle()
            nc.vector.tensor_scalar(tiles_of[:], count[:], 0.0, None, ALU.is_gt)
            for n in range(1, MAX_TILES):
                settle()
                nc.vector.scalar_tensor_tensor(out=tiles_of[:], in0=count[:], scalar=float(n * W), in1=tiles_of[:],
                                               op0=ALU.is_gt, op1=ALU.add)
            settle()
            nc.vector.tensor_tensor_scan(tiles_upto[:], ones[:, 0:E], tiles_of[:], 0.0, ALU.mult, ALU.add)
            nc.vector.tensor_scalar(jump[:], tiles_of[:], -float(W), float(REGION), ALU.mult, ALU.add)
            settle()
            nc.vector.tensor_tensor(past[:], tile_ids[:].unsqueeze(2).to_broadcast([P, NT, E]),
                                    tiles_upto[:].unsqueeze(1).to_broadcast([P, NT, E]), ALU.is_ge)
            settle()
            nc.vector.tensor_reduce(table_f[:, 0, :], past[:], AX_X, ALU.add)
            settle()
            nc.vector.tensor_tensor(past[:], past[:], jump[:].unsqueeze(1).to_broadcast([P, NT, E]), ALU.mult)
            nc.vector.tensor_scalar(table_f[:, 0, :], table_f[:, 0, :], float(E - 1), None, ALU.min)
            settle()
            nc.vector.tensor_reduce(table_f[:, 1, :], past[:], AX_X, ALU.add)
            settle()
            nc.vector.scalar_tensor_tensor(out=table_f[:, 1, :], in0=tile_ids[:], scalar=float(W), in1=table_f[:, 1, :],
                                           op0=ALU.mult, op1=ALU.add)
            settle()
            nc.vector.tensor_copy(tile_table[:], table_f[:]).then_inc(table_ready, 1)
            nc.vector.tensor_copy(gate2[:], logit_gap[:]).then_inc(gap_done, 1)
            dve.wait_ge(gap_done, 2)
            nc.vector.tensor_scalar(gate_den[:], gap_exp[:], 1.0, None, ALU.add)
            settle()
            nc.vector.reciprocal(gate1[:], gate_den[:])
            settle()
            nc.vector.tensor_tensor(gate2[:], gap_exp[:], gate1[:], ALU.mult)

            def hidden(j, i):
                for f in range(FC):
                    rows = P if f < FC - 1 else FLAST
                    dve.wait_ge(silu_done, j * FC + (f + 1))
                    nc.vector.tensor_tensor(hid[i][0:rows, f, :], gate_act[f % 2][0:rows, :], bank[2 + f % 2][0:rows, :],
                                            ALU.mult).then_inc(hid_ready, 1)

            nc.vector.tensor_scalar(lead[:], tiles_of[:], float(W), -float(REGION), ALU.mult, ALU.add)
            nc.vector.tensor_copy(result_f[:], slots[:])
            for e in range(1, E):
                nc.vector.tensor_scalar(slots_past[:], slots[:], region_start[:, e:e + 1], None, ALU.is_ge)
                settle()
                nc.vector.scalar_tensor_tensor(out=result_f[:], in0=slots_past[:], scalar=lead[:, e - 1:e], in1=result_f[:],
                                               op0=ALU.mult, op1=ALU.add)
                settle()
            nc.vector.tensor_copy(result_row[:], result_f[:])

            hidden(0, 0)
            with dve.Fori(0, (NT - 2) // 2) as it:
                for u in range(2):
                    hidden(it * 2 + (1 + u), 1 - u)
            hidden(NT - 1, 1)

            dve.wait_ge(res_ready, NT * WB // 2)

            def pick_rows(t, u):
                nc.vector.tensor_copy(pick_row[u][:], result_row[:, bass.ds(t * 2, 2)]).then_inc(rows_picked, 1)

            def finish(t, u, again):
                dve.wait_ge(gathered[u], again * 32 + 32)
                nc.vector.scalar_tensor_tensor(out=half[u % 2][:], in0=y1[u][:], scalar=gate1[:, bass.ds(t, 1)],
                                               in1=xs[:, bass.ds(t * D, D)], op0=ALU.mult, op1=ALU.add)
                settle()
                dve.wait_ge(fin_stored[u], again * 16 + 16)
                nc.vector.scalar_tensor_tensor(out=fin[u][:], in0=y2[u][:], scalar=gate2[:, bass.ds(t, 1)],
                                               in1=half[u % 2][:], op0=ALU.mult, op1=ALU.add).then_inc(fin_ready, 1)

            for u in range(4):
                pick_rows(u, u)
            with dve.Fori(0, T // 4 - 1) as it:
                for u in range(4):
                    finish(it * 4 + u, u, it)
                    pick_rows(it * 4 + (4 + u), u)
            for u in range(4):
                finish(T - 4 + u, u, T // 4 - 1)


_INS = ["x", "ctx_1024", "fside_Bx16_0", "L0_xattn_ln1_w", "L0_xattn_ln1_b", "L0_xattn_ln2_w", "L0_xattn_ln2_b",
        "L0_xattn_Wq", "L0_xattn_Wkv", "L0_xattn_Wout", "L0_ffn_Wr", "L0_ffn_Wg", "L0_ffn_Wu", "L0_ffn_Wd"]


def kernel(**inputs):
    import numpy as np
    import concourse.bacc as bacc
    from concourse.bass_utils import run_bass_kernel_spmd

    nc = bacc.Bacc("TRN2", target_bir_lowering=False, num_devices=1)
    arrays, args = {}, []
    for name in _INS:
        a = np.ascontiguousarray(inputs[name])
        arrays[f"in_{name}"] = a
        args.append(nc.dram_tensor(f"in_{name}", a.shape, mybir.dt.from_np(a.dtype), kind="ExternalInput").ap())
    args.append(nc.dram_tensor("result", (B, S, D), F32, kind="ExternalOutput").ap())
    program(nc, *args)
    r = run_bass_kernel_spmd(nc, [arrays], core_ids=[0])
    return r.results[0]["result"]
```

```python
from contextlib import ExitStack

import concourse.bass as bass
from concourse import mybir

F32 = mybir.dt.float32
F32R = mybir.dt.float32r
F16 = mybir.dt.float16
I32 = mybir.dt.int32
U32 = mybir.dt.uint32
ALU = mybir.AluOpType
ACT = mybir.ActivationFunctionType
AX_X = mybir.AxisListType.X

P = 128
B, S, D = 4, 1024, 256
M, H, DH = 77, 16, 64
INNER = H * DH
E, FI = 9, 704
KT = D // P
T = B * S // P
TB = S // P
HK = H * M
KC = (HK + P - 1) // P
KLAST = HK - (KC - 1) * P
PAIRS = H // 2
BM = B * M
CR = (BM + P - 1) // P
EPS = 1e-5
QK_SCALE = float(DH) ** -0.5
BATCH_PARTS = [[(max(r * P, b * M) - r * P, min(r * P + P, b * M + M) - r * P, b)
                for b in range(B) if max(r * P, b * M) < min(r * P + P, b * M + M)] for r in range(CR)]
STORE_HEADS = 4
HEADS_IN_BANK = 512 // M
SCORE_BANKS = [(h, min(h + HEADS_IN_BANK, H)) for h in range(0, H, HEADS_IN_BANK)]
PT_GROUPS = [(c, min(c + 4, KC)) for c in range(0, KC, 4)]
NG = len(PT_GROUPS)

W = 256
WB = W // P
REGION = B * S + W
NT = (2 * B * S + E * (W - 1)) // W
MAX_TILES = B * S // W
SPARE = (NT - 2 * B * S // W) * W
ROWS = E * REGION + SPARE
FC = (FI + P - 1) // P
FHALF = FI - (FC - 1) * P
FULL = (FC - 1) * P
UNITS = FC // 2
GU = 2 * FI
GUCOLS = KT * GU
WCOLS = GUCOLS + FC * D
PIECES = [(n * FI, (n + 1) * FI) for n in range(2 * KT)] + [(GUCOLS + n * FC * D // 2, GUCOLS + (n + 1) * FC * D // 2)
                                                            for n in range(2)]
assert FHALF * 2 == P and len(PIECES) == 2 * UNITS

def program(nc, x, ctx_rows, fside, ln1_w, ln1_b, ln2_w, ln2_b, wq, wkv, wout, wr, wg, wu, wd, out):
    valmat_dram = nc.dram_tensor("valmat_dram", (2, B, H, M, D), F32).ap()
    expert_in = nc.dram_tensor("expert_in", (ROWS, D), F32).ap()
    expert_out = nc.dram_tensor("expert_out", (NT * W, D), F32).ap()

    with ExitStack() as ctx:
        def sem(name):
            return ctx.enter_context(nc.semaphore(name))

        def sb(name, shape, dt=F32, on=ctx):
            return on.enter_context(nc.sbuf_tensor(name, shape, dt))

        banks = ctx.enter_context(nc.psum_tensor("banks", [P, 8, 512], F32))
        bank = [banks[:, i, :] for i in range(8)]

        xs = sb("xs", [P, T * D])
        ident = sb("ident", [P, P])
        before_f = sb("before_f", [P, P])
        ones = sb("ones", [P, P])
        before = sb("before", [P, P], F16)
        ones_h = sb("ones_h", [P, P], F16)
        zeros = sb("zeros", [P, WB * D])
        expert_ids = sb("expert_ids", [P, E])
        region_start = sb("region_start", [P, E])
        picks_sum = sb("picks_sum", [P, E], F16)
        next_row = sb("next_row", [P, E])
        tile_ids = sb("tile_ids", [P, NT])
        minus_half = sb("minus_half", [P, T])
        eps = sb("eps", [P, 1])
        wr_sb = sb("wr_sb", [P, KT, E])
        slots = sb("slots", [P, T * 2])
        slots_past = sb("slots_past", [P, T * 2])
        result_f = sb("result_f", [P, T * 2])
        result_row = sb("result_row", [P, T * 2], I32)
        lead = sb("lead", [P, E])
        logit_gap = sb("logit_gap", [P, T])
        gate1 = sb("gate1", [P, T])
        gate2 = sb("gate2", [P, T])
        gap_exp = sb("gap_exp", [P, T])
        gate_den = sb("gate_den", [P, T])
        tile_table = sb("tile_table", [P, 2, NT], I32)
        tail_row = sb("tail_row", [P, E], I32)
        count = sb("count", [P, E])
        tiles_of = sb("tiles_of", [P, E])
        tiles_upto = sb("tiles_upto", [P, E])
        jump = sb("jump", [P, E])
        past = sb("past", [P, NT, E])
        table_f = sb("table_f", [P, 2, NT])

        att = ExitStack()
        zn = [sb(f"zn{i}", [P, D], F32, att) for i in range(2)]
        zn_t = [[sb(f"zn_t{i}_{n}", [P, KT, P], F32R, att) for n in ("hi", "lo")] for i in range(2)]
        xn = [sb(f"xn{i}", [P, D], F32, att) for i in range(4)]
        xn_t = [sb(f"xn_t{i}", [P, KT, P], F32, att) for i in range(2)]
        top_slot = [sb(f"top_slot{i}", [P, 2], I32, att) for i in range(4)]
        x_stats = sb("x_stats", [P, T, 6], F32, att)
        x_mean = sb("x_mean", [P, T], F32, att)
        x_var = sb("x_var", [P, T], F32, att)
        x_odd = sb("x_odd", [P, T], F32, att)
        x_off = sb("x_off", [P, T], F32, att)
        x_rstd = sb("x_rstd", [P, T], F32, att)
        x_var2 = sb("x_var2", [P, T], F32, att)
        y_stats = sb("y_stats", [P, 6], F32, att)
        y_mv = sb("y_mv", [P, 2], F32, att)
        y_var = sb("y_var", [P, 1], F32, att)
        y_rstd = sb("y_rstd", [P, 1], F32, att)
        row_max = sb("row_max", [P, H], F32, att)
        row_sum = [sb(f"row_sum{i}", [P, H], F32, att) for i in range(2)]
        row_inv = [sb(f"row_inv{i}", [P, H], F32, att) for i in range(2)]
        logits = sb("logits", [P, E], F32, att)
        top8 = sb("top8", [P, 8], F32, att)
        top8_id = sb("top8_id", [P, 8], U32, att)
        pick = sb("pick", [P, 2, E], F32, att)
        picks = sb("picks", [P, E], F16, att)
        picked = sb("picked", [P, 2, E], F32, att)
        slot_f = sb("slot_f", [P, 2], F32, att)
        prob = [sb(f"prob{i}", [P, HK], F32, att) for i in range(2)]
        prep = ExitStack()
        wkv_sb = sb("wkv_sb", [P, KT, 2 * INNER], F32, prep)
        wq_sb = sb("wq_sb", [P, KT, INNER], F32, prep)
        wout_sb = sb("wout_sb", [P, PAIRS, 2, D], F32, prep)
        v_t = sb("v_t", [P, PAIRS, BM], F32, prep)
        val_st = [[sb(f"val_st{r}_{n}", [P, STORE_HEADS, D], F32R, prep) for n in ("hi", "lo")] for r in range(CR)]
        prep.close()
        keymat = [sb(f"keymat_{n}", [P, B, KT * HK], F32R, att) for n in ("hi", "lo")]
        prep = ExitStack()
        wq_head = sb("wq_head", [P, PAIRS, 2, D], F32, prep)
        k_head = sb("k_head", [P, PAIRS, 2, BM], F32, prep)
        c_sb = sb("c_sb", [M, B, D], F32, prep)
        c_stats = sb("c_stats", [M, B, 6], F32, prep)
        c_mv = sb("c_mv", [M, B, 2], F32, prep)
        c_rstd = sb("c_rstd", [M, B], F32, prep)
        c_t = sb("c_t", [P, KT, BM], F32, prep)
        ln_cols = sb("ln_cols", [P, 4, KT], F32, prep)
        q_mix = sb("q_mix", [P, KT], F32, prep)
        mix = sb("mix", [P, KT, D], F32, prep)
        side = sb("side", [P, B, H], F32, prep)
        side_scale = sb("side_scale", [P, B, H], F32, prep)
        side_shift = sb("side_shift", [P, B, H], F32, prep)
        prep.close()
        prob_t = [[sb(f"prob_t{i}_{n}", [P, KC, P], F32R, att) for n in ("hi", "lo")] for i in range(2)]
        valmat = [sb(f"valmat_{n}", [P, 2, KC, D], F32R, att) for n in ("hi", "lo")]
        att.close()

        ffn = ExitStack()
        wgt = [sb(f"wgt{i}", [P, WCOLS], F32, ffn) for i in range(2)]
        wgt_hi = [sb(f"wgt_hi{i}", [P, WCOLS], F32R, ffn) for i in range(2)]
        wgt_lo = [sb(f"wgt_lo{i}", [P, WCOLS], F32R, ffn) for i in range(2)]
        tok = [sb(f"tok{i}", [P, WB, D], F32, ffn) for i in range(2)]
        tok_t = [[sb(f"tok_t{i}_{n}", [P, KT, W], F32R, ffn) for n in ("hi", "lo")] for i in range(2)]
        gate_act = [sb(f"gate_act{i}", [P, 2, W], F32, ffn) for i in range(2)]
        hid_f = [sb(f"hid_f{i}", [P, 2, W], F32, ffn) for i in range(2)]
        hid = [[sb(f"hid{i}_{n}", [P, FC, W], F32R, ffn) for n in ("hi", "lo")] for i in range(2)]
        res = [sb(f"res{i}", [P, WB, D], F32, ffn) for i in range(2)]
        y1 = [sb(f"y1_{i}", [P, D], F32, ffn) for i in range(4)]
        y2 = [sb(f"y2_{i}", [P, D], F32, ffn) for i in range(4)]
        pick_row = [sb(f"pick_row{i}", [P, 2], I32, ffn) for i in range(4)]
        half = [sb(f"half{i}", [P, D], F32, ffn) for i in range(2)]
        fin = [sb(f"fin{i}", [P, D], F32, ffn) for i in range(4)]
        ffn.close()

        def gate_up_of(w):
            return w[:, 0:GUCOLS].rearrange("p (k f) -> p k f", k=KT)

        def down_of(w):
            return w[:, GUCOLS:].rearrange("p (c n) -> p c n", c=FC)

        def product(to, a, b, first, last):
            nc.tensor.matmul(to, a[0], b[0], start=first, stop=False)
            nc.tensor.matmul(to, a[0], b[1], start=False, stop=False)
            return nc.tensor.matmul(to, a[1], b[0], start=False, stop=last)

        x_loaded = sem("x_loaded")
        ctx_loaded = sem("ctx_loaded")
        wkv_loaded = sem("wkv_loaded")
        wq_loaded = sem("wq_loaded")
        wout_loaded = sem("wout_loaded")
        small_loaded = sem("small_loaded")
        consts_zero = sem("consts_zero")
        consts_made = sem("consts_made")
        ctx_stats = sem("ctx_stats")
        ctx_rstd = sem("ctx_rstd")
        ctx_normed = sem("ctx_normed")
        mix_made = sem("mix_made")
        x_stats_made = sem("x_stats_made")
        x_rstd_pow = sem("x_rstd_pow")
        x_var2_made = sem("x_var2_made")
        x_rstd_pow2 = sem("x_rstd_pow2")
        halves_filled = sem("halves_filled")
        prep_made = sem("prep_made")
        prep_moved = sem("prep_moved")
        keys_made = sem("keys_made")
        keys_moved = sem("keys_moved")
        mat_made = sem("mat_made")
        mat_hi = sem("mat_hi")
        mat_lo = sem("mat_lo")
        val_stored = [sem(f"val_stored{r}") for r in range(CR)]
        valmat_loaded = sem("valmat_loaded")
        x_off_made = sem("x_off_made")
        zn_ready = sem("zn_ready")
        turn_done = sem("turn_done")
        turn_moved = sem("turn_moved")
        zn_split = sem("zn_split")
        scores_done = sem("scores_done")
        scores_moved = sem("scores_moved")
        exp_done = sem("exp_done")
        sum_done = sem("sum_done")
        inv_done = sem("inv_done")
        prob_ready = sem("prob_ready")
        prob_turned = sem("prob_turned")
        prob_moved = sem("prob_moved")
        prob_split = sem("prob_split")
        att_done = sem("att_done")
        att_added = sem("att_added")
        y_stats_made = sem("y_stats_made")
        y_var_made = sem("y_var_made")
        y_rstd_made = sem("y_rstd_made")
        xn_ready = sem("xn_ready")
        logits_done = sem("logits_done")
        picks_ready = sem("picks_ready")
        ranks_done = sem("ranks_done")
        slot_ready = sem("slot_ready")
        scattered = [sem(f"scattered{i}") for i in range(4)]
        scatters_begun = sem("scatters_begun")
        gathers_begun = sem("gathers_begun")
        loads_begun = sem("loads_begun")
        spare_zeroed = sem("spare_zeroed")
        table_ready = sem("table_ready")
        gap_done = sem("gap_done")
        tails_zeroed = sem("tails_zeroed")
        wgu_loaded = [sem(f"wgu_loaded{i}") for i in range(2)]
        wd_loaded = [sem(f"wd_loaded{i}") for i in range(2)]
        tok_loaded = [sem(f"tok_loaded{i}") for i in range(2)]
        tok_turned = sem("tok_turned")
        tok_moved = sem("tok_moved")
        tok_split = sem("tok_split")
        weights_hi = sem("weights_hi")
        weights_split = sem("weights_split")
        hid_made = sem("hid_made")
        hid_hi = sem("hid_hi")
        pads_zeroed = sem("pads_zeroed")
        gu_done = sem("gu_done")
        silu_done = sem("silu_done")
        hid_ready = sem("hid_ready")
        down_done = sem("down_done")
        res_ready = sem("res_ready")
        res_stored = [sem(f"res_stored{i}") for i in range(2)]
        rows_picked = sem("rows_picked")
        gathered = [sem(f"gathered{i}") for i in range(4)]
        fin_ready = sem("fin_ready")
        fin_stored = [sem(f"fin_stored{i}") for i in range(4)]

        PREP_V = KT
        PREP_WQ = PREP_V + PAIRS
        PREP = PREP_WQ + PAIRS
        STORE_PAIRS = STORE_HEADS // 2
        STORES = H // STORE_HEADS
        VALS = STORES * CR * STORE_PAIRS
        MATS = VALS + H * KT
        VAL_LOAD = 4 * 16

        def prep_bank(n):
            return bank[n % 4]

        def val_place(m):
            return m // (CR * STORE_PAIRS), m // STORE_PAIRS % CR, m % STORE_PAIRS

        def context_rows(r):
            return min(P, BM - r * P)

        def key_place(m):
            return (m - VALS) // KT, (m - VALS) % KT

        LOOP0, UNROLL = 7, 8

        def all_steps(eng, step):
            for s in range(LOOP0):
                step(s, s)
            with eng.Fori(0, T // UNROLL - 1) as i:
                for c in range(LOOP0, LOOP0 + UNROLL):
                    step(i * UNROLL + c, c)
            for s in range(T - UNROLL + LOOP0, T + 4):
                step(s, s)

        def batch_of(t, c):
            return t // TB if isinstance(t, int) else (t - c) // UNROLL + c // UNROLL

        def has(s, lag):
            return not isinstance(s, int) or 0 <= s - lag < T

        def turns(s):
            return has(s, -1) or has(s, 3)

        def turn_count(s):
            return s + 1

        def part_of(keys, b):
            return keys[:, b, :] if isinstance(b, int) else keys[:, bass.ds(b, 1), :].rearrange("p a n -> p (a n)")

        def half_of(vals, b):
            return vals[:, b % 2] if isinstance(b, int) else vals[:, bass.ds(b % 2, 1)].rearrange("p a c n -> p (a c) n")

        def turned_chunks(c0, c1):
            return [(P, c0, c1)] if c1 < KC else [(P, c0, c1 - 1), (KLAST, c1 - 1, c1)]

        def turned_bank(t, g, rows, m0, m1):
            return banks[0:rows, 3 + (t * NG + g) % 2, m0 * P:m1 * P].rearrange("p (c n) -> p c n", n=P)

        block = ctx.enter_context(nc.Block())

        @block.sync
        def _(sp):
            for i in range(2):
                sp.sem_inc(res_stored[i], 16)
            for i in range(4):
                sp.sem_inc(fin_stored[i], 16)
            sp.dma_start(c_sb[:], ctx_rows.rearrange("b k d -> k b d")).then_inc(ctx_loaded, 16)
            for i, v in enumerate((ln1_w, ln1_b, ln2_w, ln2_b)):
                sp.dma_start(ln_cols[:, i, :], v.rearrange("(k p) -> p k", p=P),
                             allow_slow_non_contiguous=True).then_inc(small_loaded, 16)
            sp.dma_start(side[:], fside.partition_broadcast(P)).then_inc(small_loaded, 16)
            sp.dma_start(wkv_sb[:], wkv.rearrange("(k p) n -> p k n", p=P)).then_inc(wkv_loaded, 16)
            sp.dma_start(wq_sb[:], wq.rearrange("(k p) n -> p k n", p=P)).then_inc(wq_loaded, 16)
            by_half = wout.rearrange("(c two p) n -> two p c n", two=2, p=DH)
            for i in range(2):
                sp.dma_start(wout_sb[i * DH:(i + 1) * DH, :, i, :], by_half[i]).then_inc(wout_loaded, 16)
            sp.dma_start(wr_sb[:], wr.rearrange("(k p) e -> p k e", p=P)).then_inc(small_loaded, 16)
            tokens = x.rearrange("b (t p) d -> p (b t) d", p=P)
            for b in range(B):
                sp.dma_start(xs[:, b * TB * D:(b + 1) * TB * D].rearrange("p (t d) -> p t d", d=D),
                             tokens[:, b * TB:(b + 1) * TB, :]).then_inc(x_loaded, 16)
            sp.wait_ge(consts_zero, 2)
            for i in range(SPARE // W):
                at = E * REGION + i * W
                sp.dma_start(expert_in[at:at + W, :].rearrange("(a p) d -> p a d", p=P),
                             zeros[:].rearrange("p (a d) -> p a d", d=D)).then_inc(spare_zeroed, 16)
            for g in range(STORES):
                heads = slice(g * STORE_HEADS, (g + 1) * STORE_HEADS)
                for r in range(CR):
                    sp.wait_ge(mat_lo, ((g * CR + r) + 1) * STORE_PAIRS)
                    for n in range(2):
                        for r0, r1, b in BATCH_PARTS[r]:
                            k = r * P + r0 - b * M
                            sp.dma_start(valmat_dram[n, b, heads, k:k + r1 - r0, :].rearrange("h k n -> k h n"),
                                         val_st[r][n][r0:r1].bitcast(F32)).then_inc(val_stored[r], 16)
            for r in range(CR):
                sp.wait_ge(val_stored[r], 32 * len(BATCH_PARTS[r]) * STORES)
            sp.wait_ge(mat_made, MATS)
            for b in range(B):
                if b:
                    sp.wait_ge(valmat_loaded, b * VAL_LOAD)
                if b >= 2:
                    sp.wait_ge(att_done, (b - 1) * TB)
                for n in range(2):
                    rows = valmat_dram[n, b].rearrange("h k n -> (h k) n")
                    sp.dma_start(valmat[n][:, b % 2, 0:KC - 1, :].bitcast(F32), rows[0:(KC - 1) * P, :].rearrange("(c p) n -> p c n", p=P)
                                 ).then_inc(valmat_loaded, 16)
                    sp.dma_start(valmat[n][0:KLAST, b % 2, KC - 1, :].bitcast(F32), rows[(KC - 1) * P:, :]).then_inc(valmat_loaded, 16)
            sp.wait_ge(table_ready, 1)
            for e in range(E):
                row = sp.value_load(tail_row[0:1, e:e + 1], min_val=0, max_val=E * REGION - W)
                sp.dma_start(expert_in[bass.ds(row, W), :].rearrange("(a p) d -> p a d", p=P),
                             zeros[:].rearrange("p (a d) -> p a d", d=D)).then_inc(tails_zeroed, 16)
            for i in range(4):
                sp.wait_ge(scattered[i], 32 * (T // 4))
            sp.wait_ge(spare_zeroed, 16 * (SPARE // W))
            sp.wait_ge(tails_zeroed, 16 * E)

            def load(j, i):
                e = sp.value_load(tile_table[0:1, 0, bass.ds(j, 1)], min_val=0, max_val=E - 1)
                row = sp.value_load(tile_table[0:1, 1, bass.ds(j, 1)], min_val=0, max_val=ROWS - W)
                sp.dma_start(tok[i][:], expert_in[bass.ds(row, W), :].rearrange("(a p) d -> p a d", p=P)
                             ).then_inc(tok_loaded[i], 16)
                gate, up = (w[bass.ds(e, 1), :, :].rearrange("a (k p) f -> p (a k) f", p=P) for w in (wg, wu))
                to = gate_up_of(wgt[i])
                sp.dma_start(to[:, :, 0:FI], gate).then_inc(wgu_loaded[i], 16)
                sp.dma_start(to[:, :, FI:FI + FHALF], up[:, :, FULL:FI]).then_inc(wgu_loaded[i], 16)
                sp.dma_start(to[:, :, FI + FHALF:GU], up[:, :, 0:FULL]).then_inc(wgu_loaded[i], 16)
                rows = wd[bass.ds(e, 1), :, :].rearrange("a f n -> (a f) n")
                to = down_of(wgt[i])
                sp.dma_start(to[:, 0:FC - 1, :], rows[0:FULL, :].rearrange("(c p) n -> p c n", p=P)).then_inc(wd_loaded[i], 16)
                sp.dma_start(to[0:FHALF, FC - 1, :], rows[FULL:FI, :]).then_inc(wd_loaded[i], 16)

            def store(j, i):
                sp.wait_ge(res_ready, j + 1)
                sp.dma_start(expert_out[bass.ds(j * W, W), :].rearrange("(a p) d -> p a d", p=P), res[i][:]
                             ).then_inc(res_stored[i], 16)

            def step(j, i):
                sp.wait_ge(tok_turned, j)
                sp.sem_inc(loads_begun, 1)
                sp.wait_ge(weights_split, j * len(PIECES))
                sp.sem_inc(loads_begun, 1)
                load(j + 1, i)
                if not (isinstance(j, int) and j < 2):
                    store(j - 2, 1 - i)

            load(0, 0)
            load(1, 1)
            for j in range(1, 3):
                step(j, (j + 1) % 2)
            with sp.Fori(0, (NT - 4) // 2) as it:
                for u in range(2):
                    step(it * 2 + (3 + u), u)
            for j in range(NT - 3, NT):
                store(j, j % 2)
            for i in range(2):
                sp.wait_ge(res_stored[i], 16 * (NT // 2 + 1))
            result = out.rearrange("b (t p) d -> p (b t) d", p=P)
            with sp.Fori(0, T // 4) as it:
                for u in range(4):
                    sp.wait_ge(fin_ready, it * 4 + (u + 1))
                    sp.dma_start(result[:, bass.ds(it * 4 + u, 1), :].rearrange("p a d -> p (a d)"),
                                 fin[u][:]).then_inc(fin_stored[u], 16)
            for u in range(4):
                sp.wait_ge(fin_stored[u], 16 * (T // 4 + 1))

        @block.gpsimd
        def _(pool):
            nc.gpsimd.memset(zeros[:], 0.0).then_inc(consts_zero, 1)
            nc.gpsimd.memset(ident[:], 0.0).then_inc(consts_zero, 1)
            nc.gpsimd.memset(ones[:], 1.0).then_inc(consts_zero, 1)
            nc.gpsimd.memset(minus_half[:], -0.5).then_inc(consts_zero, 1)
            nc.gpsimd.memset(eps[:], EPS).then_inc(consts_zero, 1)
            pool.wait_ge(consts_zero, 5)
            nc.gpsimd.affine_select(out=ident[:], in_=ident[:], compare_op=ALU.not_equal, fill=1.0, base=0,
                                    pattern=[[-1, P]], channel_multiplier=1).then_inc(consts_made, 1)
            nc.gpsimd.affine_select(out=before_f[:], in_=ones[:], compare_op=ALU.is_gt, fill=0.0, base=0,
                                    pattern=[[1, P]], channel_multiplier=-1).then_inc(consts_made, 1)
            for to, step, n in ((expert_ids, 1, E), (region_start, REGION, E), (picks_sum, REGION // P, E), (tile_ids, 1, NT)):
                nc.gpsimd.iota(to[:], pattern=[[step, n]], base=0, channel_multiplier=0,
                               allow_small_or_imprecise_dtypes=True).then_inc(consts_made, 1)
            pool.wait_ge(consts_made, 2)
            nc.gpsimd.tensor_copy(before[:], before_f[:]).then_inc(consts_made, 1)
            nc.gpsimd.tensor_copy(ones_h[:], ones[:]).then_inc(consts_made, 1)
            pool.wait_ge(consts_made, 8)
            for i in range(2):
                other = slice((1 - i) * DH, (2 - i) * DH)
                if i:
                    pool.wait_ge(halves_filled, 2)
                nc.gpsimd.memset(wq_head[other, :, i, :], 1.0 / D).then_inc(halves_filled, 1)
                nc.gpsimd.memset(wout_sb[other, :, i, :], 0.0).then_inc(halves_filled, 1)
            pool.wait_ge(halves_filled, 4)
            pool.wait_ge(ctx_stats, 1)
            nc.gpsimd.tensor_tensor(c_rstd[:], c_rstd[:], minus_half[0:M, 0:B], ALU.pow).then_inc(ctx_rstd, 1)
            pool.wait_ge(x_stats_made, 1)
            nc.gpsimd.tensor_tensor(x_rstd[:], x_rstd[:], minus_half[:], ALU.pow).then_inc(x_rstd_pow, 1)
            pool.wait_ge(x_var2_made, 1)
            nc.gpsimd.tensor_tensor(x_var2[:], x_var2[:], minus_half[:], ALU.pow).then_inc(x_rstd_pow2, 1)

            def step(s, c):
                if has(s, 3):
                    pool.wait_ge(y_stats_made, s - 2)
                    nc.gpsimd.tensor_tensor(y_var[:], y_mv[:, 1:2], eps[:], ALU.add).then_inc(y_var_made, 1)
                    pool.wait_ge(y_var_made, s - 2)
                    nc.gpsimd.tensor_tensor(y_rstd[:], y_var[:], minus_half[:, 0:1], ALU.pow).then_inc(y_rstd_made, 1)
                if has(s, 1):
                    i = (c - 1) % 2
                    p = prob[i][:].rearrange("p (h k) -> p h k", h=H)
                    pool.wait_ge(inv_done, s)
                    nc.gpsimd.tensor_tensor(p, p, row_inv[i][:].unsqueeze(2).to_broadcast([P, H, M]), ALU.mult
                                            ).then_inc(prob_ready, 1)
                if has(s, 4):
                    i = (c - 4) % 4
                    pool.wait_ge(slot_ready, s - 3)
                    pool.sem_inc(scatters_begun, 1)
                    for k in range(2):
                        nc.gpsimd.indirect_dma_start(
                            expert_in, bass.IndirectOffsetOnAxis(ap=top_slot[i][:, k:k + 1], axis=0),
                            xn[i][:], None).then_inc(scattered[i], 16)

            all_steps(pool, step)

            for i in range(2):
                pool.wait_ge(res_stored[i], 16 * (NT // 2 + 1))
            with pool.Fori(0, T // 4) as it:
                for u in range(4):
                    pool.wait_ge(rows_picked, it * 4 + (u + 1))
                    pool.sem_inc(gathers_begun, 1)
                    for k, y in enumerate((y1, y2)):
                        nc.gpsimd.indirect_dma_start(
                            y[u][:], None, expert_out,
                            bass.IndirectOffsetOnAxis(ap=pick_row[u][:, k:k + 1], axis=0)).then_inc(gathered[u], 16)

        @block.scalar
        def _(act):
            def empty(n, to, src):
                act.wait_ge(prep_made, n + 1)
                nc.scalar.activation(to, src, ACT.Copy).then_inc(prep_moved, 1)

            act.wait_ge(small_loaded, 96)
            for k in range(KT):
                act.wait_ge(prep_made, k + 1)
                nc.scalar.activation(c_t[:, k, :], prep_bank(k)[:, 0:BM], ACT.Identity,
                                     bias=ln_cols[:, 1, k:k + 1], scale=ln_cols[:, 0, k:k + 1]).then_inc(prep_moved, 1)
            for c in range(PAIRS):
                empty(PREP_V + c, v_t[:, c, :], prep_bank(PREP_V + c)[:, 0:BM])
            for c in range(PAIRS):
                act.wait_ge(prep_made, PREP_WQ + c + 1)
                for i in range(2):
                    rows = slice(i * DH, (i + 1) * DH)
                    ins = nc.scalar.activation(wq_head[rows, c, i, :], prep_bank(PREP_WQ + c)[rows, 0:D], ACT.Copy)
                ins.then_inc(prep_moved, 1)
            for m in range(VALS):
                g, r, c = val_place(m)
                n = context_rows(r)
                act.wait_ge(mat_made, m + 1)
                if g and c == 0:
                    act.wait_ge(val_stored[r], 32 * len(BATCH_PARTS[r]) * g)
                nc.scalar.activation(val_st[r][0][0:n, 2 * c:2 * c + 2, :],
                                     bank[m % 8][0:n, :].rearrange("p (h n) -> p h n", h=2), ACT.Copy).then_inc(mat_hi, 1)
            for r in range(CR):
                act.wait_ge(val_stored[r], 32 * len(BATCH_PARTS[r]) * STORES)
            for m in range(VALS, MATS):
                h, k = key_place(m)
                at = k * HK + h * M
                act.wait_ge(mat_made, m + 1)
                nc.scalar.activation(keymat[0][:, :, at:at + M], bank[m % 8][:, 0:BM].rearrange("p (b k) -> p b k", b=B),
                                     ACT.Copy).then_inc(mat_hi, 1)

            def normed_plus_one(t, i):
                nc.scalar.activation(zn[i][:], xs[:, bass.ds(t * D, D)], ACT.Identity,
                                     bias=x_off[:, bass.ds(t, 1)], scale=x_rstd[:, bass.ds(t, 1)]).then_inc(zn_ready, 1)

            def turn_move(s, c):
                act.wait_ge(turn_done, s + 2)
                src = bank[5].rearrange("p (k n) -> p k n", n=P)
                if has(s, -1):
                    ins = nc.scalar.activation(zn_t[(c + 1) % 2][0][:], src[:, 0:KT, :], ACT.Copy)
                if has(s, 3):
                    ins = nc.scalar.activation(xn_t[(c - 3) % 2][:], src[:, KT:2 * KT, :], ACT.Copy)
                ins.then_inc(turn_moved, 1)

            def prob_round(t, c, g):
                act.wait_ge(prob_turned, t * NG + (g + 1))
                c0, c1 = PT_GROUPS[g]
                for rows, m0, m1 in turned_chunks(c0, c1):
                    ins = nc.scalar.activation(prob_t[c % 2][0][0:rows, m0:m1, :],
                                               turned_bank(c, g, rows, m0 - c0, m1 - c0), ACT.Copy)
                ins.then_inc(prob_moved, 1)

            def step(s, c):
                if has(s, 2):
                    for g in range(NG - 1):
                        prob_round(s - 2, c - 2, g)
                if has(s, -1):
                    normed_plus_one(s + 1, (c + 1) % 2)
                if has(s, 2):
                    prob_round(s - 2, c - 2, NG - 1)
                if turns(s):
                    turn_move(s, c)
                if has(s, 0):
                    act.wait_ge(scores_moved, s + 1)
                    nc.scalar.activation(prob[c % 2][:], prob[c % 2][:], ACT.Exp).then_inc(exp_done, 1)

            act.wait_ge(x_off_made, 1)
            normed_plus_one(0, 0)
            turn_move(-1, -1)
            all_steps(act, step)
            act.wait_ge(gap_done, 1)
            nc.scalar.activation(gap_exp[:], logit_gap[:], ACT.Exp).then_inc(gap_done, 1)

            def tok_move(j, i):
                act.wait_ge(tok_turned, j + 1)
                nc.scalar.activation(tok_t[i][0][:].rearrange("p k n -> p (k n)"), bank[4 + i], ACT.Copy).then_inc(tok_moved, 1)

            def round_pieces(j, i, u):
                loads, sem_ = (j // 2 if isinstance(j, int) else (j - i) // 2), (wgu_loaded if u < UNITS - 1 else wd_loaded)[i]
                act.wait_ge(sem_, loads * (48 if u < UNITS - 1 else 32) + (48 if u < UNITS - 1 else 32))
                if u == UNITS - 1 and not (isinstance(j, int) and j < 2):
                    act.wait_ge(down_done, j - 1)
                for p0, p1 in PIECES[2 * u:2 * u + 2]:
                    nc.scalar.activation(wgt_hi[i][:, p0:p1], wgt[i][:, p0:p1], ACT.Copy).then_inc(weights_hi, 1)

            def silu(j, i, u):
                q = (i * UNITS + u) % 2
                act.wait_ge(gu_done, j * UNITS + (u + 1))
                if u < UNITS - 1:
                    nc.scalar.activation(gate_act[q][:], banks[:, 2 * q:2 * q + 2, 0:W], ACT.Silu).then_inc(silu_done, 1)
                else:
                    nc.scalar.activation(gate_act[q][:, 0, :], bank[2 * q][:, 0:W], ACT.Silu)
                    nc.scalar.activation(gate_act[q][FHALF:P, 1, :], bank[2 * q + 1][0:FHALF, 0:W], ACT.Silu).then_inc(silu_done, 1)

            def hid_round(j, i, u):
                q = (i * UNITS + u) % 2
                act.wait_ge(hid_made, j * UNITS + (u + 1))
                if u < UNITS - 1:
                    nc.scalar.activation(hid[i][0][:, 2 * u:2 * u + 2, :], hid_f[q][:], ACT.Copy).then_inc(hid_hi, 1)
                else:
                    nc.scalar.activation(hid[i][0][:, FC - 2, :], hid_f[q][:, 0, :], ACT.Copy)
                    nc.scalar.activation(hid[i][0][0:FHALF, FC - 1, :], hid_f[q][0:FHALF, 1, :], ACT.Copy).then_inc(hid_hi, 1)

            def res_move(j, i):
                act.wait_ge(down_done, j + 1)
                act.wait_ge(res_stored[i], ((j - i) // 2) * 16 + 16)
                nc.scalar.activation(res[i][:].rearrange("p a n -> p (a n)"), bank[6 + i], ACT.Copy).then_inc(res_ready, 1)

            def expert_step(j, i, ahead=True, behind=True):
                for u in range(UNITS):
                    silu(j, i, u)
                    if ahead:
                        round_pieces(j + 1, 1 - i, u)
                    hid_round(j, i, u)
                    if u == UNITS - 2:
                        if ahead:
                            tok_move(j + 1, 1 - i)
                        if behind:
                            res_move(j - 1, 1 - i)

            act.wait_ge(pads_zeroed, 1)
            for u in range(UNITS):
                round_pieces(0, 0, u)
            tok_move(0, 0)
            expert_step(0, 0, behind=False)
            for j in range(1, 3):
                expert_step(j, j % 2)
            with act.Fori(0, (NT - 4) // 2) as it:
                for u in range(2):
                    expert_step(it * 2 + (3 + u), 1 - u)
            expert_step(NT - 1, 1, ahead=False)
            res_move(NT - 1, 1)

        @block.tensor
        def _(pe):
            def fill(n):
                if n >= 4:
                    pe.wait_ge(prep_moved, n - 3)
                return prep_bank(n)

            pe.wait_ge(consts_made, 2)
            pe.wait_ge(ctx_normed, 1)
            for k in range(KT):
                to = fill(k)
                for b in range(B):
                    mm = nc.tensor.transpose(to[:, b * M:(b + 1) * M], c_sb[:, b, k * P:(k + 1) * P], ident[0:M, 0:M])
                mm.then_inc(prep_made, 1)
            pe.wait_ge(prep_moved, KT)
            pe.wait_ge(wkv_loaded, 16)

            def turned_kv(to, c):
                for k in range(KT):
                    mm = nc.tensor.matmul(to[:, 0:BM], wkv_sb[:, k, c * P:(c + 1) * P], c_t[:, k, :],
                                          start=k == 0, stop=k == KT - 1)
                return mm

            for c in range(PAIRS):
                if c >= 4:
                    pe.wait_ge(keys_moved, c - 3)
                turned_kv(bank[4 + c % 4], c).then_inc(keys_made, 1)
                turned_kv(fill(PREP_V + c), PAIRS + c).then_inc(prep_made, 1)
            pe.wait_ge(mix_made, 1)
            pe.wait_ge(wq_loaded, 16)
            for c in range(PAIRS):
                to = fill(PREP_WQ + c)
                for k in range(KT):
                    mm = nc.tensor.matmul(to[:, 0:D], wq_sb[:, k, c * P:(c + 1) * P], mix[:, k, :],
                                          start=k == 0, stop=k == KT - 1)
                mm.then_inc(prep_made, 1)
            pe.wait_ge(prep_moved, PREP)
            pe.wait_ge(keys_moved, PAIRS)
            pe.wait_ge(halves_filled, 4)
            pe.wait_ge(wout_loaded, 32)
            for m in range(VALS):
                g, r, c = val_place(m)
                n = context_rows(r)
                c += g * STORE_PAIRS
                if m >= 8:
                    pe.wait_ge(mat_lo, m - 7)
                nc.tensor.matmul(bank[m % 8][0:n, :], v_t[:, c, r * P:r * P + n], wout_sb[:, c, :, :].rearrange("p h n -> p (h n)"),
                                 start=True, stop=True).then_inc(mat_made, 1)
            for m in range(VALS, MATS):
                h, k = key_place(m)
                pe.wait_ge(mat_lo, m - 7)
                nc.tensor.matmul(bank[m % 8][:, 0:BM], wq_head[:, h // 2, h % 2, k * P:(k + 1) * P], k_head[:, h // 2, h % 2, :],
                                 start=True, stop=True).then_inc(mat_made, 1)
            pe.wait_ge(mat_lo, MATS)

            def turn(s, c):
                if c >= 0:
                    pe.wait_ge(turn_moved, turn_count(s))
                    pe.wait_ge(zn_split, s + 1 if has(s, 0) else T)
                if has(s, -1):
                    pe.wait_ge(zn_ready, s + 2)
                    for k in range(KT):
                        mm = nc.tensor.transpose(bank[5][:, k * P:(k + 1) * P], zn[(c + 1) % 2][:, k * P:(k + 1) * P], ident[:])
                if has(s, 3):
                    pe.wait_ge(xn_ready, s - 2)
                    for k in range(KT):
                        mm = nc.tensor.transpose(bank[5][:, (KT + k) * P:(KT + k + 1) * P],
                                                 xn[(c - 3) % 4][:, k * P:(k + 1) * P], ident[:])
                mm.then_inc(turn_done, 1)

            def scores(s, c, i):
                h0, h1 = SCORE_BANKS[i]
                b = batch_of(s, c)
                for k in range(KT):
                    at = k * HK + h0 * M
                    mm = product(bank[i][:, 0:(h1 - h0) * M], [z[:, k, :] for z in zn_t[c % 2]],
                                 [part_of(z, b)[:, at:at + (h1 - h0) * M] for z in keymat], k == 0, k == KT - 1)
                return mm

            def turn_probs(t, c, g):
                c0, c1 = PT_GROUPS[g]
                if c * NG + g >= 2:
                    pe.wait_ge(prob_split, t * NG + (g - 1))
                for m in range(c0, c1):
                    n = P if m < KC - 1 else KLAST
                    mm = nc.tensor.transpose(bank[3 + (c * NG + g) % 2][0:n, (m - c0) * P:(m - c0 + 1) * P],
                                             prob[c % 2][:, m * P:m * P + n], ident[:])
                mm.then_inc(prob_turned, 1)

            def attend(t, c, g):
                pe.wait_ge(prob_split, t * NG + (g + 1))
                b = batch_of(t, c)
                for m in range(*PT_GROUPS[g]):
                    n = P if m < KC - 1 else KLAST
                    mm = product(bank[6][:, 0:D], [p[0:n, m, :] for p in prob_t[c % 2]],
                                 [half_of(v, b)[0:n, m, :] for v in valmat], m == 0, m == KC - 1)
                return mm

            def step(s, c):
                if has(s, 2):
                    pe.wait_ge(prob_ready, s - 1)
                    for g in range(NG - 1):
                        turn_probs(s - 2, c - 2, g)
                if has(s, 0):
                    pe.wait_ge(zn_split, s + 1)
                    if c:
                        pe.wait_ge(scores_moved, s)
                    scores(s, c, 0)
                if has(s, 2):
                    turn_probs(s - 2, c - 2, NG - 1)
                if has(s, 0):
                    for i in range(1, len(SCORE_BANKS)):
                        mm = scores(s, c, i)
                    mm.then_inc(scores_done, 1)
                if turns(s):
                    turn(s, c)
                if has(s, 2):
                    if (c - 2) % UNROLL == 0:
                        pe.wait_ge(valmat_loaded, batch_of(s - 2, c - 2) * VAL_LOAD + VAL_LOAD)
                    if c > 2:
                        pe.wait_ge(att_added, s - 2)
                    attend(s - 2, c - 2, 0)
                if has(s, 3):
                    pe.wait_ge(turn_moved, turn_count(s) + 1)
                    if c > 3:
                        pe.wait_ge(slot_ready, s - 3)
                    for k in range(KT):
                        mm = nc.tensor.matmul(bank[7][:, 0:E], xn_t[(c - 3) % 2][:, k, :], wr_sb[:, k, :],
                                              start=k == 0, stop=k == KT - 1)
                    mm.then_inc(logits_done, 1)
                if has(s, 2):
                    for g in range(1, NG):
                        mm = attend(s - 2, c - 2, g)
                    mm.then_inc(att_done, 1)
                if has(s, 3):
                    pe.wait_ge(picks_ready, s - 2)
                    nc.tensor.matmul(bank[7][:, 16:16 + E], before[:], picks[:], start=True, stop=False)
                    nc.tensor.matmul(bank[7][:, 16:16 + E], ones_h[:], picks_sum[:], start=False, stop=True
                                     ).then_inc(ranks_done, 1)

            turn(-1, -1)
            all_steps(pe, step)

            pe.wait_ge(slot_ready, T)
            nc.tensor.matmul(bank[7][:, 16:16 + E], ones_h[:], picks_sum[:], start=True, stop=True).then_inc(ranks_done, 1)

            def tok_turn(j, i):
                pe.wait_ge(tok_loaded[i], (j // 2 if isinstance(j, int) else (j - i) // 2) * 16 + 16)
                if not (isinstance(j, int) and j < 2):
                    pe.wait_ge(tok_split, j - 1)
                for k in range(KT):
                    for a in range(WB):
                        mm = nc.tensor.transpose(bank[4 + i][:, k * W + a * P:k * W + (a + 1) * P],
                                                 tok[i][:, a, k * P:(k + 1) * P], ident[:])
                mm.then_inc(tok_turned, 1)

            def gate_up(j, i, u):
                q = (i * UNITS + u) % 2
                pe.wait_ge(weights_split, j * len(PIECES) + 2 * KT)
                pe.wait_ge(tok_split, j + 1)
                if not (isinstance(j, int) and j * UNITS + u < 2):
                    pe.wait_ge(hid_made, j * UNITS + (u - 1))
                w = [gate_up_of(x) for x in (wgt_hi[i], wgt_lo[i])]
                for f in range(2 * u, 2 * u + 2):
                    starts = [(0, f * P), (W, FI + FHALF + f * P)] if f < FC - 1 else [(0, FULL)]
                    for at, col in starts:
                        for k in range(KT):
                            mm = product(bank[2 * q + f % 2][:, at:at + W], [x[:, k, col:col + P] for x in w],
                                         [x[:, k, :] for x in tok_t[i]], k == 0, k == KT - 1)
                mm.then_inc(gu_done, 1)

            def down(j, i):
                pe.wait_ge(weights_split, j * len(PIECES) + len(PIECES))
                pe.wait_ge(hid_ready, j * UNITS + UNITS)
                if not (isinstance(j, int) and j < 2):
                    pe.wait_ge(res_ready, j - 1)
                w = [down_of(x) for x in (wgt_hi[i], wgt_lo[i])]
                for a in range(WB):
                    for f in range(FC):
                        mm = product(bank[6 + i][:, a * D:(a + 1) * D], [x[:, f, a * P:(a + 1) * P] for x in hid[i]],
                                     [x[:, f, :] for x in w], f == 0, f == FC - 1)
                mm.then_inc(down_done, 1)

            def expert_step(j, i, ahead=True, behind=True):
                for u in range(UNITS):
                    gate_up(j, i, u)
                    if u == UNITS - 2:
                        if ahead:
                            tok_turn(j + 1, 1 - i)
                        if behind:
                            down(j - 1, 1 - i)

            tok_turn(0, 0)
            expert_step(0, 0, behind=False)
            for j in range(1, 3):
                expert_step(j, j % 2)
            with pe.Fori(0, (NT - 4) // 2) as it:
                for u in range(2):
                    expert_step(it * 2 + (3 + u), 1 - u)
            expert_step(NT - 1, 1, ahead=False)
            down(NT - 1, 1)

        @block.vector
        def _(dve):
            def settle():
                dve.drain()

            dve.wait_ge(ctx_loaded, 16)
            for b in range(B):
                nc.vector.bn_stats(c_stats[:, b, :], c_sb[:, b, :])
            settle()
            for b in range(B):
                nc.vector.bn_aggr(c_mv[:, b, :], c_stats[:, b, :])
            settle()
            nc.vector.tensor_scalar(c_rstd[:], c_mv[:, :, 1], EPS, None, ALU.add).then_inc(ctx_stats, 1)
            dve.wait_ge(ctx_rstd, 1)
            for b in range(B):
                ins = nc.vector.tensor_scalar(c_sb[:, b, :], c_sb[:, b, :], c_mv[:, b, 0:1], c_rstd[:, b:b + 1],
                                              ALU.subtract, ALU.mult)
            ins.then_inc(ctx_normed, 1)
            dve.wait_ge(small_loaded, 96)
            dve.wait_ge(consts_zero, 5)
            dve.wait_ge(consts_made, 1)
            nc.vector.tensor_tensor(q_mix[:], ln_cols[:, 3, :], ln_cols[:, 2, :], ALU.subtract)
            nc.vector.tensor_scalar(side_scale[:], side[:], 1.0, QK_SCALE, ALU.add, ALU.mult)
            nc.vector.tensor_scalar(side_shift[:], side[:], QK_SCALE, None, ALU.mult)
            settle()
            nc.vector.tensor_scalar(q_mix[:], q_mix[:], 1.0 / D, None, ALU.mult)
            settle()
            for k in range(KT):
                nc.vector.tensor_scalar(mix[:, k, :], zeros[:, 0:D], q_mix[:, k:k + 1], None, ALU.add)
            settle()
            for k in range(KT):
                ins = nc.vector.tensor_scalar(mix[:, k, k * P:(k + 1) * P], ident[:], ln_cols[:, 2, k:k + 1], q_mix[:, k:k + 1],
                                              ALU.mult, ALU.add)
            ins.then_inc(mix_made, 1)
            for c in range(PAIRS):
                dve.wait_ge(keys_made, c + 1)
                for i in range(2):
                    own = slice(i * DH, (i + 1) * DH)
                    other = slice((1 - i) * DH, (2 - i) * DH)
                    keys = bank[4 + c % 4][own, 0:BM].rearrange("p (b k) -> p b k", b=B)
                    for rows, by in ((own, side_scale), (other, side_shift)):
                        ins = nc.vector.tensor_tensor(k_head[rows, c, i, :].rearrange("p (b k) -> p b k", b=B), keys,
                                                      by[own, :, 2 * c + i].unsqueeze(2).to_broadcast([DH, B, M]), ALU.mult)
                ins.then_inc(keys_moved, 1)

            def mat_rest(m):
                dve.wait_ge(mat_hi, m + 1)
                if m < VALS:
                    g, r, c = val_place(m)
                    n = context_rows(r)
                    hi, lo = (z[0:n, 2 * c:2 * c + 2, :] for z in val_st[r])
                    src = bank[m % 8][0:n, :].rearrange("p (h n) -> p h n", h=2)
                    if g and c == 0:
                        dve.wait_ge(val_stored[r], 32 * len(BATCH_PARTS[r]) * g)
                else:
                    h, k = key_place(m)
                    at = k * HK + h * M
                    hi, lo = (z[:, :, at:at + M] for z in keymat)
                    src = bank[m % 8][:, 0:BM].rearrange("p (b k) -> p b k", b=B)
                nc.vector.tensor_tensor(lo, src, hi.bitcast(F32), ALU.subtract).then_inc(mat_lo, 1)

            for m in range(VALS):
                mat_rest(m)
            dve.wait_ge(x_loaded, 16 * B)
            with dve.Fori(0, T // 4) as it:
                for u in range(4):
                    t = it * 4 + u
                    nc.vector.bn_stats(x_stats[:, bass.ds(t, 1), :].rearrange("p a s -> p (a s)"), xs[:, bass.ds(t * D, D)])
            settle()
            nc.vector.tensor_tensor(x_mean[:], x_stats[:, :, 1], x_stats[:, :, 4], ALU.add)
            nc.vector.tensor_tensor(x_odd[:], x_stats[:, :, 4], x_stats[:, :, 1], ALU.subtract)
            nc.vector.tensor_tensor(x_var[:], x_stats[:, :, 2], x_stats[:, :, 5], ALU.add)
            settle()
            nc.vector.tensor_scalar(x_mean[:], x_mean[:], 0.5, None, ALU.mult)
            nc.vector.scalar_tensor_tensor(out=x_odd[:], in0=x_odd[:], scalar=0.25, in1=x_odd[:], op0=ALU.mult, op1=ALU.mult)
            settle()
            nc.vector.scalar_tensor_tensor(out=x_var[:], in0=x_var[:], scalar=1.0 / D, in1=x_odd[:], op0=ALU.mult, op1=ALU.add)
            settle()
            nc.vector.tensor_scalar(x_rstd[:], x_var[:], EPS, None, ALU.add).then_inc(x_stats_made, 1)
            third = (MATS - VALS) // 3
            for m in range(VALS, VALS + third):
                mat_rest(m)
            dve.wait_ge(x_rstd_pow, 1)
            nc.vector.tensor_tensor(x_var2[:], x_var[:], x_rstd[:], ALU.mult)
            settle()
            nc.vector.tensor_tensor(x_var2[:], x_var2[:], x_rstd[:], ALU.mult)
            settle()
            nc.vector.tensor_scalar(x_var2[:], x_var2[:], EPS, None, ALU.add).then_inc(x_var2_made, 1)
            for m in range(VALS + third, MATS):
                mat_rest(m)
            dve.wait_ge(x_rstd_pow2, 1)
            nc.vector.tensor_tensor(x_rstd[:], x_rstd[:], x_var2[:], ALU.mult)
            settle()
            nc.vector.scalar_tensor_tensor(out=x_off[:], in0=x_mean[:], scalar=-1.0, in1=x_rstd[:], op0=ALU.mult, op1=ALU.mult)
            settle()
            nc.vector.tensor_scalar(x_off[:], x_off[:], 1.0, None, ALU.add).then_inc(x_off_made, 1)

            def zn_rest(s, c):
                dve.wait_ge(turn_moved, s + 2)
                to = zn_t[(c + 1) % 2]
                nc.vector.tensor_tensor(to[1][:], bank[5][:, 0:KT * P].rearrange("p (k n) -> p k n", n=P), to[0][:].bitcast(F32),
                                        ALU.subtract).then_inc(zn_split, 1)

            def prob_rest(t, c, g):
                c0, c1 = PT_GROUPS[g]
                dve.wait_ge(prob_moved, t * NG + (g + 1))
                for rows, m0, m1 in turned_chunks(c0, c1):
                    hi, lo = (p[0:rows, m0:m1, :] for p in prob_t[c % 2])
                    ins = nc.vector.tensor_tensor(lo, turned_bank(c, g, rows, m0 - c0, m1 - c0), hi.bitcast(F32), ALU.subtract)
                ins.then_inc(prob_split, 1)

            def add_attention(t):
                dve.wait_ge(att_done, t + 1)
                row = xs[:, bass.ds(t * D, D)]
                nc.vector.tensor_tensor(row, row, bank[6][:, 0:D], ALU.add).then_inc(att_added, 1)
                settle()
                nc.vector.bn_stats(y_stats[:], row)
                settle()
                nc.vector.bn_aggr(y_mv[:], y_stats[:]).then_inc(y_stats_made, 1)

            def normalise(t, c):
                dve.wait_ge(y_rstd_made, t + 1)
                if c >= 4:
                    dve.wait_ge(scattered[c % 4], ((t - c) // 4 + c // 4) * 32)
                nc.vector.tensor_scalar(xn[c % 4][:], xs[:, bass.ds(t * D, D)], y_mv[:, 0:1], y_rstd[:],
                                        ALU.subtract, ALU.mult).then_inc(xn_ready, 1)

            def softmax_in(t, c):
                dve.wait_ge(scores_done, t + 1)
                for i, (h0, h1) in enumerate(SCORE_BANKS):
                    nc.vector.tensor_reduce(row_max[:, h0:h1], bank[i][:, 0:(h1 - h0) * M].rearrange("p (h k) -> p h k", k=M),
                                            AX_X, ALU.max)
                settle()
                for i, (h0, h1) in enumerate(SCORE_BANKS):
                    ins = nc.vector.tensor_tensor(
                        prob[c % 2][:, h0 * M:h1 * M].rearrange("p (h k) -> p h k", k=M),
                        bank[i][:, 0:(h1 - h0) * M].rearrange("p (h k) -> p h k", k=M),
                        row_max[:, h0:h1].unsqueeze(2).to_broadcast([P, h1 - h0, M]), ALU.subtract)
                ins.then_inc(scores_moved, 1)

            def softmax_sum(t, c):
                dve.wait_ge(exp_done, t + 1)
                nc.vector.tensor_reduce(row_sum[c % 2][:], prob[c % 2][:].rearrange("p (h k) -> p h k", k=M), AX_X, ALU.add)
                settle()
                nc.vector.reciprocal(row_inv[c % 2][:], row_sum[c % 2][:]).then_inc(inv_done, 1)

            def route(t):
                dve.wait_ge(logits_done, t + 1)
                nc.vector.tensor_copy(logits[:], bank[7][:, 0:E])
                settle()
                nc.vector.max(top8[:], logits[:])
                settle()
                nc.vector.max_index(top8_id[:], top8[:], logits[:])
                nc.vector.tensor_tensor(logit_gap[:, bass.ds(t, 1)], top8[:, 1:2], top8[:, 0:1], ALU.subtract)
                settle()
                nc.vector.tensor_tensor(pick[:], expert_ids[:].unsqueeze(1).to_broadcast([P, 2, E]),
                                        top8_id[:, 0:2].unsqueeze(2).to_broadcast([P, 2, E]), ALU.is_equal)
                settle()
                nc.vector.tensor_tensor(picks[:], pick[:, 0, :], pick[:, 1, :], ALU.add).then_inc(picks_ready, 1)

            def allot(t, c):
                dve.wait_ge(ranks_done, t + 1)
                nc.vector.tensor_tensor(picked[:], pick[:], bank[7][:, 16:16 + E].unsqueeze(1).to_broadcast([P, 2, E]), ALU.mult)
                nc.vector.tensor_tensor(picks_sum[:], picks_sum[:], picks[:], ALU.add)
                settle()
                nc.vector.tensor_reduce(slot_f[:], picked[:], AX_X, ALU.add)
                settle()
                nc.vector.tensor_copy(slots[:, bass.ds(t * 2, 2)], slot_f[:])
                nc.vector.tensor_copy(top_slot[c % 4][:], slot_f[:]).then_inc(slot_ready, 1)

            def step(s, c):
                if has(s, 3):
                    add_attention(s - 3)
                if has(s, 2):
                    for g in range(NG - 1):
                        prob_rest(s - 2, c - 2, g)
                if has(s, 3):
                    normalise(s - 3, c - 3)
                if has(s, 4):
                    allot(s - 4, c - 4)
                if has(s, 2):
                    prob_rest(s - 2, c - 2, NG - 1)
                if has(s, 1):
                    softmax_sum(s - 1, c - 1)
                if has(s, 0):
                    softmax_in(s, c)
                if has(s, -1):
                    zn_rest(s, c)
                if has(s, 3):
                    route(s - 3)

            dve.wait_ge(consts_made, 8)
            zn_rest(-1, -1)
            all_steps(dve, step)
            dve.wait_ge(ranks_done, T + 1)
            nc.vector.tensor_copy(next_row[:], bank[7][:, 16:16 + E])
            settle()

            for i in range(2):
                nc.vector.memset(down_of(wgt[i])[FHALF:P, FC - 1, :], 0.0)
                for part in hid[i]:
                    ins = nc.vector.memset(part[FHALF:P, FC - 1, :].bitcast(U32), 0)
            ins.then_inc(pads_zeroed, 1)

            nc.vector.tensor_tensor(count[:], next_row[:], region_start[:], ALU.subtract)
            nc.vector.tensor_copy(tail_row[:], next_row[:])
            settle()
            nc.vector.tensor_scalar(tiles_of[:], count[:], 0.0, None, ALU.is_gt)
            for n in range(1, MAX_TILES):
                settle()
                nc.vector.scalar_tensor_tensor(out=tiles_of[:], in0=count[:], scalar=float(n * W), in1=tiles_of[:],
                                               op0=ALU.is_gt, op1=ALU.add)
            settle()
            nc.vector.tensor_tensor_scan(tiles_upto[:], ones[:, 0:E], tiles_of[:], 0.0, ALU.mult, ALU.add)
            nc.vector.tensor_scalar(jump[:], tiles_of[:], -float(W), float(REGION), ALU.mult, ALU.add)
            settle()
            nc.vector.tensor_tensor(past[:], tile_ids[:].unsqueeze(2).to_broadcast([P, NT, E]),
                                    tiles_upto[:].unsqueeze(1).to_broadcast([P, NT, E]), ALU.is_ge)
            settle()
            nc.vector.tensor_reduce(table_f[:, 0, :], past[:], AX_X, ALU.add)
            settle()
            nc.vector.tensor_tensor(past[:], past[:], jump[:].unsqueeze(1).to_broadcast([P, NT, E]), ALU.mult)
            nc.vector.tensor_scalar(table_f[:, 0, :], table_f[:, 0, :], float(E - 1), None, ALU.min)
            settle()
            nc.vector.tensor_reduce(table_f[:, 1, :], past[:], AX_X, ALU.add)
            settle()
            nc.vector.scalar_tensor_tensor(out=table_f[:, 1, :], in0=tile_ids[:], scalar=float(W), in1=table_f[:, 1, :],
                                           op0=ALU.mult, op1=ALU.add)
            settle()
            nc.vector.tensor_copy(tile_table[:], table_f[:]).then_inc(table_ready, 1)
            nc.vector.tensor_scalar(lead[:], tiles_of[:], float(W), -float(REGION), ALU.mult, ALU.add)
            nc.vector.tensor_copy(result_f[:], slots[:])
            for e in range(1, E):
                nc.vector.tensor_scalar(slots_past[:], slots[:], region_start[:, e:e + 1], None, ALU.is_ge)
                settle()
                nc.vector.scalar_tensor_tensor(out=result_f[:], in0=slots_past[:], scalar=lead[:, e - 1:e], in1=result_f[:],
                                               op0=ALU.mult, op1=ALU.add)
                settle()
            nc.vector.tensor_copy(result_row[:], result_f[:])
            nc.vector.tensor_copy(gate2[:], logit_gap[:]).then_inc(gap_done, 1)
            dve.wait_ge(gap_done, 2)
            nc.vector.tensor_scalar(gate_den[:], gap_exp[:], 1.0, None, ALU.add)
            settle()
            nc.vector.reciprocal(gate1[:], gate_den[:])
            settle()
            nc.vector.tensor_tensor(gate2[:], gap_exp[:], gate1[:], ALU.mult)

            def tok_rest(j, i):
                dve.wait_ge(tok_moved, j + 1)
                nc.vector.tensor_tensor(tok_t[i][1][:].rearrange("p k n -> p (k n)"), bank[4 + i],
                                        tok_t[i][0][:].rearrange("p k n -> p (k n)").bitcast(F32), ALU.subtract).then_inc(tok_split, 1)

            def rest_pieces(j, i, u):
                for n in range(2 * u, 2 * u + 2):
                    p0, p1 = PIECES[n]
                    dve.wait_ge(weights_hi, j * len(PIECES) + (n + 1))
                    nc.vector.tensor_tensor(wgt_lo[i][:, p0:p1], wgt[i][:, p0:p1], wgt_hi[i][:, p0:p1].bitcast(F32), ALU.subtract
                                            ).then_inc(weights_split, 1)

            def hidden(j, i, u):
                q = (i * UNITS + u) % 2
                dve.wait_ge(silu_done, j * UNITS + (u + 1))
                if u < UNITS - 1:
                    nc.vector.tensor_tensor(hid_f[q][:], gate_act[q][:], banks[:, 2 * q:2 * q + 2, W:2 * W], ALU.mult).then_inc(hid_made, 1)
                else:
                    nc.vector.tensor_tensor(hid_f[q][:, 0, :], gate_act[q][:, 0, :], bank[2 * q][:, W:2 * W], ALU.mult)
                    nc.vector.tensor_tensor(hid_f[q][0:FHALF, 1, :], gate_act[q][FHALF:P, 1, :], bank[2 * q + 1][FHALF:P, 0:W], ALU.mult
                                            ).then_inc(hid_made, 1)

            def hid_rest(j, i, u):
                q = (i * UNITS + u) % 2
                dve.wait_ge(hid_hi, j * UNITS + (u + 1))
                hi, lo = hid[i]
                if u < UNITS - 1:
                    nc.vector.tensor_tensor(lo[:, 2 * u:2 * u + 2, :], hid_f[q][:], hi[:, 2 * u:2 * u + 2, :].bitcast(F32), ALU.subtract
                                            ).then_inc(hid_ready, 1)
                else:
                    nc.vector.tensor_tensor(lo[:, FC - 2, :], hid_f[q][:, 0, :], hi[:, FC - 2, :].bitcast(F32), ALU.subtract)
                    nc.vector.tensor_tensor(lo[0:FHALF, FC - 1, :], hid_f[q][0:FHALF, 1, :], hi[0:FHALF, FC - 1, :].bitcast(F32),
                                            ALU.subtract).then_inc(hid_ready, 1)

            def expert_step(j, i, ahead=True):
                for u in range(UNITS):
                    hidden(j, i, u)
                    if ahead:
                        rest_pieces(j + 1, 1 - i, u)
                    hid_rest(j, i, u)
                    if ahead and u == UNITS - 2:
                        tok_rest(j + 1, 1 - i)

            for u in range(UNITS):
                rest_pieces(0, 0, u)
            tok_rest(0, 0)
            expert_step(0, 0)
            for j in range(1, 3):
                expert_step(j, j % 2)
            with dve.Fori(0, (NT - 4) // 2) as it:
                for u in range(2):
                    expert_step(it * 2 + (3 + u), 1 - u)
            expert_step(NT - 1, 1, ahead=False)

            dve.wait_ge(res_ready, NT)

            def pick_rows(t, u):
                nc.vector.tensor_copy(pick_row[u][:], result_row[:, bass.ds(t * 2, 2)]).then_inc(rows_picked, 1)

            def finish(t, u, again):
                dve.wait_ge(gathered[u], again * 32 + 32)
                nc.vector.scalar_tensor_tensor(out=half[u % 2][:], in0=y1[u][:], scalar=gate1[:, bass.ds(t, 1)],
                                               in1=xs[:, bass.ds(t * D, D)], op0=ALU.mult, op1=ALU.add)
                settle()
                dve.wait_ge(fin_stored[u], again * 16 + 16)
                nc.vector.scalar_tensor_tensor(out=fin[u][:], in0=y2[u][:], scalar=gate2[:, bass.ds(t, 1)],
                                               in1=half[u % 2][:], op0=ALU.mult, op1=ALU.add).then_inc(fin_ready, 1)

            for u in range(4):
                pick_rows(u, u)
            with dve.Fori(0, T // 4 - 1) as it:
                for u in range(4):
                    finish(it * 4 + u, u, it)
                    pick_rows(it * 4 + (4 + u), u)
            for u in range(4):
                finish(T - 4 + u, u, T // 4 - 1)


_INS = ["x", "ctx_1024", "fside_Bx16_0", "L0_xattn_ln1_w", "L0_xattn_ln1_b", "L0_xattn_ln2_w", "L0_xattn_ln2_b",
        "L0_xattn_Wq", "L0_xattn_Wkv", "L0_xattn_Wout", "L0_ffn_Wr", "L0_ffn_Wg", "L0_ffn_Wu", "L0_ffn_Wd"]


def kernel(**inputs):
    import numpy as np
    import concourse.bacc as bacc
    from concourse.bass_utils import run_bass_kernel_spmd

    nc = bacc.Bacc("TRN2", target_bir_lowering=False, num_devices=1)
    arrays, args = {}, []
    for name in _INS:
        a = np.ascontiguousarray(inputs[name])
        arrays[f"in_{name}"] = a
        args.append(nc.dram_tensor(f"in_{name}", a.shape, mybir.dt.from_np(a.dtype), kind="ExternalInput").ap())
    args.append(nc.dram_tensor("result", (B, S, D), F32, kind="ExternalOutput").ap())
    program(nc, *args)
    r = run_bass_kernel_spmd(nc, [arrays], core_ids=[0])
    return r.results[0]["result"]
```

```python
from contextlib import ExitStack

import concourse.bass as bass
from concourse import mybir

F32 = mybir.dt.float32
F32R = mybir.dt.float32r
F16 = mybir.dt.float16
I32 = mybir.dt.int32
U32 = mybir.dt.uint32
ALU = mybir.AluOpType
ACT = mybir.ActivationFunctionType
AX_X = mybir.AxisListType.X

P = 128
B, S, D = 4, 1024, 256
M, H, DH = 77, 16, 64
INNER = H * DH
E, FI = 9, 704
KT = D // P
T = B * S // P
TB = S // P
HK = H * M
KC = (HK + P - 1) // P
KLAST = HK - (KC - 1) * P
PAIRS = H // 2
BM = B * M
CR = (BM + P - 1) // P
EPS = 1e-5
QK_SCALE = float(DH) ** -0.5
BATCH_PARTS = [[(max(r * P, b * M) - r * P, min(r * P + P, b * M + M) - r * P, b)
                for b in range(B) if max(r * P, b * M) < min(r * P + P, b * M + M)] for r in range(CR)]
KV_PIECES = [slice(n * INNER + i * INNER // 2, n * INNER + (i + 1) * INNER // 2) for i in range(2) for n in range(2)]
STATS_EARLY = 20
STORE_HEADS = 4
STORE_BUFFERS = 4
HEADS_IN_BANK = 512 // M
EARLY_HEADS = 4
SCORE_BANKS = [(h, min(h + HEADS_IN_BANK, H)) for h in range(0, H, HEADS_IN_BANK)]
DIRECT = len(SCORE_BANKS) - 1
PT_GROUPS = [(c, min(c + 4, KC)) for c in range(0, KC, 4)]
NG = len(PT_GROUPS)

W = 256
WB = W // P
REGION = B * S + W
NT = (2 * B * S + E * (W - 1)) // W
MAX_TILES = B * S // W
SPARE = (NT - 2 * B * S // W) * W
ROWS = E * REGION + SPARE
GATE, TOKEN = D, D + 1
ROW = D + 2
FC = (FI + P - 1) // P
FHALF = FI - (FC - 1) * P
FULL = (FC - 1) * P
UNITS = FC // 2
GU = 2 * FI
GUCOLS = KT * GU
WCOLS = GUCOLS + FC * D
PIECES = [(n * FI, (n + 1) * FI) for n in range(2 * KT)] + [(GUCOLS, WCOLS - D), (WCOLS - D, WCOLS)]
assert FHALF * 2 == P and len(PIECES) == 2 * UNITS

def program(nc, x, ctx_rows, fside, ln1_w, ln1_b, ln2_w, ln2_b, wq, wkv, wout, wr, wg, wu, wd, out):
    valmat_dram = nc.dram_tensor("valmat_dram", (B, H, M, 2, D), F32).ap()
    expert_in = nc.dram_tensor("expert_in", (ROWS, ROW), F32).ap()

    with ExitStack() as ctx:
        def sem(name):
            return ctx.enter_context(nc.semaphore(name))

        def sb(name, shape, dt=F32, on=ctx):
            return on.enter_context(nc.sbuf_tensor(name, shape, dt))

        banks = ctx.enter_context(nc.psum_tensor("banks", [P, 8, 512], F32))
        bank = [banks[:, i, :] for i in range(8)]

        xs = sb("xs", [P, T * D])
        ident = sb("ident", [P, P])
        before_f = sb("before_f", [P, P])
        ones = sb("ones", [P, P])
        before = sb("before", [P, P], F16)
        ones_h = sb("ones_h", [P, P], F16)
        blank = sb("blank", [P, WB, ROW])
        tile_steps = sb("tile_steps", [P, MAX_TILES])
        token_ids = sb("token_ids", [P, T])
        expert_ids = sb("expert_ids", [P, E])
        region_start = sb("region_start", [P, E])
        picks_sum = sb("picks_sum", [P, E], F16)
        next_row = sb("next_row", [P, E])
        tile_ids = sb("tile_ids", [P, NT])
        minus_half = sb("minus_half", [P, T])
        eps = sb("eps", [P, 1])
        wr_sb = sb("wr_sb", [P, KT, E])
        tile_table = sb("tile_table", [P, 2, NT], I32)
        tail_row = sb("tail_row", [P, E], I32)
        count = sb("count", [P, E])
        tiles_of = sb("tiles_of", [P, E])
        tiles_upto = sb("tiles_upto", [P, E])
        jump = sb("jump", [P, E])
        past = sb("past", [P, NT, E])
        fresh = sb("fresh", [P, NT], I32)
        fresh_f = sb("fresh_f", [P, NT])
        tile_used = sb("tile_used", [P, E, MAX_TILES])
        table_f = sb("table_f", [P, 2, NT])
        xn = [sb(f"xn{i}", [P, 2, ROW]) for i in range(4)]
        gap = [sb(f"gap{i}", [P, 1]) for i in range(2)]
        gap_exp = [sb(f"gap_exp{i}", [P, 1]) for i in range(2)]
        gate_den = [sb(f"gate_den{i}", [P, 1]) for i in range(2)]
        top_slot = [sb(f"top_slot{i}", [P, 2], I32) for i in range(4)]

        att = ExitStack()
        zn = [sb(f"zn{i}", [P, D], F32, att) for i in range(2)]
        zn_t = [[sb(f"zn_t{i}_{n}", [P, KT, P], F32R, att) for n in ("hi", "lo")] for i in range(2)]
        xn_t = [sb(f"xn_t{i}", [P, KT, P], F32, att) for i in range(2)]
        x_stats = sb("x_stats", [P, T, 6], F32, att)
        x_mean = sb("x_mean", [P, T], F32, att)
        x_var = sb("x_var", [P, T], F32, att)
        x_odd = sb("x_odd", [P, T], F32, att)
        x_off = sb("x_off", [P, T], F32, att)
        x_rstd = sb("x_rstd", [P, T], F32, att)
        x_var2 = sb("x_var2", [P, T], F32, att)
        y_stats = sb("y_stats", [P, 6], F32, att)
        y_mv = sb("y_mv", [P, 2], F32, att)
        y_var = sb("y_var", [P, 1], F32, att)
        y_rstd = sb("y_rstd", [P, 1], F32, att)
        row_min = [sb(f"row_min{i}", [P, H], F32, att) for i in range(2)]
        row_sum = [sb(f"row_sum{i}", [P, H], F32, att) for i in range(2)]
        row_inv = [sb(f"row_inv{i}", [P, H], F32, att) for i in range(2)]
        logits = sb("logits", [P, E], F32, att)
        top8 = sb("top8", [P, 8], F32, att)
        top8_id = sb("top8_id", [P, 8], U32, att)
        pick = sb("pick", [P, 2, E], F32, att)
        picks = sb("picks", [P, E], F16, att)
        picked = sb("picked", [P, 2, E], F32, att)
        slot_f = sb("slot_f", [P, 2], F32, att)
        prep = ExitStack()
        wkv_hi = sb("wkv_hi", [P, KT, 2 * INNER], F32R, prep)
        wkv_lo = sb("wkv_lo", [P, KT, 2 * INNER], F32R, prep)
        wq_sb = sb("wq_sb", [P, KT, INNER], F32, prep)
        wout_sb = sb("wout_sb", [P, PAIRS, 2, D], F32, prep)
        v_t = sb("v_t", [P, PAIRS, BM], F32, prep)
        c_sb = sb("c_sb", [M, B, D], F32, prep)
        c_t = sb("c_t", [P, KT, BM], F32, prep)
        mix = sb("mix", [P, KT, D], F32, prep)
        prep.close()
        keymat = [sb(f"keymat_{n}", [P, B, KT * HK], F32R, att) for n in ("hi", "lo")]
        prep = ExitStack()
        wq_head = sb("wq_head", [P, PAIRS, 2, D], F32, prep)
        k_head = sb("k_head", [P, PAIRS, 2, BM], F32, prep)
        early = ExitStack()
        wkv_sb = sb("wkv_sb", [P, KT, 2 * INNER], F32, early)
        c_stats = sb("c_stats", [M, B, 6], F32, early)
        c_mv = sb("c_mv", [M, B, 2], F32, early)
        c_rstd = sb("c_rstd", [M, B], F32, early)
        c_parts = [sb(f"c_{n}", [P, KT, BM], F32R, early) for n in ("hi", "lo")]
        ln_cols = sb("ln_cols", [P, 4, KT], F32, early)
        q_mix = sb("q_mix", [P, KT], F32, early)
        side = sb("side", [P, B, H], F32, early)
        side_scale = sb("side_scale", [P, B, H], F32, early)
        side_shift = sb("side_shift", [P, B, H], F32, early)
        early.close()
        val_st = [sb(f"val_st{i}", [P, STORE_HEADS, 2, D], F32R, prep) for i in range(STORE_BUFFERS)]
        prep.close()
        prob = [sb(f"prob{i}", [P, HK], F32, att) for i in range(2)]
        prob_t = [[sb(f"prob_t{i}_{n}", [P, KC, P], F32R, att) for n in ("hi", "lo")] for i in range(2)]
        valmat = sb("valmat", [P, 2, KC, 2, D], F32R, att)
        att.close()

        ffn = ExitStack()
        tok = [sb(f"tok{i}", [P, WB, ROW], F32, ffn) for i in range(2)]
        tok_t = [[sb(f"tok_t{i}_{n}", [P, KT, W], F32R, ffn) for n in ("hi", "lo")] for i in range(2)]
        wgt = [sb(f"wgt{i}", [P, WCOLS], F32, ffn) for i in range(2)]
        wgt_hi = [sb(f"wgt_hi{i}", [P, WCOLS], F32R, ffn) for i in range(2)]
        wgt_lo = [sb(f"wgt_lo{i}", [P, WCOLS], F32R, ffn) for i in range(2)]
        gate_act = [sb(f"gate_act{i}", [P, 2, W], F32, ffn) for i in range(2)]
        hid_f = [sb(f"hid_f{i}", [P, 2, W], F32, ffn) for i in range(2)]
        hid = [[sb(f"hid{i}_{n}", [P, FC, W], F32R, ffn) for n in ("hi", "lo")] for i in range(2)]
        res = [sb(f"res{i}", [P, WB, D], F32, ffn) for i in range(2)]
        tok_gate = [sb(f"tok_gate{i}", [P, WB], F32, ffn) for i in range(2)]
        tok_id = [sb(f"tok_id{i}", [P, WB], I32, ffn) for i in range(2)]
        ffn.close()

        def gate_up_of(w):
            return w[:, 0:GUCOLS].rearrange("p (k f) -> p k f", k=KT)

        def down_of(w):
            return w[:, GUCOLS:].rearrange("p (c n) -> p c n", c=FC)

        def product(to, a, b, first, last):
            nc.tensor.matmul(to, a[0], b[0], start=first, stop=False)
            nc.tensor.matmul(to, a[0], b[1], start=False, stop=False)
            return nc.tensor.matmul(to, a[1], b[0], start=False, stop=last)

        x_loaded = [sem(f"x_loaded{b}") for b in range(B)]
        ctx_loaded = sem("ctx_loaded")
        wkv_loaded = [sem(f"wkv_loaded{i}") for i in range(len(KV_PIECES))]
        wkv_hi_made = sem("wkv_hi_made")
        wkv_split = sem("wkv_split")
        ctx_made = sem("ctx_made")
        ctx_turned = sem("ctx_turned")
        ctx_hi = sem("ctx_hi")
        ctx_split = sem("ctx_split")
        wq_loaded = sem("wq_loaded")
        wout_loaded = sem("wout_loaded")
        small_loaded = sem("small_loaded")
        consts_zero = sem("consts_zero")
        consts_made = sem("consts_made")
        ctx_stats = sem("ctx_stats")
        ctx_rstd = sem("ctx_rstd")
        ctx_normed = sem("ctx_normed")
        mix_made = sem("mix_made")
        x_stats_made = sem("x_stats_made")
        x_rstd_pow = sem("x_rstd_pow")
        x_var2_made = sem("x_var2_made")
        x_rstd_pow2 = sem("x_rstd_pow2")
        halves_filled = sem("halves_filled")
        prep_made = sem("prep_made")
        prep_moved = sem("prep_moved")
        keys_made = sem("keys_made")
        keys_moved = sem("keys_moved")
        mat_made = sem("mat_made")
        mat_hi = sem("mat_hi")
        mat_lo = sem("mat_lo")
        val_stored = [sem(f"val_stored{i}") for i in range(STORE_BUFFERS)]
        valmat_loaded = sem("valmat_loaded")
        x_off_made = sem("x_off_made")
        zn_ready = sem("zn_ready")
        turn_done = sem("turn_done")
        turn_moved = sem("turn_moved")
        zn_split = sem("zn_split")
        scores_done = sem("scores_done")
        row_min_made = sem("row_min_made")
        scores_moved = sem("scores_moved")
        last_exp_done = sem("last_exp_done")
        exp_done = sem("exp_done")
        sum_done = sem("sum_done")
        inv_done = sem("inv_done")
        prob_ready = sem("prob_ready")
        prob_turned = sem("prob_turned")
        prob_moved = sem("prob_moved")
        prob_split = sem("prob_split")
        att_done = sem("att_done")
        att_added = sem("att_added")
        y_stats_made = sem("y_stats_made")
        y_var_made = sem("y_var_made")
        y_rstd_made = sem("y_rstd_made")
        xn_ready = sem("xn_ready")
        logits_done = sem("logits_done")
        picks_ready = sem("picks_ready")
        ranks_done = sem("ranks_done")
        slot_ready = sem("slot_ready")
        scattered = [sem(f"scattered{i}") for i in range(4)]
        scatters_begun = sem("scatters_begun")
        gap_ready = sem("gap_ready")
        gap_exp_done = sem("gap_exp_done")
        gate_den_made = sem("gate_den_made")
        gate_made = sem("gate_made")
        rows_made = sem("rows_made")
        sums_stored = sem("sums_stored")
        tok_noted = sem("tok_noted")
        results_begun = sem("results_begun")
        added = sem("added")
        loads_begun = sem("loads_begun")
        blank_made = sem("blank_made")
        spare_stored = sem("spare_stored")
        table_ready = sem("table_ready")
        fresh_ready = sem("fresh_ready")
        tail_row_made = sem("tail_row_made")
        tails_stored = sem("tails_stored")
        wgu_loaded = [sem(f"wgu_loaded{i}") for i in range(2)]
        wd_loaded = [sem(f"wd_loaded{i}") for i in range(2)]
        tok_loaded = [sem(f"tok_loaded{i}") for i in range(2)]
        tok_turned = sem("tok_turned")
        tok_moved = sem("tok_moved")
        tok_split = sem("tok_split")
        weights_hi = sem("weights_hi")
        weights_split = sem("weights_split")
        hid_made = sem("hid_made")
        hid_hi = sem("hid_hi")
        pads_zeroed = sem("pads_zeroed")
        gu_done = sem("gu_done")
        silu_done = sem("silu_done")
        hid_ready = sem("hid_ready")
        down_done = sem("down_done")
        res_ready = sem("res_ready")

        PREP_V = 0
        PREP_WQ = PREP_V + PAIRS
        PREP = PREP_WQ + PAIRS
        STORE_PAIRS = STORE_HEADS // 2
        STORES = H // STORE_HEADS * CR
        VALS = STORES * STORE_PAIRS
        MATS = VALS + H * KT
        X_OFF_AT = (VALS + MATS) // 2
        KEYS_EARLY = VALS + SCORE_BANKS[DIRECT][0] * KT
        LAST_BANKS = (6, 7, 3)
        TURN_AT = MATS - len(LAST_BANKS)
        VAL_LOAD = 2 * 16
        GU_LOADS = DOWN_LOADS = 3 * 16

        def prep_bank(n):
            return bank[n % 4]

        def mat_bank(m):
            return bank[m % 8 if m < TURN_AT else LAST_BANKS[m - TURN_AT]]

        def mats_before(m):
            return m - 7 if m < TURN_AT else max(n for n in range(TURN_AT) if n % 8 == LAST_BANKS[m - TURN_AT]) + 1

        def val_place(m):
            return m // STORE_PAIRS, m % STORE_PAIRS

        def stored_before(n):
            return sum(16 * len(BATCH_PARTS[i % CR]) for i in range(n % STORE_BUFFERS, n, STORE_BUFFERS))

        def context_rows(r):
            return min(P, BM - r * P)

        def key_place(m):
            return (m - VALS) // KT, (m - VALS) % KT

        LOOP0, UNROLL = 7, 8

        def all_steps(eng, step):
            for s in range(LOOP0):
                step(s, s)
            with eng.Fori(0, T // UNROLL - 1) as i:
                for c in range(LOOP0, LOOP0 + UNROLL):
                    step(i * UNROLL + c, c)
            for s in range(T - UNROLL + LOOP0, T + 5):
                step(s, s)

        def batch_of(t, c):
            return t // TB if isinstance(t, int) else (t - c) // UNROLL + c // UNROLL

        def has(s, lag):
            return not isinstance(s, int) or 0 <= s - lag < T

        def turns(s):
            return has(s, -1) or has(s, 3)

        def part_of(keys, b):
            return keys[:, b, :] if isinstance(b, int) else keys[:, bass.ds(b, 1), :].rearrange("p a n -> p (a n)")

        def half_of(vals, b):
            return vals[:, b % 2] if isinstance(b, int) else vals[:, bass.ds(b % 2, 1)].rearrange("p a c two n -> p (a c) two n")

        def turned_chunks(c0, c1):
            return [(P, c0, c1)] if c1 < KC else [(P, c0, c1 - 1), (KLAST, c1 - 1, c1)]

        def turned_bank(t, g, rows, m0, m1):
            return banks[0:rows, 3 + (t * NG + g) % 2, m0 * P:m1 * P].rearrange("p (c n) -> p c n", n=P)

        ACT_TAILS = E // 2

        def store_tail(eng, e):
            row = eng.value_load(tail_row[0:1, e:e + 1], min_val=0, max_val=E * REGION - W)
            eng.dma_start(expert_in[bass.ds(row, W), :].rearrange("(a p) d -> p a d", p=P), blank[:]).then_inc(tails_stored, 16)

        block = ctx.enter_context(nc.Block())

        @block.sync
        def _(sp):
            sp.dma_start(c_sb[:], ctx_rows.rearrange("b k d -> k b d")).then_inc(ctx_loaded, 16)
            for i, v in enumerate((ln1_w, ln1_b, ln2_w, ln2_b)):
                sp.dma_start(ln_cols[:, i, :], v.rearrange("(k p) -> p k", p=P),
                             allow_slow_non_contiguous=True).then_inc(small_loaded, 16)
            sp.dma_start(side[:], fside.partition_broadcast(P)).then_inc(small_loaded, 16)
            sp.dma_start(wr_sb[:], wr.rearrange("(k p) e -> p k e", p=P)).then_inc(small_loaded, 16)
            for i, cols in enumerate(KV_PIECES):
                sp.dma_start(wkv_sb[:, :, cols], wkv.rearrange("(k p) n -> p k n", p=P)[:, :, cols]
                             ).then_inc(wkv_loaded[i], 16)
            sp.dma_start(wq_sb[:], wq.rearrange("(k p) n -> p k n", p=P)).then_inc(wq_loaded, 16)
            by_half = wout.rearrange("(c two p) n -> two p c n", two=2, p=DH)
            for i in range(2):
                sp.dma_start(wout_sb[i * DH:(i + 1) * DH, :, i, :], by_half[i]).then_inc(wout_loaded, 16)
            tokens = x.rearrange("b (t p) d -> p (b t) d", p=P)
            for b in range(B):
                sp.dma_start(xs[:, b * TB * D:(b + 1) * TB * D].rearrange("p (t d) -> p t d", d=D),
                             tokens[:, b * TB:(b + 1) * TB, :]).then_inc(x_loaded[b], 16)
            sp.wait_ge(blank_made, 2)
            for i in range(SPARE // W):
                at = E * REGION + i * W
                sp.dma_start(expert_in[at:at + W, :].rearrange("(a p) d -> p a d", p=P), blank[:]).then_inc(spare_stored, 16)
            sp.dma_start(out[B * S:, :].rearrange("(a p) d -> p a d", p=P), blank[:, :, 0:D]).then_inc(sums_stored, 16)
            for n in range(STORES):
                r, i = n % CR, n % STORE_BUFFERS
                heads = slice(n // CR * STORE_HEADS, (n // CR + 1) * STORE_HEADS)
                sp.wait_ge(mat_lo, (n + 1) * STORE_PAIRS)
                for r0, r1, b in BATCH_PARTS[r]:
                    k = r * P + r0 - b * M
                    sp.dma_start(valmat_dram[b, heads, k:k + r1 - r0, :, :].rearrange("h k two n -> k h (two n)"),
                                 val_st[i][r0:r1].rearrange("k h two n -> k h (two n)").bitcast(F32)).then_inc(val_stored[i], 16)
            for n in range(STORES, STORES + STORE_BUFFERS):
                sp.wait_ge(val_stored[n % STORE_BUFFERS], stored_before(n))
            sp.wait_ge(mat_made, MATS)

            def store_sums(t0, t1):
                sp.wait_ge(att_added, t1)
                sp.dma_start(out[t0 * P:t1 * P, :].rearrange("(t p) d -> p t d", p=P),
                             xs[:, t0 * D:t1 * D].rearrange("p (t d) -> p t d", d=D)).then_inc(sums_stored, 16)

            for b in range(B):
                if b:
                    sp.wait_ge(valmat_loaded, b * VAL_LOAD)
                if b == 2:
                    store_sums(0, TB)
                if b >= 2:
                    sp.wait_ge(att_done, (b - 1) * TB)
                rows = valmat_dram[b].rearrange("h k two n -> (h k) two n")
                sp.dma_start(valmat[:, b % 2, 0:KC - 1, :, :].bitcast(F32),
                             rows[0:(KC - 1) * P].rearrange("(c p) two n -> p c two n", p=P)).then_inc(valmat_loaded, 16)
                sp.dma_start(valmat[0:KLAST, b % 2, KC - 1, :, :].bitcast(F32), rows[(KC - 1) * P:]).then_inc(valmat_loaded, 16)
            for b in range(1, B - 1):
                store_sums(b * TB, (b + 1) * TB)

            def load_gate_up(e, i, needed=None):
                gate, up = (w[bass.ds(e, 1), :, :].rearrange("a (k p) f -> p (a k) f", p=P) for w in (wg, wu))
                to = gate_up_of(wgt[i])
                sp.dma_start(to[:, :, 0:FI], gate, cond=needed).then_inc(wgu_loaded[i], 16)
                sp.dma_start(to[:, :, FI:FI + FHALF], up[:, :, FULL:FI], cond=needed).then_inc(wgu_loaded[i], 16)
                sp.dma_start(to[:, :, FI + FHALF:GU], up[:, :, 0:FULL], cond=needed).then_inc(wgu_loaded[i], 16)

            def load_down(e, i, needed=None):
                rows = wd[bass.ds(e, 1), :, :].rearrange("a f n -> (a f) n")
                to = down_of(wgt[i])
                sp.dma_start(to[:, 0:FC - 1, :], rows[0:FULL, :].rearrange("(c p) n -> p c n", p=P), cond=needed).then_inc(wd_loaded[i], 16)
                for n in range(2):
                    sp.dma_start(to[n * FHALF:(n + 1) * FHALF, FC - 1, :], rows[FULL:FI, :], cond=needed).then_inc(wd_loaded[i], 16)

            def expert_of(j):
                return sp.value_load(tile_table[0:1, 0, bass.ds(j, 1)], min_val=0, max_val=E - 1)

            def load_tokens(j, i):
                row = sp.value_load(tile_table[0:1, 1, bass.ds(j, 1)], min_val=0, max_val=ROWS - W)
                sp.dma_start(tok[i][:], expert_in[bass.ds(row, W), :].rearrange("(a p) d -> p a d", p=P)
                             ).then_inc(tok_loaded[i], 16)

            sp.wait_ge(scores_done, T * len(SCORE_BANKS))
            for i in range(2):
                load_gate_up(0, i)
                load_down(0, i)
            store_sums(T - TB, T - 2)
            store_sums(T - 2, T)
            sp.wait_ge(tail_row_made, 1)
            for e in range(ACT_TAILS, E):
                store_tail(sp, e)
            sp.wait_ge(table_ready, 1)
            for i in range(2):
                e = expert_of(i)
                sp.wait_ge(wgu_loaded[i], GU_LOADS)
                load_gate_up(e, i, e != 0)
                sp.wait_ge(wd_loaded[i], DOWN_LOADS)
                load_down(e, i, e != 0)
            for i in range(4):
                sp.wait_ge(scattered[i], 32 * (T // 4))
            sp.wait_ge(spare_stored, 16 * (SPARE // W))
            sp.wait_ge(tails_stored, 16 * E)

            def step(j, i):
                sp.wait_ge(tok_turned, j)
                sp.sem_inc(loads_begun, 1)
                sp.wait_ge(tok_noted, j)
                sp.sem_inc(loads_begun, 1)
                sp.wait_ge(weights_split, j * len(PIECES))
                sp.sem_inc(loads_begun, 1)
                load_tokens(j + 1, i)
                e = expert_of(j + 1)
                needed = sp.value_load(fresh[0:1, bass.ds(j + 1, 1)], min_val=0, max_val=1) != 0
                load_gate_up(e, i, needed)
                load_down(e, i, needed)

            for i in range(2):
                load_tokens(i, i)
            sp.wait_ge(fresh_ready, 1)
            for j in range(1, 3):
                step(j, (j + 1) % 2)
            with sp.Fori(0, (NT - 4) // 2) as it:
                for u in range(2):
                    step(it * 2 + (3 + u), u)
            sp.wait_ge(added, NT * WB * 16)

        @block.gpsimd
        def _(pool):
            nc.gpsimd.memset(blank[:], 0.0).then_inc(consts_zero, 1)
            nc.gpsimd.memset(ident[:], 0.0).then_inc(consts_zero, 1)
            nc.gpsimd.memset(ones[:], 1.0).then_inc(consts_zero, 1)
            nc.gpsimd.memset(minus_half[:], -0.5).then_inc(consts_zero, 1)
            nc.gpsimd.memset(eps[:], EPS).then_inc(consts_zero, 1)
            pool.wait_ge(consts_zero, 5)
            nc.gpsimd.affine_select(out=ident[:], in_=ident[:], compare_op=ALU.not_equal, fill=1.0, base=0,
                                    pattern=[[-1, P]], channel_multiplier=1).then_inc(consts_made, 1)
            nc.gpsimd.affine_select(out=before_f[:], in_=ones[:], compare_op=ALU.is_gt, fill=0.0, base=0,
                                    pattern=[[1, P]], channel_multiplier=-1).then_inc(consts_made, 1)
            for to, step, n in ((expert_ids, 1, E), (region_start, REGION, E), (picks_sum, REGION // P, E), (tile_ids, 1, NT),
                                (tile_steps, W, MAX_TILES)):
                nc.gpsimd.iota(to[:], pattern=[[step, n]], base=0, channel_multiplier=0,
                               allow_small_or_imprecise_dtypes=True).then_inc(consts_made, 1)
            for to, first, n in ((token_ids[:], 0, T), (blank[:, :, TOKEN], B * S, WB)):
                nc.gpsimd.iota(to, pattern=[[P, n]], base=first, channel_multiplier=1,
                               allow_small_or_imprecise_dtypes=True).then_inc(blank_made, 1)
            pool.wait_ge(consts_made, 2)
            nc.gpsimd.tensor_copy(before[:], before_f[:]).then_inc(consts_made, 1)
            nc.gpsimd.tensor_copy(ones_h[:], ones[:]).then_inc(consts_made, 1)
            pool.wait_ge(ctx_stats, 1)
            nc.gpsimd.tensor_tensor(c_rstd[:], c_rstd[:], minus_half[0:M, 0:B], ALU.pow).then_inc(ctx_rstd, 1)
            pool.wait_ge(consts_made, 9)
            pool.wait_ge(ctx_rstd, 1)
            for i in range(2):
                other = slice((1 - i) * DH, (2 - i) * DH)
                if i:
                    pool.wait_ge(halves_filled, 2)
                nc.gpsimd.memset(wq_head[other, :, i, :], 1.0 / D).then_inc(halves_filled, 1)
                nc.gpsimd.memset(wout_sb[other, :, i, :], 0.0).then_inc(halves_filled, 1)
            pool.wait_ge(halves_filled, 4)
            pool.wait_ge(x_stats_made, 1)
            nc.gpsimd.tensor_tensor(x_rstd[:], x_rstd[:], minus_half[:], ALU.pow).then_inc(x_rstd_pow, 1)
            pool.wait_ge(x_var2_made, 1)
            nc.gpsimd.tensor_tensor(x_var2[:], x_var2[:], minus_half[:], ALU.pow).then_inc(x_rstd_pow2, 1)

            def make_rows(t, c):
                row = xn[c % 4]
                pool.wait_ge(gate_made, t + 1)
                nc.gpsimd.tensor_tensor(row[:, 1, GATE:GATE + 1], gap_exp[c % 2][:], row[:, 0, GATE:GATE + 1], ALU.mult
                                        ).then_inc(rows_made, 1)
                nc.gpsimd.tensor_copy(row[:, 1, 0:D], row[:, 0, 0:D]).then_inc(rows_made, 1)
                nc.gpsimd.tensor_copy(row[:, :, TOKEN], token_ids[:, bass.ds(t, 1)].to_broadcast([P, 2])).then_inc(rows_made, 1)

            def scatter(t, c):
                pool.wait_ge(rows_made, t * 3 + 3)
                pool.sem_inc(scatters_begun, 1)
                pool.wait_ge(slot_ready, t + 1)
                pool.sem_inc(scatters_begun, 1)
                for k in range(2):
                    nc.gpsimd.indirect_dma_start(
                        expert_in, bass.IndirectOffsetOnAxis(ap=top_slot[c % 4][:, k:k + 1], axis=0),
                        xn[c % 4][:, k, :], None).then_inc(scattered[c % 4], 16)

            def gate_sum(t, c):
                pool.wait_ge(gap_exp_done, t + 1)
                nc.gpsimd.tensor_tensor(gate_den[c % 2][:], gap_exp[c % 2][:], ones[:, 0:1], ALU.add).then_inc(gate_den_made, 1)

            def divide(t, i):
                p = prob[i][:].rearrange("p (h k) -> p h k", h=H)
                pool.wait_ge(inv_done, t + 1)
                nc.gpsimd.tensor_tensor(p, p, row_inv[i][:].unsqueeze(2).to_broadcast([P, H, M]), ALU.mult
                                        ).then_inc(prob_ready, 1)

            def step(s, c):
                if has(s, 3):
                    pool.wait_ge(y_stats_made, s - 2)
                    nc.gpsimd.tensor_tensor(y_var[:], y_mv[:, 1:2], eps[:], ALU.add).then_inc(y_var_made, 1)
                    pool.wait_ge(y_var_made, s - 2)
                    nc.gpsimd.tensor_tensor(y_rstd[:], y_var[:], minus_half[:, 0:1], ALU.pow).then_inc(y_rstd_made, 1)
                if has(s, 5):
                    make_rows(s - 5, c - 5)
                if has(s, 1):
                    divide(s - 1, (c - 1) % 2)
                behind = isinstance(s, int) and s >= T
                if behind and has(s, 4):
                    gate_sum(s - 4, c - 4)
                if has(s, 5):
                    scatter(s - 5, c - 5)
                if not behind and has(s, 4):
                    gate_sum(s - 4, c - 4)

            all_steps(pool, step)

            def note(j, i):
                pool.wait_ge(tok_loaded[i], (j // 2 if isinstance(j, int) else (j - i) // 2) * 16 + 16)
                pool.sem_inc(results_begun, 1)
                nc.gpsimd.tensor_copy(tok_gate[i][:], tok[i][:, :, GATE])
                nc.gpsimd.tensor_copy(tok_id[i][:], tok[i][:, :, TOKEN]).then_inc(tok_noted, 1)

            def add_results(j, i):
                pool.wait_ge(res_ready, j + 1)
                pool.sem_inc(results_begun, 1)
                for a in range(WB):
                    nc.gpsimd.indirect_dma_start(out, bass.IndirectOffsetOnAxis(ap=tok_id[i][:, a:a + 1], axis=0),
                                                 res[i][:, a, :], None, compute_op=ALU.add).then_inc(added, 16)
                pool.wait_ge(added, j * (WB * 16) + WB * 16)
                pool.sem_inc(results_begun, 1)

            note(0, 0)
            note(1, 1)
            pool.wait_ge(tok_noted, 2)
            pool.wait_ge(sums_stored, 16 * (B + 2))
            for j in range(2):
                add_results(j, j)
                note(j + 2, j)
            with pool.Fori(0, (NT - 4) // 2) as it:
                for u in range(2):
                    j = it * 2 + (2 + u)
                    pool.wait_ge(tok_noted, j + 1)
                    pool.sem_inc(results_begun, 1)
                    add_results(j, u)
                    note(j + 2, u)
            pool.wait_ge(tok_noted, NT)
            for j in range(NT - 2, NT):
                add_results(j, j % 2)

        @block.scalar
        def _(act):
            def empty(n, to, src):
                act.wait_ge(prep_made, n + 1)
                nc.scalar.activation(to, src, ACT.Copy).then_inc(prep_moved, 1)

            def round_kv(pieces):
                for i in pieces:
                    act.wait_ge(wkv_loaded[i], 16)
                    nc.scalar.activation(wkv_hi[:, :, KV_PIECES[i]], wkv_sb[:, :, KV_PIECES[i]], ACT.Copy).then_inc(wkv_hi_made, 1)

            round_kv(range(2))
            act.wait_ge(small_loaded, 96)
            for k in range(KT):
                act.wait_ge(ctx_made, k + 1)
                nc.scalar.activation(c_t[:, k, :], prep_bank(k)[:, 0:BM], ACT.Identity,
                                     bias=ln_cols[:, 1, k:k + 1], scale=ln_cols[:, 0, k:k + 1]).then_inc(ctx_turned, 1)
            act.wait_ge(ctx_turned, KT)
            nc.scalar.activation(c_parts[0][:], c_t[:], ACT.Copy).then_inc(ctx_hi, 1)
            round_kv(range(2, len(KV_PIECES)))
            for c in range(PAIRS):
                empty(PREP_V + c, v_t[:, c, :], prep_bank(PREP_V + c)[:, 0:BM])
            for c in range(PAIRS):
                act.wait_ge(prep_made, PREP_WQ + c + 1)
                for i in range(2):
                    rows = slice(i * DH, (i + 1) * DH)
                    ins = nc.scalar.activation(wq_head[rows, c, i, :], prep_bank(PREP_WQ + c)[rows, 0:D], ACT.Copy)
                ins.then_inc(prep_moved, 1)
            for m in range(VALS):
                n, c = val_place(m)
                i, rows = n % STORE_BUFFERS, context_rows(n % CR)
                act.wait_ge(mat_made, m + 1)
                if n >= STORE_BUFFERS and c == 0:
                    act.wait_ge(val_stored[i], stored_before(n))
                nc.scalar.activation(val_st[i][0:rows, 2 * c:2 * c + 2, 0, :],
                                     mat_bank(m)[0:rows, :].rearrange("p (h n) -> p h n", h=2), ACT.Copy).then_inc(mat_hi, 1)
            def normed_plus_one(t, i):
                nc.scalar.activation(zn[i][:], xs[:, bass.ds(t * D, D)], ACT.Identity,
                                     bias=x_off[:, bass.ds(t, 1)], scale=x_rstd[:, bass.ds(t, 1)]).then_inc(zn_ready, 1)

            def turn_move(s, c):
                act.wait_ge(turn_done, s + 2)
                src = bank[5].rearrange("p (k n) -> p k n", n=P)
                if has(s, -1):
                    ins = nc.scalar.activation(zn_t[(c + 1) % 2][0][:], src[:, 0:KT, :], ACT.Copy)
                if has(s, 3):
                    ins = nc.scalar.activation(xn_t[(c + 1) % 2][:], src[:, KT:2 * KT, :], ACT.Copy)
                ins.then_inc(turn_moved, 1)

            for m in range(VALS, MATS):
                h, k = key_place(m)
                at = k * HK + h * M
                if m == TURN_AT:
                    turn_move(-1, -1)
                act.wait_ge(mat_made, m + 1)
                nc.scalar.activation(keymat[0][:, :, at:at + M], mat_bank(m)[:, 0:BM].rearrange("p (b k) -> p b k", b=B),
                                     ACT.Copy).then_inc(mat_hi, 1)
                if m == X_OFF_AT:
                    act.wait_ge(x_off_made, 1)
                    normed_plus_one(0, 0)

            def softmax_exp(t, c, h0, h1):
                act.wait_ge(scores_moved, t * DIRECT + (-(-h1 // HEADS_IN_BANK)))
                for h in range(h0, h1):
                    p = prob[c % 2][:, h * M:(h + 1) * M]
                    ins = nc.scalar.activation(p, p, ACT.Exp, scale=-1.0, accum_out=row_sum[c % 2][:, h:h + 1])
                return ins

            def softmax_last(t, c):
                act.wait_ge(row_min_made, t + 1)
                h0, h1 = SCORE_BANKS[DIRECT]
                for h in range(h0, h1):
                    ins = nc.scalar.activation(prob[c % 2][:, h * M:(h + 1) * M], bank[DIRECT][:, (h - h0) * M:(h - h0 + 1) * M],
                                               ACT.Exp, bias=row_min[c % 2][:, h:h + 1], scale=-1.0,
                                               accum_out=row_sum[c % 2][:, h:h + 1])
                ins.then_inc(last_exp_done, 1)

            def prob_round(t, c, g):
                act.wait_ge(prob_turned, t * NG + (g + 1))
                c0, c1 = PT_GROUPS[g]
                for rows, m0, m1 in turned_chunks(c0, c1):
                    ins = nc.scalar.activation(prob_t[c % 2][0][0:rows, m0:m1, :],
                                               turned_bank(c, g, rows, m0 - c0, m1 - c0), ACT.Copy)
                ins.then_inc(prob_moved, 1)

            def step(s, c):
                if has(s, 2):
                    for g in range(NG - 1):
                        prob_round(s - 2, c - 2, g)
                if has(s, -1):
                    normed_plus_one(s + 1, (c + 1) % 2)
                if has(s, 1):
                    softmax_exp(s - 1, c - 1, EARLY_HEADS, SCORE_BANKS[DIRECT][0]).then_inc(exp_done, 1)
                if has(s, 2):
                    prob_round(s - 2, c - 2, NG - 1)
                if turns(s):
                    turn_move(s, c)
                if has(s, 4):
                    act.wait_ge(gap_ready, s - 3)
                    nc.scalar.activation(gap_exp[c % 2][:], gap[c % 2][:], ACT.Exp).then_inc(gap_exp_done, 1)
                if has(s, 0):
                    softmax_last(s, c)
                    softmax_exp(s, c, 0, EARLY_HEADS)

            all_steps(act, step)

            def tok_move(j, i):
                act.wait_ge(tok_turned, j + 1)
                nc.scalar.activation(tok_t[i][0][:].rearrange("p k n -> p (k n)"), bank[4 + i], ACT.Copy).then_inc(tok_moved, 1)

            def round_pieces(j, i, u):
                before_it = j // 2 if isinstance(j, int) else (j - i) // 2
                loaded, loads = (wgu_loaded, GU_LOADS) if u < UNITS - 1 else (wd_loaded, DOWN_LOADS)
                act.wait_ge(loaded[i], before_it * loads + 2 * loads)
                if u == UNITS - 1 and not (isinstance(j, int) and j < 2):
                    act.wait_ge(down_done, j - 1)
                for p0, p1 in PIECES[2 * u:2 * u + 2]:
                    nc.scalar.activation(wgt_hi[i][:, p0:p1], wgt[i][:, p0:p1], ACT.Copy).then_inc(weights_hi, 1)

            def silu(j, i, u):
                q = (i * UNITS + u) % 2
                act.wait_ge(gu_done, j * UNITS + (u + 1))
                if u < UNITS - 1:
                    nc.scalar.activation(gate_act[q][:], banks[:, 2 * q:2 * q + 2, 0:W], ACT.Silu).then_inc(silu_done, 1)
                else:
                    nc.scalar.activation(gate_act[q][:, 0, :], bank[2 * q][:, 0:W], ACT.Silu)
                    nc.scalar.activation(gate_act[q][FHALF:P, 1, :], bank[2 * q + 1][0:FHALF, 0:W], ACT.Silu).then_inc(silu_done, 1)

            def hid_round(j, i, u):
                q = (i * UNITS + u) % 2
                act.wait_ge(hid_made, j * UNITS + (u + 1))
                if u < UNITS - 1:
                    nc.scalar.activation(hid[i][0][:, 2 * u:2 * u + 2, :], hid_f[q][:], ACT.Copy).then_inc(hid_hi, 1)
                else:
                    nc.scalar.activation(hid[i][0][:, FC - 2, :], hid_f[q][:, 0, :], ACT.Copy)
                    nc.scalar.activation(hid[i][0][0:FHALF, FC - 1, :], hid_f[q][0:FHALF, 1, :], ACT.Copy).then_inc(hid_hi, 1)

            def res_move(j, i):
                act.wait_ge(down_done, j + 1)
                act.wait_ge(tok_noted, j + 1)
                if not (isinstance(j, int) and j < 2):
                    act.wait_ge(added, (j - 1) * (WB * 16))
                for a in range(WB):
                    ins = nc.scalar.activation(res[i][:, a, :], bank[6 + i][:, a * D:(a + 1) * D], ACT.Copy, scale=tok_gate[i][:, a:a + 1])
                ins.then_inc(res_ready, 1)

            def expert_step(j, i, ahead=True, behind_at=UNITS - 2):
                for u in range(UNITS):
                    silu(j, i, u)
                    if ahead:
                        round_pieces(j + 1, 1 - i, u)
                    hid_round(j, i, u)
                    if u == UNITS - 2 and ahead:
                        tok_move(j + 1, 1 - i)
                    if u == behind_at:
                        res_move(j - 1, 1 - i)

            act.wait_ge(tail_row_made, 1)
            for e in range(ACT_TAILS):
                store_tail(act, e)
            act.wait_ge(pads_zeroed, 1)
            for u in range(UNITS):
                round_pieces(0, 0, u)
            round_pieces(1, 1, 0)
            for j in range(2):
                tok_move(j, j)
            for u in range(1, UNITS):
                round_pieces(1, 1, u)
            expert_step(0, 0, ahead=False, behind_at=None)
            for j in range(1, 3):
                expert_step(j, j % 2)
            with act.Fori(0, (NT - 4) // 2) as it:
                for u in range(2):
                    expert_step(it * 2 + (3 + u), 1 - u)
            expert_step(NT - 1, 1, ahead=False, behind_at=UNITS - 1)
            res_move(NT - 1, 1)

        @block.tensor
        def _(pe):
            def fill(n):
                if n >= 4:
                    pe.wait_ge(prep_moved, n - 3)
                return prep_bank(n)

            pe.wait_ge(consts_made, 2)
            pe.wait_ge(ctx_normed, 1)
            for k in range(KT):
                for b in range(B):
                    mm = nc.tensor.transpose(bank[k][:, b * M:(b + 1) * M], c_sb[:, b, k * P:(k + 1) * P], ident[0:M, 0:M])
                mm.then_inc(ctx_made, 1)
            pe.wait_ge(ctx_split, 1)

            def turned_kv(to, c):
                for k in range(KT):
                    mm = product(to[:, 0:BM], [w[:, k, c * P:(c + 1) * P] for w in (wkv_hi, wkv_lo)],
                                 [x[:, k, :] for x in c_parts], k == 0, k == KT - 1)
                return mm

            for c in range(PAIRS):
                pe.wait_ge(wkv_split, 2 if c < PAIRS // 2 else 4)
                if c >= 4:
                    pe.wait_ge(keys_moved, c - 3)
                turned_kv(bank[4 + c % 4], c).then_inc(keys_made, 1)
                turned_kv(fill(PREP_V + c), PAIRS + c).then_inc(prep_made, 1)
            pe.wait_ge(mix_made, 1)
            pe.wait_ge(wq_loaded, 16)
            for c in range(PAIRS):
                to = fill(PREP_WQ + c)
                for k in range(KT):
                    mm = nc.tensor.matmul(to[:, 0:D], wq_sb[:, k, c * P:(c + 1) * P], mix[:, k, :],
                                          start=k == 0, stop=k == KT - 1)
                mm.then_inc(prep_made, 1)
            pe.wait_ge(prep_moved, PREP_WQ)
            pe.wait_ge(keys_moved, PAIRS)
            pe.wait_ge(halves_filled, 4)
            pe.wait_ge(wout_loaded, 32)
            for m in range(VALS):
                n, c = val_place(m)
                r, rows = n % CR, context_rows(n % CR)
                c += n // CR * STORE_PAIRS
                if m < 4:
                    pe.wait_ge(prep_moved, PREP - 3 + m)
                if m >= 8:
                    pe.wait_ge(mat_lo, mats_before(m))
                nc.tensor.matmul(mat_bank(m)[0:rows, :], v_t[:, c, r * P:r * P + rows], wout_sb[:, c, :, :].rearrange("p h n -> p (h n)"),
                                 start=True, stop=True).then_inc(mat_made, 1)
            def turn(s, c):
                if c >= 0:
                    pe.wait_ge(turn_moved, s + 1)
                    pe.wait_ge(zn_split, s + 1 if has(s, 0) else T)
                if has(s, -1):
                    pe.wait_ge(zn_ready, s + 2)
                    for k in range(KT):
                        mm = nc.tensor.transpose(bank[5][:, k * P:(k + 1) * P], zn[(c + 1) % 2][:, k * P:(k + 1) * P], ident[:])
                if has(s, 3):
                    pe.wait_ge(xn_ready, s - 2)
                    for k in range(KT):
                        mm = nc.tensor.transpose(bank[5][:, (KT + k) * P:(KT + k + 1) * P],
                                                 xn[(c - 3) % 4][:, 0, k * P:(k + 1) * P], ident[:])
                mm.then_inc(turn_done, 1)

            for m in range(VALS, MATS):
                h, k = key_place(m)
                if m == TURN_AT:
                    pe.wait_ge(mat_lo, TURN_AT - 7)
                    turn(-1, -1)
                pe.wait_ge(mat_lo, mats_before(m))
                nc.tensor.matmul(mat_bank(m)[:, 0:BM], wq_head[:, h // 2, h % 2, k * P:(k + 1) * P], k_head[:, h // 2, h % 2, :],
                                 start=True, stop=True).then_inc(mat_made, 1)
            def scores(s, c, i):
                h0, h1 = SCORE_BANKS[i]
                b = batch_of(s, c)
                for k in range(KT):
                    at = k * HK + h0 * M
                    mm = product(bank[i][:, 0:(h1 - h0) * M], [z[:, k, :] for z in zn_t[c % 2]],
                                 [part_of(z, b)[:, at:at + (h1 - h0) * M] for z in keymat], k == 0, k == KT - 1)
                return mm

            def turn_probs(t, c, g):
                c0, c1 = PT_GROUPS[g]
                if c * NG + g >= 2:
                    pe.wait_ge(prob_split, t * NG + (g - 1))
                for m in range(c0, c1):
                    n = P if m < KC - 1 else KLAST
                    mm = nc.tensor.transpose(bank[3 + (c * NG + g) % 2][0:n, (m - c0) * P:(m - c0 + 1) * P],
                                             prob[c % 2][:, m * P:m * P + n], ident[:])
                mm.then_inc(prob_turned, 1)

            def attend(t, c, g):
                pe.wait_ge(prob_split, t * NG + (g + 1))
                vals = half_of(valmat, batch_of(t, c))
                for m in range(*PT_GROUPS[g]):
                    n = P if m < KC - 1 else KLAST
                    mm = product(bank[6][:, 0:D], [p[0:n, m, :] for p in prob_t[c % 2]],
                                 [vals[0:n, m, i, :] for i in range(2)], m == 0, m == KC - 1)
                return mm

            def step(s, c):
                if has(s, 2):
                    pe.wait_ge(prob_ready, s - 1)
                    for g in range(NG - 1):
                        turn_probs(s - 2, c - 2, g)
                if has(s, 4):
                    pe.wait_ge(turn_moved, s + 1)
                    if c > 4:
                        pe.wait_ge(slot_ready, s - 4)
                    for k in range(KT):
                        mm = nc.tensor.matmul(bank[7][:, 0:E], xn_t[c % 2][:, k, :], wr_sb[:, k, :],
                                              start=k == 0, stop=k == KT - 1)
                    mm.then_inc(logits_done, 1)
                if has(s, 0):
                    pe.wait_ge(zn_split, s + 1)
                    if c:
                        pe.wait_ge(scores_moved, s * DIRECT)
                    else:
                        pe.wait_ge(mat_lo, KEYS_EARLY)
                    for i in range(DIRECT):
                        scores(s, c, i).then_inc(scores_done, 1)
                if has(s, 2):
                    turn_probs(s - 2, c - 2, NG - 1)
                if has(s, 0):
                    if c:
                        pe.wait_ge(last_exp_done, s)
                    else:
                        pe.wait_ge(mat_lo, MATS)
                    scores(s, c, DIRECT).then_inc(scores_done, 1)
                if turns(s):
                    turn(s, c)
                if has(s, 4):
                    pe.wait_ge(picks_ready, s - 3)
                    nc.tensor.matmul(bank[7][:, 16:16 + E], before[:], picks[:], start=True, stop=False)
                    nc.tensor.matmul(bank[7][:, 16:16 + E], ones_h[:], picks_sum[:], start=False, stop=True
                                     ).then_inc(ranks_done, 1)
                if has(s, 2):
                    if (c - 2) % UNROLL == 0:
                        pe.wait_ge(valmat_loaded, batch_of(s - 2, c - 2) * VAL_LOAD + VAL_LOAD)
                    if c > 2:
                        pe.wait_ge(att_added, s - 2)
                    for g in range(NG):
                        mm = attend(s - 2, c - 2, g)
                    mm.then_inc(att_done, 1)

            all_steps(pe, step)

            pe.wait_ge(slot_ready, T)
            nc.tensor.matmul(bank[7][:, 16:16 + E], ones_h[:], picks_sum[:], start=True, stop=True).then_inc(ranks_done, 1)

            def tok_turn(j, i):
                pe.wait_ge(tok_loaded[i], (j // 2 if isinstance(j, int) else (j - i) // 2) * 16 + 16)
                if not (isinstance(j, int) and j < 2):
                    pe.wait_ge(tok_split, j - 1)
                for k in range(KT):
                    for a in range(WB):
                        mm = nc.tensor.transpose(bank[4 + i][:, k * W + a * P:k * W + (a + 1) * P],
                                                 tok[i][:, a, k * P:(k + 1) * P], ident[:])
                mm.then_inc(tok_turned, 1)

            def gate_up(j, i, u):
                q = (i * UNITS + u) % 2
                pe.wait_ge(weights_split, j * len(PIECES) + 2 * KT)
                pe.wait_ge(tok_split, j + 1)
                if not (isinstance(j, int) and j * UNITS + u < 2):
                    pe.wait_ge(hid_made, j * UNITS + (u - 1))
                w = [gate_up_of(x) for x in (wgt_hi[i], wgt_lo[i])]
                for f in range(2 * u, 2 * u + 2):
                    starts = [(0, f * P), (W, FI + FHALF + f * P)] if f < FC - 1 else [(0, FULL)]
                    for at, col in starts:
                        for k in range(KT):
                            mm = product(bank[2 * q + f % 2][:, at:at + W], [x[:, k, col:col + P] for x in w],
                                         [x[:, k, :] for x in tok_t[i]], k == 0, k == KT - 1)
                mm.then_inc(gu_done, 1)

            def down(j, i):
                pe.wait_ge(weights_split, j * len(PIECES) + len(PIECES))
                pe.wait_ge(hid_ready, j * UNITS + UNITS)
                if not (isinstance(j, int) and j < 2):
                    pe.wait_ge(res_ready, j - 1)
                w = [down_of(x) for x in (wgt_hi[i], wgt_lo[i])]
                for a in range(WB):
                    to = bank[6 + i][:, a * D:(a + 1) * D]
                    h = [x[:, :, a * P:(a + 1) * P] for x in hid[i]]
                    for f in range(FC - 1):
                        product(to, [x[:, f, :] for x in h], [x[:, f, :] for x in w], f == 0, False)
                    for x in w:
                        mm = nc.tensor.matmul(to, h[0][:, FC - 1, :], x[:, FC - 1, :], start=False, stop=x is w[1])
                mm.then_inc(down_done, 1)

            def expert_step(j, i, ahead=True, behind_at=UNITS - 2):
                for u in range(UNITS):
                    gate_up(j, i, u)
                    if u == UNITS - 2 and ahead:
                        tok_turn(j + 1, 1 - i)
                    if u == behind_at:
                        down(j - 1, 1 - i)

            for j in range(2):
                tok_turn(j, j)
            expert_step(0, 0, ahead=False, behind_at=None)
            for j in range(1, 3):
                expert_step(j, j % 2)
            with pe.Fori(0, (NT - 4) // 2) as it:
                for u in range(2):
                    expert_step(it * 2 + (3 + u), 1 - u)
            expert_step(NT - 1, 1, ahead=False, behind_at=UNITS - 1)
            down(NT - 1, 1)

        @block.vector
        def _(dve):
            def settle():
                dve.drain()

            dve.wait_ge(ctx_loaded, 16)
            for b in range(B):
                nc.vector.bn_stats(c_stats[:, b, :], c_sb[:, b, :])
            settle()
            for b in range(B):
                nc.vector.bn_aggr(c_mv[:, b, :], c_stats[:, b, :])
            settle()
            nc.vector.tensor_scalar(c_rstd[:], c_mv[:, :, 1], EPS, None, ALU.add).then_inc(ctx_stats, 1)
            dve.wait_ge(ctx_rstd, 1)
            for b in range(B):
                ins = nc.vector.tensor_scalar(c_sb[:, b, :], c_sb[:, b, :], c_mv[:, b, 0:1], c_rstd[:, b:b + 1],
                                              ALU.subtract, ALU.mult)
            ins.then_inc(ctx_normed, 1)

            def rest_kv(pieces):
                for i in pieces:
                    cols = KV_PIECES[i]
                    dve.wait_ge(wkv_hi_made, i + 1)
                    nc.vector.tensor_tensor(wkv_lo[:, :, cols], wkv_sb[:, :, cols], wkv_hi[:, :, cols].bitcast(F32),
                                            ALU.subtract).then_inc(wkv_split, 1)

            rest_kv(range(2))
            dve.wait_ge(ctx_hi, 1)
            nc.vector.tensor_tensor(c_parts[1][:], c_t[:], c_parts[0][:].bitcast(F32), ALU.subtract).then_inc(ctx_split, 1)
            rest_kv(range(2, len(KV_PIECES)))
            dve.wait_ge(small_loaded, 96)
            dve.wait_ge(consts_zero, 5)
            dve.wait_ge(consts_made, 1)
            nc.vector.tensor_tensor(q_mix[:], ln_cols[:, 3, :], ln_cols[:, 2, :], ALU.subtract)
            nc.vector.tensor_scalar(side_scale[:], side[:], 1.0, -QK_SCALE, ALU.add, ALU.mult)
            nc.vector.tensor_scalar(side_shift[:], side[:], -QK_SCALE, None, ALU.mult)
            settle()
            nc.vector.tensor_scalar(q_mix[:], q_mix[:], 1.0 / D, None, ALU.mult)
            settle()
            for k in range(KT):
                nc.vector.tensor_scalar(mix[:, k, :], blank[:, 0, 0:D], q_mix[:, k:k + 1], None, ALU.add)
            settle()
            for k in range(KT):
                ins = nc.vector.tensor_scalar(mix[:, k, k * P:(k + 1) * P], ident[:], ln_cols[:, 2, k:k + 1], q_mix[:, k:k + 1],
                                              ALU.mult, ALU.add)
            ins.then_inc(mix_made, 1)
            for c in range(PAIRS):
                dve.wait_ge(keys_made, c + 1)
                for i in range(2):
                    own = slice(i * DH, (i + 1) * DH)
                    other = slice((1 - i) * DH, (2 - i) * DH)
                    keys = bank[4 + c % 4][own, 0:BM].rearrange("p (b k) -> p b k", b=B)
                    for rows, by in ((own, side_scale), (other, side_shift)):
                        ins = nc.vector.tensor_tensor(k_head[rows, c, i, :].rearrange("p (b k) -> p b k", b=B), keys,
                                                      by[own, :, 2 * c + i].unsqueeze(2).to_broadcast([DH, B, M]), ALU.mult)
                ins.then_inc(keys_moved, 1)

            def mat_rest(m):
                dve.wait_ge(mat_hi, m + 1)
                if m < VALS:
                    n, c = val_place(m)
                    i, rows = n % STORE_BUFFERS, context_rows(n % CR)
                    hi, lo = (val_st[i][0:rows, 2 * c:2 * c + 2, part, :] for part in range(2))
                    src = mat_bank(m)[0:rows, :].rearrange("p (h n) -> p h n", h=2)
                    if n >= STORE_BUFFERS and c == 0:
                        dve.wait_ge(val_stored[i], stored_before(n))
                else:
                    h, k = key_place(m)
                    at = k * HK + h * M
                    hi, lo = (z[:, :, at:at + M] for z in keymat)
                    src = mat_bank(m)[:, 0:BM].rearrange("p (b k) -> p b k", b=B)
                nc.vector.tensor_tensor(lo, src, hi.bitcast(F32), ALU.subtract).then_inc(mat_lo, 1)

            def token_stats(t0, t1):
                for t in range(t0, t1):
                    dve.wait_ge(x_loaded[t // TB], 16)
                    nc.vector.bn_stats(x_stats[:, t, :], xs[:, t * D:(t + 1) * D])

            token_stats(0, STATS_EARLY)
            for m in range(VALS // 2):
                mat_rest(m)
                left = T - STATS_EARLY
                token_stats(STATS_EARLY + m * left // (VALS // 2), STATS_EARLY + (m + 1) * left // (VALS // 2))
            settle()
            nc.vector.tensor_tensor(x_mean[:], x_stats[:, :, 1], x_stats[:, :, 4], ALU.add)
            nc.vector.tensor_tensor(x_odd[:], x_stats[:, :, 4], x_stats[:, :, 1], ALU.subtract)
            nc.vector.tensor_tensor(x_var[:], x_stats[:, :, 2], x_stats[:, :, 5], ALU.add)
            settle()
            nc.vector.tensor_scalar(x_mean[:], x_mean[:], 0.5, None, ALU.mult)
            nc.vector.scalar_tensor_tensor(out=x_odd[:], in0=x_odd[:], scalar=0.25, in1=x_odd[:], op0=ALU.mult, op1=ALU.mult)
            settle()
            nc.vector.scalar_tensor_tensor(out=x_var[:], in0=x_var[:], scalar=1.0 / D, in1=x_odd[:], op0=ALU.mult, op1=ALU.add)
            settle()
            nc.vector.tensor_scalar(x_rstd[:], x_var[:], EPS, None, ALU.add).then_inc(x_stats_made, 1)
            for m in range(VALS // 2, VALS):
                mat_rest(m)
            dve.wait_ge(x_rstd_pow, 1)
            nc.vector.tensor_tensor(x_var2[:], x_var[:], x_rstd[:], ALU.mult)
            settle()
            nc.vector.tensor_tensor(x_var2[:], x_var2[:], x_rstd[:], ALU.mult)
            settle()
            nc.vector.tensor_scalar(x_var2[:], x_var2[:], EPS, None, ALU.add).then_inc(x_var2_made, 1)
            for m in range(VALS, X_OFF_AT):
                mat_rest(m)
            dve.wait_ge(x_rstd_pow2, 1)
            nc.vector.tensor_tensor(x_rstd[:], x_rstd[:], x_var2[:], ALU.mult)
            settle()
            nc.vector.scalar_tensor_tensor(out=x_off[:], in0=x_mean[:], scalar=-1.0, in1=x_rstd[:], op0=ALU.mult, op1=ALU.mult)
            settle()
            nc.vector.tensor_scalar(x_off[:], x_off[:], 1.0, None, ALU.add).then_inc(x_off_made, 1)
            def zn_rest(s, c):
                dve.wait_ge(turn_moved, s + 2)
                to = zn_t[(c + 1) % 2]
                nc.vector.tensor_tensor(to[1][:], bank[5][:, 0:KT * P].rearrange("p (k n) -> p k n", n=P), to[0][:].bitcast(F32),
                                        ALU.subtract).then_inc(zn_split, 1)

            for m in range(X_OFF_AT, MATS):
                if m == TURN_AT:
                    zn_rest(-1, -1)
                mat_rest(m)

            def prob_rest(t, c, g):
                c0, c1 = PT_GROUPS[g]
                dve.wait_ge(prob_moved, t * NG + (g + 1))
                for rows, m0, m1 in turned_chunks(c0, c1):
                    hi, lo = (p[0:rows, m0:m1, :] for p in prob_t[c % 2])
                    ins = nc.vector.tensor_tensor(lo, turned_bank(c, g, rows, m0 - c0, m1 - c0), hi.bitcast(F32), ALU.subtract)
                ins.then_inc(prob_split, 1)

            def add_attention(t):
                dve.wait_ge(att_done, t + 1)
                row = xs[:, bass.ds(t * D, D)]
                nc.vector.tensor_tensor(row, row, bank[6][:, 0:D], ALU.add).then_inc(att_added, 1)
                settle()
                nc.vector.bn_stats(y_stats[:], row)
                settle()
                nc.vector.bn_aggr(y_mv[:], y_stats[:]).then_inc(y_stats_made, 1)

            def normalise(t, c):
                dve.wait_ge(y_rstd_made, t + 1)
                if c >= 4:
                    dve.wait_ge(scattered[c % 4], ((t - c) // 4 + c // 4) * 32)
                nc.vector.tensor_scalar(xn[c % 4][:, 0, 0:D], xs[:, bass.ds(t * D, D)], y_mv[:, 0:1], y_rstd[:],
                                        ALU.subtract, ALU.mult).then_inc(xn_ready, 1)

            def softmax_min(t, c):
                for i, (h0, h1) in enumerate(SCORE_BANKS):
                    dve.wait_ge(scores_done, t * len(SCORE_BANKS) + (i + 1))
                    ins = nc.vector.tensor_reduce(row_min[c % 2][:, h0:h1], bank[i][:, 0:(h1 - h0) * M].rearrange("p (h k) -> p h k", k=M),
                                                  AX_X, ALU.min)
                ins.then_inc(row_min_made, 1)

            def softmax_in(t, c):
                settle()
                for i, (h0, h1) in enumerate(SCORE_BANKS[:DIRECT]):
                    nc.vector.tensor_tensor(
                        prob[c % 2][:, h0 * M:h1 * M].rearrange("p (h k) -> p h k", k=M),
                        bank[i][:, 0:(h1 - h0) * M].rearrange("p (h k) -> p h k", k=M),
                        row_min[c % 2][:, h0:h1].unsqueeze(2).to_broadcast([P, h1 - h0, M]), ALU.subtract).then_inc(scores_moved, 1)

            def softmax_inv(t, c):
                dve.wait_ge(exp_done, t + 1)
                nc.vector.reciprocal(row_inv[c % 2][:], row_sum[c % 2][:]).then_inc(inv_done, 1)

            def route(t, c):
                dve.wait_ge(logits_done, t + 1)
                nc.vector.tensor_copy(logits[:], bank[7][:, 0:E])
                settle()
                nc.vector.max(top8[:], logits[:])
                settle()
                nc.vector.max_index(top8_id[:], top8[:], logits[:])
                nc.vector.tensor_tensor(gap[c % 2][:], top8[:, 1:2], top8[:, 0:1], ALU.subtract).then_inc(gap_ready, 1)
                settle()
                nc.vector.tensor_tensor(pick[:], expert_ids[:].unsqueeze(1).to_broadcast([P, 2, E]),
                                        top8_id[:, 0:2].unsqueeze(2).to_broadcast([P, 2, E]), ALU.is_equal)
                settle()
                nc.vector.tensor_tensor(picks[:], pick[:, 0, :], pick[:, 1, :], ALU.add).then_inc(picks_ready, 1)

            def allot(t, c):
                dve.wait_ge(ranks_done, t + 1)
                nc.vector.tensor_tensor(picked[:], pick[:], bank[7][:, 16:16 + E].unsqueeze(1).to_broadcast([P, 2, E]), ALU.mult)
                nc.vector.tensor_tensor(picks_sum[:], picks_sum[:], picks[:], ALU.add)
                settle()
                nc.vector.tensor_reduce(slot_f[:], picked[:], AX_X, ALU.add)
                settle()
                nc.vector.tensor_copy(top_slot[c % 4][:], slot_f[:]).then_inc(slot_ready, 1)

            def step(s, c):
                if has(s, 3):
                    add_attention(s - 3)
                if has(s, 2):
                    for g in range(NG - 1):
                        prob_rest(s - 2, c - 2, g)
                if has(s, 5):
                    dve.wait_ge(gate_den_made, s - 4)
                    nc.vector.reciprocal(xn[(c - 5) % 4][:, 0, GATE:GATE + 1], gate_den[(c - 5) % 2][:]).then_inc(gate_made, 1)
                if has(s, 3):
                    normalise(s - 3, c - 3)
                if has(s, 4):
                    route(s - 4, c - 4)
                if has(s, 1):
                    softmax_inv(s - 1, c - 1)
                if has(s, 2):
                    prob_rest(s - 2, c - 2, NG - 1)
                if has(s, 0):
                    softmax_min(s, c)
                    softmax_in(s, c)
                if has(s, -1):
                    zn_rest(s, c)
                if has(s, 4):
                    allot(s - 4, c - 4)

            dve.wait_ge(consts_made, 9)
            for n in range(STORES, STORES + STORE_BUFFERS):
                dve.wait_ge(val_stored[n % STORE_BUFFERS], stored_before(n))
            all_steps(dve, step)
            dve.wait_ge(ranks_done, T + 1)
            nc.vector.tensor_copy(next_row[:], bank[7][:, 16:16 + E])
            settle()

            nc.vector.tensor_tensor(count[:], next_row[:], region_start[:], ALU.subtract)
            nc.vector.tensor_copy(tail_row[:], next_row[:]).then_inc(tail_row_made, 1)
            settle()
            nc.vector.tensor_tensor(tile_used[:], count[:].unsqueeze(2).to_broadcast([P, E, MAX_TILES]),
                                    tile_steps[:].unsqueeze(1).to_broadcast([P, E, MAX_TILES]), ALU.is_gt)
            settle()
            nc.vector.tensor_reduce(tiles_of[:], tile_used[:], AX_X, ALU.add)
            settle()
            nc.vector.tensor_tensor_scan(tiles_upto[:], ones[:, 0:E], tiles_of[:], 0.0, ALU.mult, ALU.add)
            nc.vector.tensor_scalar(jump[:], tiles_of[:], -float(W), float(REGION), ALU.mult, ALU.add)
            settle()
            nc.vector.tensor_tensor(past[:], tile_ids[:].unsqueeze(2).to_broadcast([P, NT, E]),
                                    tiles_upto[:].unsqueeze(1).to_broadcast([P, NT, E]), ALU.is_ge)
            settle()
            nc.vector.tensor_reduce(table_f[:, 0, :], past[:], AX_X, ALU.add)
            settle()
            nc.vector.tensor_tensor(past[:], past[:], jump[:].unsqueeze(1).to_broadcast([P, NT, E]), ALU.mult)
            nc.vector.tensor_scalar(tile_table[:, 0, :], table_f[:, 0, :], float(E - 1), None, ALU.min)
            settle()
            nc.vector.tensor_reduce(table_f[:, 1, :], past[:], AX_X, ALU.add)
            settle()
            nc.vector.scalar_tensor_tensor(out=tile_table[:, 1, :], in0=tile_ids[:], scalar=float(W), in1=table_f[:, 1, :],
                                           op0=ALU.mult, op1=ALU.add).then_inc(table_ready, 1)
            settle()
            nc.vector.tensor_tensor(fresh_f[:, 2:NT], tile_table[:, 0, 2:NT], tile_table[:, 0, 0:NT - 2], ALU.not_equal)
            settle()
            nc.vector.tensor_copy(fresh[:, 2:NT], fresh_f[:, 2:NT]).then_inc(fresh_ready, 1)
            for i in range(2):
                ins = nc.vector.memset(down_of(wgt_lo[i])[FHALF:P, FC - 1, :].bitcast(U32), 0)
            ins.then_inc(pads_zeroed, 1)

            def tok_rest(j, i):
                dve.wait_ge(tok_moved, j + 1)
                nc.vector.tensor_tensor(tok_t[i][1][:].rearrange("p k n -> p (k n)"), bank[4 + i],
                                        tok_t[i][0][:].rearrange("p k n -> p (k n)").bitcast(F32), ALU.subtract).then_inc(tok_split, 1)

            def rest_pieces(j, i, u):
                for n in range(2 * u, 2 * u + 2):
                    p0, p1 = PIECES[n]
                    rows = P if n < len(PIECES) - 1 else FHALF
                    dve.wait_ge(weights_hi, j * len(PIECES) + (n + 1))
                    nc.vector.tensor_tensor(wgt_lo[i][0:rows, p0:p1], wgt[i][0:rows, p0:p1], wgt_hi[i][0:rows, p0:p1].bitcast(F32),
                                            ALU.subtract).then_inc(weights_split, 1)

            def hidden(j, i, u):
                q = (i * UNITS + u) % 2
                dve.wait_ge(silu_done, j * UNITS + (u + 1))
                if u < UNITS - 1:
                    nc.vector.tensor_tensor(hid_f[q][:], gate_act[q][:], banks[:, 2 * q:2 * q + 2, W:2 * W], ALU.mult).then_inc(hid_made, 1)
                else:
                    nc.vector.tensor_tensor(hid_f[q][:, 0, :], gate_act[q][:, 0, :], bank[2 * q][:, W:2 * W], ALU.mult)
                    nc.vector.tensor_tensor(hid_f[q][0:FHALF, 1, :], gate_act[q][FHALF:P, 1, :], bank[2 * q + 1][FHALF:P, 0:W], ALU.mult
                                            ).then_inc(hid_made, 1)

            def hid_rest(j, i, u):
                q = (i * UNITS + u) % 2
                dve.wait_ge(hid_hi, j * UNITS + (u + 1))
                hi, lo = hid[i]
                if u < UNITS - 1:
                    nc.vector.tensor_tensor(lo[:, 2 * u:2 * u + 2, :], hid_f[q][:], hi[:, 2 * u:2 * u + 2, :].bitcast(F32), ALU.subtract
                                            ).then_inc(hid_ready, 1)
                else:
                    nc.vector.tensor_tensor(lo[:, FC - 2, :], hid_f[q][:, 0, :], hi[:, FC - 2, :].bitcast(F32), ALU.subtract)
                    nc.vector.tensor_tensor(hi[FHALF:P, FC - 1, :], hid_f[q][0:FHALF, 1, :], hi[0:FHALF, FC - 1, :].bitcast(F32),
                                            ALU.subtract).then_inc(hid_ready, 1)

            def expert_step(j, i, ahead=True):
                for u in range(UNITS):
                    hidden(j, i, u)
                    if ahead:
                        rest_pieces(j + 1, 1 - i, u)
                    hid_rest(j, i, u)
                    if ahead and u == UNITS - 2:
                        tok_rest(j + 1, 1 - i)

            for u in range(UNITS):
                rest_pieces(0, 0, u)
            rest_pieces(1, 1, 0)
            for j in range(2):
                tok_rest(j, j)
            for u in range(1, UNITS):
                rest_pieces(1, 1, u)
            expert_step(0, 0, ahead=False)
            for j in range(1, 3):
                expert_step(j, j % 2)
            with dve.Fori(0, (NT - 4) // 2) as it:
                for u in range(2):
                    expert_step(it * 2 + (3 + u), 1 - u)
            expert_step(NT - 1, 1, ahead=False)


_INS = ["x", "ctx_1024", "fside_Bx16_0", "L0_xattn_ln1_w", "L0_xattn_ln1_b", "L0_xattn_ln2_w", "L0_xattn_ln2_b",
        "L0_xattn_Wq", "L0_xattn_Wkv", "L0_xattn_Wout", "L0_ffn_Wr", "L0_ffn_Wg", "L0_ffn_Wu", "L0_ffn_Wd"]


def kernel(**inputs):
    import numpy as np
    import concourse.bacc as bacc
    from concourse.bass_utils import run_bass_kernel_spmd

    nc = bacc.Bacc("TRN2", target_bir_lowering=False, num_devices=1)
    arrays, args = {}, []
    for name in _INS:
        a = np.ascontiguousarray(inputs[name])
        arrays[f"in_{name}"] = a
        args.append(nc.dram_tensor(f"in_{name}", a.shape, mybir.dt.from_np(a.dtype), kind="ExternalInput").ap())
    args.append(nc.dram_tensor("result", (B * S + W, D), F32, kind="ExternalOutput").ap())
    program(nc, *args)
    r = run_bass_kernel_spmd(nc, [arrays], core_ids=[0])
    return r.results[0]["result"][:B * S].reshape(B, S, D)
```
